# Optimizing a Trainium2 kernel written in Bass

```python
import numpy as np
import jax
import jax.numpy as jnp

def _softmax(x, axis=-1):
    return jax.nn.softmax(x, axis=axis)

def _gelu(x):
    return jax.nn.gelu(x, approximate=True)

def _silu(x):
    return jax.nn.silu(x)

def _sigmoid(x):
    return jax.nn.sigmoid(x)

def _layernorm(x, axis=-1, eps=1e-05):
    m = jnp.mean(x, axis=axis, keepdims=True)
    v = jnp.var(x, axis=axis, keepdims=True)
    return (x - m) / jnp.sqrt(v + eps)

def _scatter_add(tgt, idx, src, axis=0):
    return tgt.at[idx].add(src)

def _segment_sum(src, seg, n):
    return jax.ops.segment_sum(src, seg, n)
kernel_name = 'mk_seq_postln_d1_jaxref_r8_fe6ef7'

def setup_inputs(seed: int=0):
    np.random.seed(seed)
    _w = jnp.asarray

    def _L0_attn_setup():
        import jax, jax.numpy as jnp
        import numpy as np
        D = 128
        H = 16
        DH = D // H
        key = jax.random.key(seed)
        ks = jax.random.split(key, 7)
        s = 0.02
        return {'z': jax.random.normal(ks[0], (8, 128, D), dtype=jnp.float32), 'ln_w': jnp.ones((D,), dtype=jnp.float32), 'ln_b': jnp.zeros((D,), dtype=jnp.float32), 'W_qkv': jax.random.normal(ks[1], (D, 3 * D), dtype=jnp.float32) * s, 'b_qkv': jnp.zeros((3 * D,), dtype=jnp.float32), 'W_proj': jax.random.normal(ks[2], (D, D), dtype=jnp.float32) * s, 'b_proj': jnp.zeros((D,), dtype=jnp.float32)}
    _L0_attn_in = _L0_attn_setup()

    def _L0_ffn_setup():
        import jax, jax.numpy as jnp
        import numpy as np
        D = 128
        N_EXP = 8
        TOP_K = 1
        key = jax.random.key(seed)
        ks = jax.random.split(key, 7)
        s = 0.02
        return {'x': jax.random.normal(ks[0], (4, 256, D), jnp.float32), 'gate_w': jax.random.normal(ks[1], (D, N_EXP), jnp.float32) * s, 'gate_b': jnp.zeros((N_EXP,), jnp.float32), 'w1': jax.random.normal(ks[2], (N_EXP, D, 4 * D), jnp.float32) * s, 'b1': jnp.zeros((N_EXP, 4 * D), jnp.float32), 'w2': jax.random.normal(ks[3], (N_EXP, 4 * D, D), jnp.float32) * s, 'b2': jnp.zeros((N_EXP, D), jnp.float32)}
    _L0_ffn_in = _L0_ffn_setup()
    _d = {'L0_attn_z': _L0_attn_in['z'], 'L0_attn_ln_w': _L0_attn_in['ln_w'], 'L0_attn_ln_b': _L0_attn_in['ln_b'], 'L0_attn_W_qkv': _L0_attn_in['W_qkv'], 'L0_attn_b_qkv': _L0_attn_in['b_qkv'], 'L0_attn_W_proj': _L0_attn_in['W_proj'], 'L0_attn_b_proj': _L0_attn_in['b_proj'], 'L0_ffn_gate_w': _L0_ffn_in['gate_w'], 'L0_ffn_gate_b': _L0_ffn_in['gate_b'], 'L0_ffn_w1': _L0_ffn_in['w1'], 'L0_ffn_b1': _L0_ffn_in['b1'], 'L0_ffn_w2': _L0_ffn_in['w2'], 'L0_ffn_b2': _L0_ffn_in['b2']}
    _x0 = _d['L0_attn_z']
    _d['L0_attn_z'] = jax.random.normal(jax.random.fold_in(jax.random.key(seed), 1), (8, 512, 128), dtype=_x0.dtype)
    del _x0
    return _d

def reference(L0_attn_z, L0_attn_ln_w, L0_attn_ln_b, L0_attn_W_qkv, L0_attn_b_qkv, L0_attn_W_proj, L0_attn_b_proj, L0_ffn_gate_w, L0_ffn_gate_b, L0_ffn_w1, L0_ffn_b1, L0_ffn_w2, L0_ffn_b2):

    def _L0_attn_ref(z, ln_w, ln_b, W_qkv, b_qkv, W_proj, b_proj):
        import jax, jax.numpy as jnp
        import numpy as np
        D = 128
        H = 16
        DH = D // H
        b, n, d = z.shape
        mu = jnp.mean(z, axis=-1, keepdims=True)
        var = jnp.var(z, axis=-1, keepdims=True)
        zn = (z - mu) / jnp.sqrt(var + 1e-05) * ln_w + ln_b
        qkv = (zn @ W_qkv + b_qkv).reshape(b, n, 3, H, DH)
        q = qkv[:, :, 0].transpose(0, 2, 1, 3)
        k = qkv[:, :, 1].transpose(0, 2, 1, 3)
        v = qkv[:, :, 2].transpose(0, 2, 1, 3)
        scale = 1.0 / jnp.sqrt(jnp.asarray(DH, dtype=z.dtype))
        scores = jnp.einsum('bhqd,bhkd->bhqk', q, k) * scale
        attn = jax.nn.softmax(scores, axis=-1)
        msa = jnp.einsum('bhqk,bhkd->bhqd', attn, v)
        msa_cat = msa.transpose(0, 2, 1, 3).reshape(b, n, d)
        out = msa_cat @ W_proj + b_proj
        return z + out

    def _L0_ffn_ref(x, gate_w, gate_b, w1, b1, w2, b2):
        import jax, jax.numpy as jnp
        import numpy as np
        D = 128
        N_EXP = 8
        TOP_K = 1
        b, s, d = x.shape
        xf = x.reshape(-1, d)
        logits = xf @ gate_w + gate_b
        pb = jax.nn.softmax(logits, axis=-1)
        _, idx = jax.lax.top_k(pb, TOP_K)
        sel = jnp.any(idx[:, :, None] == jnp.arange(N_EXP)[None, None, :], axis=1)
        weights = pb * sel

        def expert_step(acc, params):
            w1e, b1e, w2e, b2e, wgt = params
            h = jax.nn.gelu(xf @ w1e + b1e, approximate=False)
            y = h @ w2e + b2e
            return (acc + wgt[:, None] * y, None)
        out0 = jnp.zeros_like(xf)
        out, _ = jax.lax.scan(expert_step, out0, (w1, b1, w2, b2, weights.T))
        return out.reshape(b, s, d)
    x = L0_attn_z
    x = _layernorm(x + _L0_attn_ref(x, L0_attn_ln_w, L0_attn_ln_b, L0_attn_W_qkv, L0_attn_b_qkv, L0_attn_W_proj, L0_attn_b_proj), axis=-1)
    x = _layernorm(x + _L0_ffn_ref(x, L0_ffn_gate_w, L0_ffn_gate_b, L0_ffn_w1, L0_ffn_b1, L0_ffn_w2, L0_ffn_b2), axis=-1)
    return x

_drawn_inputs = setup_inputs


def setup_inputs(seed=0):
    import zlib

    import numpy as np

    out = dict(_drawn_inputs(seed))
    spreads = {'L0_attn_ln_w': (1.0, 0.6),
     'L0_attn_ln_b': (0.0, 0.8),
     'L0_attn_b_qkv': (0.0, 0.665),
     'L0_attn_b_proj': (0.0, 0.1),
     'L0_ffn_gate_b': (0.0, 0.5),
     'L0_ffn_b1': (0.0, 0.8),
     'L0_ffn_b2': (0.0, 0.474)}
    factors = {'L0_attn_W_qkv': 8.0,
     'L0_attn_W_proj': 4.265,
     'L0_ffn_gate_w': 3.063,
     'L0_ffn_w1': 5.991,
     'L0_ffn_w2': 5.461}
    for name, (base, spread) in spreads.items():
        noise = np.random.default_rng([zlib.crc32(name.encode()), seed]).standard_normal(out[name].shape)
        drawn = base * np.exp(spread * noise) if base else spread * noise
        out[name] = jnp.asarray(drawn.astype(out[name].dtype))
    for name, factor in factors.items():
        out[name] = (out[name] * factor).astype(out[name].dtype)
    return out
```

```python
import concourse.bass as bass
from concourse import mybir
from contextlib import ExitStack

F32 = mybir.dt.float32
BF16 = mybir.dt.bfloat16
I32 = mybir.dt.int32
U32 = mybir.dt.uint32
ALU = mybir.AluOpType
ACT = mybir.ActivationFunctionType
AX = mybir.AxisListType

P = 128
B, S, D = 8, 512, 128
H, DH = 16, 8
E, FF = 8, 512
QB = S // P
TILES = B * QB
GRP = 4
NG = H // GRP
UNITS = B * NG
PARTS = 3
ROWS = PARTS * PARTS * DH
KROWS = 96
HW = 32
EPS = 1e-5
SCALE = DH ** -0.5
ROW = D + 2
CAP = TILES * P + P
STEP = 4
NT = -(-(TILES + E - 1) // STEP) * STEP
FC = FF // P
PROJ_AT = {(1, 1): 0, (1, 2): 1, (2, 2): 2, (3, 2): 3}
PROJ_AFTER = {(1, 2): 0, (1, 3): 1, (2, 3): 2, (3, 3): 3}
NORM_AT = ((), (0,), (1,), (2, 3))
FAR = 1 << 20
ROUND = 1.5 * 2.0 ** 23


def build(nc, z, ln_w, ln_b, w_qk, w_v, b_qk, b_v, w_proj, b_proj, gate_w, gate_b, w1, b1, w2, b2, out):
    ctx = ExitStack()
    with ctx:
        def sb(name, shape, dt=F32):
            return ctx.enter_context(nc.sbuf_tensor(name, shape, dt))

        def sem(name):
            return ctx.enter_context(nc.semaphore(name))

        q_parts = nc.dram_tensor("q_parts", (B, PARTS * DH, H, S), BF16).ap()
        k_parts = nc.dram_tensor("k_parts", (B, 5 * DH, H, S), BF16).ap()
        routed = nc.dram_tensor("routed", (E * CAP, ROW), F32).ap()

        ident = sb("ident", [P, P])
        ident_b = sb("ident_b", [P, P], BF16)
        below = sb("below", [P, P], BF16)
        ones_b = sb("ones_b", [P, P], BF16)
        zero_rows = sb("zero_rows", [PARTS, S], BF16)
        one_rows = sb("one_rows", [PARTS, S], BF16)
        half = sb("half", [P, TILES])
        ln_wc, ln_bc = sb("ln_wc", [P, 1]), sb("ln_bc", [P, 1])
        b_qkc = sb("b_qkc", [P, 2])
        wqk_sb = sb("wqk_sb", [P, 2 * D])
        wv_sb = sb("wv_sb", [P, D])
        bv_sb = sb("bv_sb", [P, D])
        wp_sb = sb("wp_sb", [P, D])
        bp_sb = sb("bp_sb", [P, D])
        gw_sb = sb("gw_sb", [P, E])
        gb_sb = sb("gb_sb", [P, E])
        w1_sb = sb("w1_sb", [P, E * FF])
        w2_sb = sb("w2_sb", [P, E * FC * D])
        b1_sb = sb("b1_sb", [P, E * FF])
        b2_sb = sb("b2_sb", [P, E * D])

        x_sb = sb("x_sb", [P, TILES, ROW])
        v_all = sb("v_all", [P, TILES, D])

        stats = sb("stats", [P, QB, 6])
        mv = sb("mv", [P, TILES, 2])
        ve = sb("ve", [P, TILES])
        rstd = sb("rstd", [P, TILES])
        stats2 = sb("stats2", [P, TILES, 6])
        mean2 = sb("mean2", [P, TILES])
        mom = sb("mom", [P, 4, TILES])
        zn = sb("zn", [P, 2, QB, D])
        znT = sb("znT", [P, 2, S])
        rest = sb("rest", [P, 2, 2, S])
        parts = sb("parts", [P, 2, 2, PARTS, S], BF16)

        onehot = sb("onehot", [P, TILES, E], BF16)
        top, total, found, slot_f = (sb(n, [P, TILES]) for n in ("top", "total", "found", "slot_f"))
        slot = sb("slot", [P, TILES], U32)
        pad_f, pad_slot = sb("pad_f", [P, E]), sb("pad_slot", [P, E], U32)
        numbers = sb("numbers", [P, 2 * E + 1 + 2 * NT], I32)
        numbers_f = sb("numbers_f", [P, 2 * E + 1 + 2 * NT])
        pad_row = sb("pad_row", [P, ROW])
        tiles_of, ends0, ends1, weight_of = (sb(n, [1, E]) for n in ("tiles_of", "ends0", "ends1", "weight_of"))
        after, after_w = sb("after", [1, NT, E - 1]), sb("after_w", [1, NT, E - 1])
        table_f, table = sb("table_f", [1, 2, NT]), sb("table", [1, 2, NT], I32)
        limit = sb("limit", [1, 1])

        rows = sb("rows", [P, STEP, ROW])
        xT = sb("xT", [P, 2, P])
        pre, hid = rest[:, 0], rest[:, 1]
        hidT = zn[:, :, :, :].rearrange("p k t d -> p k (t d)")
        y_sb = sb("y_sb", [P, QB, D])
        res = sb("res", [P, STEP, D])
        res_number = sb("res_number", [P, STEP], I32)
        fstats = sb("fstats", [P, STEP, 6])
        fmean = sb("fmean", [P, STEP])
        fvar = sb("fvar", [P, STEP])
        frstd = sb("frstd", [P, STEP])
        final = sb("final", [P, STEP, D])
        out_number = sb("out_number", [P, STEP], I32)

        qs = sb("qs", [KROWS, NG, GRP, S], BF16)
        ks = sb("ks", [KROWS, NG, GRP, S], BF16)
        vs = sb("vs", [P, NG, QB, GRP, HW])
        negm = sb("negm", [P, QB, GRP])
        negm_r = sb("negm_r", [P, QB, GRP])
        negm_p = sb("negm_p", [P, QB, PARTS, GRP], BF16)
        mrow = sb("mrow", [PARTS * GRP, S], BF16)
        probs = sb("probs", [P, 2 * GRP, S])
        logits, shifted, ex, cand, onehot_f, *sums = (
            probs[:, k, 0:TILES * E].rearrange("p (t e) -> p t e", e=E) for k in range(7))
        oT = sb("oT", [P, NG, S])
        rec = sb("rec", [P, H])
        o_sb = sb("o_sb", [P, QB, D])
        oT_sb = sb("oT_sb", [P, P])

        ps = ctx.enter_context(nc.psum_tensor("ps", [P, 8, 512], F32))

        names = """consts weights moe_weights ident_ok stat_link stat_ok ve_ok rstd_ok ones_in
            max_ok max_used nm_link nm_ok mT_ok mrow_ok pair_ok exp_ok vs_ok pv_ok pv_copied
            tr_ok rec_ok norm_ok oT_ok oT_copied proj_ok y_ok y_kept moment_link stat2_link stat2_ok
            var2_ok rstd2_ok x1_ok x1T_ok x1T_copied logits_ok route_link shifted_ok ex_ok onehot_ok ranks_ok
            slots_ok table_ok numbers_ok routed_out consts2
            xT_ok xTc_ok mm1_ok add_ok gelu_ok hT_ok hTc_ok mm2_ok y1_ok res_ok fstat_link var_ok frstd_ok
            final_ok stored""".split()
        sm = {n: sem(n) for n in names}
        pr = {n: [sem(f"{n}{k}") for k in range(2)] for n in
              "zn_ok zT_ok znT_ok q_ok k_ok v_ok hi_ok rest_ok mid_ok lo_ok v_all_ok".split()}
        z_in = [sem(f"z_in{b}") for b in range(B)]
        rows_in = [sem(f"rows_in{k}") for k in range(STEP)]
        loaded = [sem(f"unit_loaded{g}") for g in range(NG)]
        mrow_in = [sem(f"mrow_in{g}") for g in range(NG)]
        parts_free = [sem(f"parts_out{k}") for k in range(2)]
        LOAD = 16 * 7

        block = ctx.enter_context(nc.Block())

        def heads(rows_):
            return rows_[:, :].rearrange("p (o n) -> p o n", o=1).to_broadcast([PARTS, GRP, S])

        @block.sync
        def _(sp):
            zt = z.rearrange("(t p) d -> p t d", p=P)
            for b in range(B):
                sp.dma_start(x_sb[:, QB * b:QB * (b + 1), 0:D], zt[:, QB * b:QB * (b + 1), :])\
                  .then_inc(z_in[b], 16)
                if b == 0:
                    col = lambda a: a.rearrange("(p o) -> p o", o=1)
                    row = lambda a: a.rearrange("(o n) -> o n", o=1).to_broadcast([P, a.shape[0]])
                    with nc.allow_non_contiguous_dma(reason="a few columns of parameters"):
                        for dst, src in ((ln_wc[:, :], col(ln_w)), (ln_bc[:, :], col(ln_b)),
                                         (b_qkc[:, :], b_qk.rearrange("(s p) -> p s", p=P)),
                                         (wqk_sb[:, :], w_qk), (wv_sb[:, :], w_v), (bv_sb[:, :], row(b_v)),
                                         (wp_sb[:, :], w_proj), (bp_sb[:, :], row(b_proj)),
                                         (gw_sb[:, :], gate_w), (gb_sb[:, :], row(gate_b))):
                            sp.dma_start(dst, src).then_inc(sm["weights"], 16)
            def pair(i, first):
                for par in range(2):
                    b = 2 * i + par
                    sp.wait_ge(pr["lo_ok"][par], 2 * i + 2)
                    sp.dma_start(q_parts[bass.ds(b, 1)].rearrange("o (t d) h n -> (o d h) t n", t=PARTS),
                                 parts[:, par, 0]).then_inc(parts_free[par], 16)
                    kd = k_parts[bass.ds(b, 1)].rearrange("o (t d) h n -> (o d h) t n", t=5)
                    sp.dma_start(kd[:, 0:PARTS, :], parts[:, par, 1]).then_inc(parts_free[par], 16)
                    sp.dma_start(kd[:, PARTS:5, :], parts[:, par, 1, 0:2]).then_inc(parts_free[par], 16)

            pair(0, True)
            with sp.Fori(1, B // 2) as i:
                pair(i, False)
            sp.wait_ge(sm["consts"], 5)
            for g in range(NG):
                sp.dma_start(ks[ROWS:ROWS + PARTS, g, :, :], heads(one_rows))\
                  .then_inc(sm["ones_in"], 16)
            for par in range(2):
                sp.wait_ge(parts_free[par], 48 * (B // 2))

            def load(b, g):
                for s in range(PARTS):
                    r = slice(s * PARTS * DH, (s + 1) * PARTS * DH)
                    sp.dma_start(qs[r, g], q_parts[bass.ds(b, 1), :, GRP * g:GRP * (g + 1), :]
                                 .rearrange("o r j n -> (o r) j n")).then_inc(loaded[g], 16)
                    sp.dma_start(ks[r, g], k_parts[bass.ds(b, 1), s * DH:(s + PARTS) * DH,
                                                   GRP * g:GRP * (g + 1), :]
                                 .rearrange("o r j n -> (o r) j n")).then_inc(loaded[g], 16)
                sp.dma_start(qs[ROWS:ROWS + PARTS, g, :, :], heads(zero_rows))\
                  .then_inc(loaded[g], 16)

            def mrow_out(v, g):
                sp.wait_ge(sm["mrow_ok"], v + 1)
                for a in range(PARTS):
                    sp.dma_start(qs[ROWS + a:ROWS + a + 1, g, :, :], mrow[GRP * a:GRP * (a + 1), :])\
                      .then_inc(mrow_in[g], 16)

            for g in range(3):
                load(0, g)
            mrow_out(0, 0)

            def slots(b, last):
                for g in range(NG):
                    s = NG * b + g
                    if not (last and g > 0):
                        if not (isinstance(b, int) and s == 0):
                            sp.wait_ge(sm["pair_ok"], 2 * QB * s)
                        load(b + (g + 3) // NG, (g + 3) % NG)
                    if not (last and g == NG - 1):
                        mrow_out(s + 1, (g + 1) % NG)

            slots(0, False)
            with sp.Fori(1, B - 1) as b:
                slots(b, False)
            slots(B - 1, True)

            def load_rows(i, k):
                at = sp.value_load(table[0:1, 0, bass.ds(i, 1)], min_val=0, max_val=E * CAP - P)
                sp.dma_start(rows[:, k, :], routed[bass.ds(at, P), :]).then_inc(rows_in[k], 16)

            sp.wait_ge(sm["table_ok"], 1)
            sp.wait_ge(sm["routed_out"], 16 * (TILES + E))
            for k in range(STEP):
                load_rows(k, k)
            with sp.Fori(0, NT // STEP - 1) as r:
                for k in range(STEP):
                    sp.wait_ge(sm["res_ok"], 2 * (STEP * r + k + 1))
                    load_rows(STEP * (r + 1) + k, k)
            sp.wait_ge(sm["stored"], 16 * NT)

        @block.gpsimd
        def _(pool):
            pool.memset(ident[:, :], 0.0).then_inc(sm["ident_ok"], 1)
            pool.memset(ones_b[:, :], 1.0).then_inc(sm["ident_ok"], 1)
            pool.memset(half[:, :], -0.5)
            pool.wait_ge(sm["ident_ok"], 2)
            pool.affine_select(out=ident[:, :], in_=ident[:, :], compare_op=ALU.not_equal, fill=1.0, base=0,
                               pattern=[[-1, P]], channel_multiplier=1).then_inc(sm["ident_ok"], 1)
            pool.affine_select(out=below[:, :], in_=ones_b[:, :], compare_op=ALU.is_gt, fill=0.0, base=0,
                               pattern=[[1, P]], channel_multiplier=-1).then_inc(sm["ident_ok"], 1)
            pool.wait_ge(sm["ident_ok"], 4)
            pool.tensor_copy(ident_b[:, :], ident[:, :]).then_inc(sm["ident_ok"], 1)
            pool.memset(zero_rows[:, :], 0.0).then_inc(sm["consts"], 1)
            pool.memset(one_rows[:, :], 1.0).then_inc(sm["consts"], 1)
            pool.wait_ge(sm["ident_ok"], 5)
            pool.wait_ge(sm["consts"], 2)
            for n, t in enumerate((qs, ks)):
                pool.memset(t[64:KROWS, :, :, :].rearrange("p g j n -> p (g j n)").bitcast(U32), 0)\
                    .then_inc(sm["consts"], 1)
            pool.wait_ge(sm["consts"], 4)
            pool.memset(vs[:, :, :, :, :], 0.0).then_inc(sm["vs_ok"], 1)
            pool.wait_ge(sm["vs_ok"], 1)
            pool.memset(vs[:, :, :, :, DH:DH + 1], 1.0).then_inc(sm["consts"], 1)
            for at, pat, base, ch in ((0, [[CAP, E]], 0, 0), (E, [[-1, E]], E, 0), (2 * E, [[0, 1]], 0, 1),
                                      (2 * E + 1, [[P, NT]], 0, 0), (2 * E + 1 + NT, [[1, NT]], 0, 0)):
                pool.iota(numbers[:, at:at + pat[0][1]], pattern=pat, base=base, channel_multiplier=ch)\
                    .then_inc(sm["consts2"], 1)
            pool.wait_ge(sm["consts2"], 5)
            pool.tensor_copy(numbers_f[:, :], numbers[:, :]).then_inc(sm["numbers_ok"], 1)
            pool.iota(x_sb[:, :, D + 1].bitcast(I32), pattern=[[P, TILES]], base=0, channel_multiplier=1)\
                .then_inc(sm["numbers_ok"], 1)
            pool.memset(pad_row[:, 0:D + 1], 0.0)
            pool.memset(pad_row[:, D + 1:ROW].bitcast(I32), FAR).then_inc(sm["numbers_ok"], 1)
            for b in range(B):
                r = slice(QB * b, QB * (b + 1))
                pool.wait_ge(sm["stat_ok"], b + 1)
                pool.tensor_scalar(ve[:, r], mv[:, r, 1], EPS, None, ALU.add).then_inc(sm["ve_ok"], 1)
                pool.wait_ge(sm["ve_ok"], b + 1)
                pool.tensor_tensor(rstd[:, r], ve[:, r], half[:, 0:QB], ALU.pow).then_inc(sm["rstd_ok"], 1)
            def pair(i, first):
                for par in range(2):
                    b = 2 * i + par
                    for side in range(2):
                        pool.wait_ge(pr["mid_ok"][par], 2 * i + side + 1)
                        pool.tensor_tensor(parts[:, par, side, 2], rest[:, par, side], parts[:, par, side, 1],
                                           ALU.subtract).then_inc(pr["lo_ok"][par], 1)

            pair(0, True)
            with pool.Fori(1, B // 2) as i:
                pair(i, False)

            def values(b, g):
                src = v_all[:, bass.ds(QB * b, QB), GRP * DH * g:GRP * DH * (g + 1)]
                pool.tensor_copy(vs[:, g, :, :, 0:DH], src.rearrange("p c (j d) -> p c j d", d=DH))\
                    .then_inc(sm["vs_ok"], 1)

            for par in range(2):
                pool.wait_ge(pr["v_all_ok"][par], B // 2)
            for g in range(NG):
                values(0, g)
            with pool.Fori(1, B) as b:
                for g in range(NG):
                    pool.wait_ge(sm["pv_ok"], QB * (NG * (b - 1) + g + 1))
                    values(b, g)

            pool.wait_ge(sm["var2_ok"], 1)
            pool.tensor_tensor(rstd[:, :], ve[:, :], half[:, :], ALU.pow).then_inc(sm["rstd2_ok"], 1)
            pool.wait_ge(sm["slots_ok"], 2)
            pool.wait_ge(sm["numbers_ok"], 3)
            for t in range(TILES):
                pool.indirect_dma_start(routed[:, :], bass.IndirectOffsetOnAxis(ap=slot[:, t:t + 1], axis=0),
                                        x_sb[:, t, :], None).then_inc(sm["routed_out"], 16)
            for e in range(E):
                pool.indirect_dma_start(routed[:, :], bass.IndirectOffsetOnAxis(ap=pad_slot[:, e:e + 1], axis=0),
                                        pad_row[:, :], None).then_inc(sm["routed_out"], 16)

            def store(r):
                pool.wait_ge(sm["var_ok"], r + 1)
                pool.tensor_tensor(frstd[:, :], fvar[:, :], half[:, 0:STEP], ALU.pow).then_inc(sm["frstd_ok"], 1)
                pool.wait_ge(sm["final_ok"], r + 1)
                for k in range(STEP):
                    pool.indirect_dma_start(
                        out[:, :], bass.IndirectOffsetOnAxis(ap=out_number[:, k:k + 1].bitcast(U32), axis=0),
                        final[:, k, :], None, bounds_check=TILES * P - 1, oob_is_err=False)\
                        .then_inc(sm["stored"], 16)

            for r in range(NT // STEP):
                store(r)

        @block.vector
        def _(dve):
            for b in range(B):
                dve.wait_ge(z_in[b], 16)
                for t in range(QB):
                    nc.vector.bn_stats(stats2[:, QB * b + t, :], x_sb[:, QB * b + t, 0:D]).then_inc(sm["stat_link"], 1)
                dve.wait_ge(sm["stat_link"], QB * b + QB)
                for t in range(QB):
                    last = nc.vector.bn_aggr(mv[:, QB * b + t, :], stats2[:, QB * b + t, :])
                last.then_inc(sm["stat_ok"], 1)
            dve.wait_ge(sm["weights"], 160)
            def pair(i, first):
                for par in range(2):
                    b = 2 * i + par
                    dve.wait_ge(sm["rstd_ok"], b + 1)
                    if not first:
                        dve.wait_ge(pr["zT_ok"][par], i)
                    for t in range(QB):
                        last = nc.vector.tensor_scalar(
                            zn[:, par, t, :], x_sb[:, bass.ds(QB * b + t, 1), 0:D].rearrange("p o d -> p (o d)"),
                            mv[:, bass.ds(QB * b + t, 1), 0], rstd[:, bass.ds(QB * b + t, 1)],
                            ALU.subtract, ALU.mult)
                    last.then_inc(pr["zn_ok"][par], 1)
                    dve.wait_ge(pr["zn_ok"][par], i + 1)
                    xb = x_sb[:, bass.ds(QB * b, QB), 0:D]
                    nc.vector.scalar_tensor_tensor(
                        out=xb, in0=xb, scalar=2.0,
                        in1=bp_sb[:, :].rearrange("p (o d) -> p o d", o=1).to_broadcast([P, QB, D]),
                        op0=ALU.mult, op1=ALU.add)
                    for side, name in ((0, "q_ok"), (1, "k_ok")):
                        dve.wait_ge(pr[name][par], i + 1)
                        dve.wait_ge(pr["hi_ok"][par], 2 * i + side + 1)
                        if not first:
                            dve.wait_ge(pr["lo_ok"][par], 2 * i)
                        nc.vector.scalar_tensor_tensor(
                            out=rest[:, par, side], in0=ps[:, 2 + 2 * side + par, :], scalar=b_qkc[:, side:side + 1],
                            in1=parts[:, par, side, 0], op0=ALU.add, op1=ALU.subtract).then_inc(pr["rest_ok"][par], 1)
                    dve.wait_ge(pr["v_ok"][par], i + 1)
                    nc.vector.tensor_tensor(
                        v_all[:, bass.ds(QB * b, QB), :], ps[:, 6 + par, :].rearrange("p (c d) -> p c d", d=D),
                        bv_sb[:, :].rearrange("p (o d) -> p o d", o=1).to_broadcast([P, QB, D]),
                        ALU.add).then_inc(pr["v_all_ok"][par], 1)

            pair(0, True)
            with dve.Fori(1, B // 2) as i:
                pair(i, False)

            def moments(st, mean, var, before):
                n = st.shape[1]
                sq, dif, dd, part = (mom[:, k, 0:n] for k in range(4))
                V = nc.vector
                V.tensor_tensor(sq, st[:, :, 2], st[:, :, 5], ALU.add).then_inc(sm["moment_link"], 1)
                V.tensor_tensor(dif, st[:, :, 1], st[:, :, 4], ALU.subtract).then_inc(sm["moment_link"], 1)
                V.tensor_tensor(part, st[:, :, 1], st[:, :, 4], ALU.add).then_inc(sm["moment_link"], 1)
                dve.wait_ge(sm["moment_link"], before + 2)
                V.tensor_tensor(dd, dif, dif, ALU.mult).then_inc(sm["moment_link"], 1)
                V.tensor_scalar(sq, sq, 1.0 / D, EPS, ALU.mult, ALU.add).then_inc(sm["moment_link"], 1)
                dve.wait_ge(sm["moment_link"], before + 5)
                V.tensor_scalar(mean, part, 0.5, None, ALU.mult).then_inc(sm["moment_link"], 1)
                dve.wait_ge(sm["moment_link"], before + 6)
                return V.scalar_tensor_tensor(out=var, in0=dd, scalar=0.25, in1=sq, op0=ALU.mult, op1=ALU.add)

            def maxima(v, j, qbs):
                for qb in qbs:
                    n = GRP * QB * v + QB * j + qb
                    if j == 0 and qb == 0 and not (isinstance(v, int) and v == 0):
                        dve.wait_ge(sm["nm_ok"], v)
                    dve.wait_ge(sm["max_ok"], n + 1)
                    nc.vector.tensor_reduce(negm[:, qb, j:j + 1], ps[:, 4 + qb % 2, :], AX.X, ALU.max,
                                            negate=True).then_inc(sm["max_used"], 1)

            def split_maxima(v):
                dve.wait_ge(sm["max_used"], GRP * QB * (v + 1))
                if not (isinstance(v, int) and v == 0):
                    dve.wait_ge(sm["mT_ok"], v)
                hi, mid, lo = (negm_p[:, :, a, :] for a in range(PARTS))
                nc.vector.tensor_copy(hi, negm[:, :, :]).then_inc(sm["nm_link"], 1)
                dve.wait_ge(sm["nm_link"], 3 * v + 1)
                nc.vector.tensor_tensor(negm_r[:, :, :], negm[:, :, :], hi, ALU.subtract)\
                    .then_inc(sm["nm_link"], 1)
                dve.wait_ge(sm["nm_link"], 3 * v + 2)
                nc.vector.tensor_copy(mid, negm_r[:, :, :]).then_inc(sm["nm_link"], 1)
                dve.wait_ge(sm["nm_link"], 3 * v + 3)
                nc.vector.tensor_tensor(lo, negm_r[:, :, :], mid, ALU.subtract).then_inc(sm["nm_ok"], 1)

            def normalise(ob, qb):
                dve.wait_ge(sm["tr_ok"], QB * ob + qb + 1)
                o = ps[:, 7, :].rearrange("p (h c) -> p h c", c=HW)
                if qb > 0:
                    dve.wait_ge(sm["norm_ok"], QB * ob + qb)
                nc.vector.reciprocal(rec[:, :], o[:, :, DH]).then_inc(sm["rec_ok"], 1)
                dve.wait_ge(sm["rec_ok"], QB * ob + qb + 1)
                nc.vector.tensor_tensor(o_sb[:, qb, :].rearrange("p (h d) -> p h d", d=DH), o[:, :, 0:DH],
                                        rec[:, :].rearrange("p (h o) -> p h o", o=1).to_broadcast([P, H, DH]),
                                        ALU.mult).then_inc(sm["norm_ok"], 1)

            def residual(ob, qb):
                t = QB * ob + qb
                dve.wait_ge(sm["proj_ok"], t + 1)
                x = x_sb[:, bass.ds(t, 1), 0:D].rearrange("p o d -> p (o d)")
                nc.vector.tensor_tensor(y_sb[:, qb, :], ps[:, 7, P:2 * P], x, ALU.add).then_inc(sm["y_ok"], 1)
                dve.wait_ge(sm["y_ok"], t + 1)
                nc.vector.bn_stats(stats[:, qb, :], y_sb[:, qb, :]).then_inc(sm["stat2_link"], 1)
                if qb == QB - 1:
                    nc.vector.tensor_copy(x_sb[:, bass.ds(QB * ob, QB), 0:D], y_sb[:, :, :])\
                      .then_inc(sm["y_kept"], 1)
                    dve.wait_ge(sm["stat2_link"], t + 1)
                    nc.vector.tensor_copy(stats2[:, bass.ds(QB * ob, QB), :], stats[:, :, :])\
                      .then_inc(sm["stat2_ok"], 1)

            def slots(b, first, last):
                for g in range(NG):
                    s = NG * b + g
                    for kc in range(QB):
                        if not (last and g >= 2):
                            maxima(s + 2, kc, (0, 1))
                        if not first and (g, kc) in PROJ_AFTER:
                            if PROJ_AFTER[g, kc] == 0:
                                dve.wait_ge(sm["max_used"], GRP * QB * (s + 2) + QB * kc + 2)
                            residual(b - 1, PROJ_AFTER[g, kc])
                        if not (last and g >= 2):
                            maxima(s + 2, kc, (2, 3))
                        if not first and g == 0:
                            for qb in NORM_AT[kc]:
                                if qb == 0:
                                    dve.wait_ge(sm["max_used"], GRP * QB * (s + 2) + QB * (kc + 1))
                                normalise(b - 1, qb)
                    if not (last and g >= 2):
                        split_maxima(s + 2)

            for v in range(2):
                for j in range(GRP):
                    maxima(v, j, range(QB))
                split_maxima(v)
            slots(0, True, False)
            with dve.Fori(1, B - 1) as b:
                slots(b, False, False)
            slots(B - 1, False, True)
            for qb in range(QB):
                normalise(B - 1, qb)
            for qb in range(QB):
                residual(B - 1, qb)

            dve.wait_ge(sm["stat2_ok"], B)
            dve.wait_ge(sm["y_kept"], B)
            moments(stats2[:, :, :], mean2[:, :], ve[:, :], 0).then_inc(sm["var2_ok"], 1)
            dve.wait_ge(sm["rstd2_ok"], 1)
            with dve.Fori(0, B) as b:
                for t in range(QB):
                    x = x_sb[:, bass.ds(QB * b + t, 1), 0:D].rearrange("p o d -> p (o d)")
                    last = nc.vector.tensor_scalar(x, x, mean2[:, bass.ds(QB * b + t, 1)],
                                                   rstd[:, bass.ds(QB * b + t, 1)], ALU.subtract, ALU.mult)
                last.then_inc(sm["x1_ok"], 1)

            links = [0]

            def link(op):
                links[0] += 1
                op.then_inc(sm["route_link"], 1)
                dve.wait_ge(sm["route_link"], links[0])

            def over_tiles(a):
                return a.rearrange("p (o e) -> p o e", o=1).to_broadcast([P, TILES, E])

            def over_experts(a):
                return a.rearrange("p (t o) -> p t o", o=1).to_broadcast([P, TILES, E])

            psx = lambda bank: ps[:, bank, 0:TILES * E].rearrange("p (t e) -> p t e", e=E)
            cap, rev = numbers_f[:, 0:E], numbers_f[:, E:2 * E]
            lane = numbers_f[:, 2 * E:2 * E + 1]
            first_row = numbers_f[0:1, 2 * E + 1:2 * E + 1 + NT]
            tile_no = numbers_f[0:1, 2 * E + 1 + NT:]
            V = nc.vector
            dve.wait_ge(sm["logits_ok"], B)
            dve.wait_ge(sm["numbers_ok"], 3)
            link(V.tensor_tensor(logits[:, :, :], psx(2), over_tiles(gb_sb[:, :]), ALU.add))
            link(V.tensor_reduce(top[:, :], logits[:, :, :], AX.X, ALU.max))
            V.tensor_tensor(shifted[:, :, :], logits[:, :, :], over_experts(top[:, :]), ALU.subtract)\
                .then_inc(sm["shifted_ok"], 1)
            link(V.tensor_tensor(ex[:, :, :], logits[:, :, :], over_experts(top[:, :]), ALU.is_equal))
            link(V.tensor_tensor(cand[:, :, :], ex[:, :, :], over_tiles(rev), ALU.mult))
            link(V.tensor_reduce(found[:, :], cand[:, :, :], AX.X, ALU.max))
            link(V.tensor_tensor(onehot_f[:, :, :], cand[:, :, :], over_experts(found[:, :]), ALU.is_equal))
            V.tensor_copy(onehot[:, :, :], onehot_f[:, :, :]).then_inc(sm["onehot_ok"], 1)
            dve.wait_ge(sm["ex_ok"], 1)
            link(V.tensor_reduce(total[:, :], shifted[:, :, :], AX.X, ALU.add))
            link(V.reciprocal(x_sb[:, :, D], total[:, :]))
            dve.wait_ge(sm["ranks_ok"], 1)
            link(V.tensor_copy(sums[0][:, :, :], psx(4)))
            a, b_ = sums
            n = 1
            while n < TILES:
                V.tensor_copy(b_[:, 0:n, :], a[:, 0:n, :])
                link(V.tensor_tensor(b_[:, n:, :], a[:, n:, :], a[:, 0:TILES - n, :], ALU.add))
                a, b_ = b_, a
                n *= 2
            count = a[:, TILES - 1, :]
            link(V.tensor_tensor(pad_f[:, :], count, cap, ALU.add))
            V.tensor_scalar(pad_slot[:, :], pad_f[:, :], lane, None, ALU.add).then_inc(sm["slots_ok"], 1)
            link(V.tensor_tensor(logits[:, :, :], a[:, :, :], psx(4), ALU.subtract))
            link(V.tensor_tensor(cand[:, :, :], psx(3), logits[:, :, :], ALU.add))
            link(V.tensor_tensor(logits[:, :, :], cand[:, :, :], over_tiles(cap), ALU.add))
            link(V.tensor_tensor(cand[:, :, :], logits[:, :, :], onehot_f[:, :, :], ALU.mult))
            link(V.tensor_reduce(slot_f[:, :], cand[:, :, :], AX.X, ALU.add))
            V.tensor_copy(slot[:, :], slot_f[:, :]).then_inc(sm["slots_ok"], 1)
            c0 = count[0:1, :]
            link(V.tensor_scalar(ends0[:, :], c0, 1.0 / P, (P - 1) / (2.0 * P), ALU.mult, ALU.add))
            link(V.tensor_scalar(ends1[:, :], ends0[:, :], ROUND, None, ALU.add))
            link(V.tensor_scalar(tiles_of[:, :], ends1[:, :], -ROUND, None, ALU.add))
            a, b_ = tiles_of, ends0
            for n in (1, 2, 4):
                V.tensor_copy(b_[:, 0:n], a[:, 0:n])
                link(V.tensor_tensor(b_[:, n:], a[:, n:], a[:, 0:E - n], ALU.add))
                a, b_ = b_, (ends1 if b_ is ends0 else ends0)
            ends = a
            shape = [1, NT, E - 1]
            link(V.tensor_tensor(after[:, :, :], tile_no.rearrange("p (i o) -> p i o", o=1).to_broadcast(shape),
                                 ends[:, 0:E - 1].rearrange("p (o e) -> p o e", o=1).to_broadcast(shape),
                                 ALU.is_ge))
            link(V.tensor_scalar(weight_of[:, :], tiles_of[:, :], -float(P), float(CAP), ALU.mult, ALU.add))
            link(V.tensor_tensor(after_w[:, :, :], after[:, :, :],
                                 weight_of[:, 0:E - 1].rearrange("p (o e) -> p o e", o=1).to_broadcast(shape),
                                 ALU.mult))
            link(V.tensor_reduce(table_f[:, 1, :], after[:, :, :], AX.X, ALU.add))
            link(V.tensor_reduce(table_f[:, 0, :], after_w[:, :, :], AX.X, ALU.add))
            link(V.tensor_tensor(table_f[:, 0, :], table_f[:, 0, :], first_row, ALU.add))
            link(V.tensor_scalar(limit[:, :], c0[:, E - 1:E], float((E - 1) * CAP), None, ALU.add))
            link(V.tensor_scalar(table_f[:, 0, :], table_f[:, 0, :], limit[:, :], None, ALU.min))
            V.tensor_copy(table[:, :, :], table_f[:, :, :]).then_inc(sm["table_ok"], 1)
            dve.wait_ge(sm["table_ok"], 1)
            dve.wait_ge(sm["moe_weights"], 64)

            def add_bias(i, k):
                dve.wait_ge(sm["mm1_ok"], i + 1)
                if not (isinstance(i, int) and i < 2):
                    dve.wait_ge(sm["gelu_ok"], i - 1)
                e = dve.value_load(table[0:1, 1, bass.ds(i, 1)], min_val=0, max_val=E - 1)
                V.tensor_tensor(pre[:, k % 2, :], ps[:, 1 + k % 2, :], b1_sb[:, bass.ds(e * FF, FF)], ALU.add)\
                    .then_inc(sm["add_ok"], 1)

            def combine(i, k, r):
                e = dve.value_load(table[0:1, 1, bass.ds(i, 1)], min_val=0, max_val=E - 1)
                if k == 0:
                    dve.wait_ge(sm["var_ok"], r)
                    dve.wait_ge(sm["final_ok"], r)
                dve.wait_ge(sm["mm2_ok"], i + 1)
                V.tensor_tensor(y_sb[:, k, :], ps[:, 4 + k % 2, 0:D], b2_sb[:, bass.ds(e * D, D)], ALU.add)\
                    .then_inc(sm["y1_ok"], 1)
                V.tensor_copy(res_number[:, k:k + 1], rows[:, k, D + 1:ROW].bitcast(I32)).then_inc(sm["res_ok"], 1)
                dve.wait_ge(sm["y1_ok"], i + 1)
                V.scalar_tensor_tensor(out=res[:, k, :], in0=y_sb[:, k, :], scalar=rows[:, k, D:D + 1],
                                       in1=rows[:, k, 0:D], op0=ALU.mult, op1=ALU.add).then_inc(sm["res_ok"], 1)
                dve.wait_ge(sm["res_ok"], 2 * i + 2)
                V.bn_stats(fstats[:, k, :], res[:, k, :]).then_inc(sm["fstat_link"], 1)

            def variances(r):
                dve.wait_ge(sm["fstat_link"], STEP * (r + 1))
                moments(fstats[:, :, :], fmean[:, :], fvar[:, :], 6 * (r + 1)).then_inc(sm["var_ok"], 1)

            def finish(r):
                dve.wait_ge(sm["frstd_ok"], r + 1)
                if not (isinstance(r, int) and r == 0):
                    dve.wait_ge(sm["stored"], 16 * STEP * r)
                V.tensor_copy(out_number[:, :], res_number[:, :])
                for k in range(STEP):
                    last = V.tensor_scalar(final[:, k, :], res[:, k, :], fmean[:, k:k + 1], frstd[:, k:k + 1],
                                           ALU.subtract, ALU.mult)
                last.then_inc(sm["final_ok"], 1)

            def steps(r, first, last):
                for k in range(STEP):
                    i = STEP * r + k
                    if not (last and k == STEP - 1):
                        add_bias(i + 1, (k + 1) % STEP)
                    if k == 0 and not first:
                        finish(r - 1)
                    combine(i, k, r)
                variances(r)

            add_bias(0, 0)
            steps(0, True, False)
            with dve.Fori(1, NT // STEP - 1) as r:
                steps(r, False, False)
            steps(NT // STEP - 1, False, True)
            finish(NT // STEP - 1)

        @block.scalar
        def _(act):
            act.dma_start(w1_sb[:, :].rearrange("p (e f) -> p e f", e=E), w1.rearrange("e d f -> d e f"))\
               .then_inc(sm["moe_weights"], 16)
            act.dma_start(w2_sb[:, :].rearrange("p (e c d) -> p (e c) d", e=E, d=D),
                          w2.rearrange("e (c f) d -> f (e c) d", f=P)).then_inc(sm["moe_weights"], 16)
            act.dma_start(b1_sb[:, :], b1.rearrange("(o n) -> o n", o=1).to_broadcast([P, E * FF]))\
               .then_inc(sm["moe_weights"], 16)
            act.dma_start(b2_sb[:, :], b2.rearrange("(o n) -> o n", o=1).to_broadcast([P, E * D]))\
               .then_inc(sm["moe_weights"], 16)
            act.wait_ge(sm["weights"], 160)
            def pair(i, first):
                for par in range(2):
                    b = 2 * i + par
                    act.wait_ge(pr["zT_ok"][par], i + 1)
                    if not first:
                        act.wait_ge(pr["v_ok"][par], i)
                    nc.scalar.activation(znT[:, par, :], ps[:, par, :], ACT.Identity, bias=ln_bc[:, 0:1],
                                         scale=ln_wc[:, 0:1]).then_inc(pr["znT_ok"][par], 1)
                    for side, name in ((0, "q_ok"), (1, "k_ok")):
                        act.wait_ge(pr[name][par], i + 1)
                        if not first:
                            act.wait_ge(parts_free[par], 48 * i)
                        nc.scalar.activation(parts[:, par, side, 0], ps[:, 2 + 2 * side + par, :], ACT.Identity,
                                             bias=b_qkc[:, side:side + 1]).then_inc(pr["hi_ok"][par], 1)
                    for side in range(2):
                        act.wait_ge(pr["rest_ok"][par], 2 * i + side + 1)
                        nc.scalar.activation(parts[:, par, side, 1], rest[:, par, side], ACT.Copy)\
                          .then_inc(pr["mid_ok"][par], 1)

            pair(0, True)
            with act.Fori(1, B // 2) as i:
                pair(i, False)

            def exps(s, kc, jp):
                n = 2 * QB * s + 2 * kc + jp
                act.wait_ge(sm["pair_ok"], n + 1)
                if not (isinstance(s, int) and s == 0 and kc < 2):
                    act.wait_ge(sm["pv_ok"], QB * s + kc - 1)
                k = GRP * (kc % 2) + 2 * jp
                nc.scalar.activation(probs[:, k:k + 2, :], ps[:, 2 * jp:2 * jp + 2, :], ACT.Exp, scale=SCALE)\
                  .then_inc(sm["exp_ok"], 1)

            def copy_pv(s, g, b=None):
                act.wait_ge(sm["pv_ok"], QB * (s + 1))
                if g == 0 and b is not None:
                    act.wait_ge(sm["tr_ok"], QB * b)
                nc.scalar.activation(oT[:, g, :], ps[:, 6, :], ACT.Copy).then_inc(sm["pv_copied"], 1)

            def copy_mrow(v):
                act.wait_ge(sm["mT_ok"], v + 1)
                nc.scalar.activation(mrow[:, :], ps[0:PARTS * GRP, 7, :], ACT.Copy).then_inc(sm["mrow_ok"], 1)

            def copy_oT(ob, qb):
                act.wait_ge(sm["oT_ok"], QB * ob + qb + 1)
                nc.scalar.activation(oT_sb[:, :], ps[:, 7, 0:P], ACT.Copy).then_inc(sm["oT_copied"], 1)

            def slots(b, first, last):
                for g in range(NG):
                    s = NG * b + g
                    for kc in range(QB):
                        exps(s, kc, 0)
                        if kc == 1 and not (last and g == NG - 1):
                            act.wait_ge(mrow_in[g], 48 * (b + 1))
                            copy_mrow(s + 1)
                        exps(s, kc, 1)
                        if kc == 0 and not (first and g == 0):
                            copy_pv(s - 1, (g - 1) % NG, None if first else b)
                        if not first and (g, kc) in PROJ_AT:
                            copy_oT(b - 1, PROJ_AT[g, kc])

            copy_mrow(0)
            slots(0, True, False)
            with act.Fori(1, B - 1) as b:
                slots(b, False, False)
            slots(B - 1, False, True)
            copy_pv(UNITS - 1, NG - 1)
            for qb in range(QB):
                copy_oT(B - 1, qb)

            for b in range(B):
                act.wait_ge(sm["x1T_ok"], b + 1)
                if b >= 2:
                    act.wait_ge(sm["logits_ok"], b - 1)
                nc.scalar.activation(znT[:, b % 2, :], ps[:, b % 2, :], ACT.Copy).then_inc(sm["x1T_copied"], 1)
            act.wait_ge(sm["shifted_ok"], 1)
            nc.scalar.activation(shifted[:, :, :], shifted[:, :, :], ACT.Exp).then_inc(sm["ex_ok"], 1)

            def copy_xT(i, k):
                act.wait_ge(sm["xT_ok"], i + 1)
                if not (isinstance(i, int) and i < 2):
                    act.wait_ge(sm["mm1_ok"], i - 1)
                nc.scalar.activation(xT[:, k % 2, :], ps[:, 0, 0:P], ACT.Copy).then_inc(sm["xTc_ok"], 1)

            def gelu(i, k):
                act.wait_ge(sm["add_ok"], i + 1)
                if not (isinstance(i, int) and i < 2):
                    act.wait_ge(sm["hT_ok"], i - 1)
                nc.scalar.activation(hid[:, k % 2, :], pre[:, k % 2, :], ACT.Gelu).then_inc(sm["gelu_ok"], 1)

            def copy_hT(i, k):
                act.wait_ge(sm["hT_ok"], i + 1)
                if not (isinstance(i, int) and i < 2):
                    act.wait_ge(sm["mm2_ok"], i - 1)
                nc.scalar.activation(hidT[:, k % 2, :], ps[:, 3, :], ACT.Copy).then_inc(sm["hTc_ok"], 1)

            def steps(r, last):
                for k in range(STEP):
                    i = STEP * r + k
                    copy_hT(i, k)
                    if not (last and k >= STEP - 2):
                        copy_xT(i + 2, (k + 2) % STEP)
                    if not (last and k == STEP - 1):
                        gelu(i + 1, (k + 1) % STEP)

            copy_xT(0, 0)
            copy_xT(1, 1)
            gelu(0, 0)
            steps(0, False)
            with act.Fori(1, NT // STEP - 1) as r:
                steps(r, False)
            steps(NT // STEP - 1, True)

        @block.tensor
        def _(pe):
            pe.wait_ge(sm["ident_ok"], 5)
            pe.wait_ge(sm["weights"], 160)
            def pair(i, first):
                for par in range(2):
                    b = 2 * i + par
                    pe.wait_ge(pr["zn_ok"][par], i + 1)
                    if not first:
                        pe.wait_ge(pr["znT_ok"][par], i)
                    for t in range(QB):
                        last = nc.tensor.transpose(ps[:, par, P * t:P * (t + 1)], zn[:, par, t, :], ident[:, :])
                    last.then_inc(pr["zT_ok"][par], 1)
                    pe.wait_ge(pr["znT_ok"][par], i + 1)
                    if not first:
                        pe.wait_ge(pr["rest_ok"][par], 2 * i)
                    for side, name in ((0, "q_ok"), (1, "k_ok")):
                        nc.tensor.matmul(ps[:, 2 + 2 * side + par, :], wqk_sb[:, D * side:D * (side + 1)],
                                         znT[:, par, :], start=True, stop=True).then_inc(pr[name][par], 1)
                    if not first:
                        pe.wait_ge(pr["v_all_ok"][par], i)
                    for t in range(QB):
                        last = nc.tensor.matmul(ps[:, 6 + par, P * t:P * (t + 1)], znT[:, par, P * t:P * (t + 1)],
                                                wv_sb[:, :], start=True, stop=True)
                    last.then_inc(pr["v_ok"][par], 1)

            pair(0, True)
            with pe.Fori(1, B // 2) as i:
                pair(i, False)
            for par in range(2):
                pe.wait_ge(pr["rest_ok"][par], B)
                pe.wait_ge(pr["hi_ok"][par], B)
                pe.wait_ge(pr["v_all_ok"][par], B // 2)
                pe.wait_ge(pr["znT_ok"][par], B // 2)
            pe.wait_ge(sm["consts"], 5)
            pe.wait_ge(sm["ones_in"], 16 * NG)

            def maximum_scores(v, g, j, qb):
                n = GRP * QB * v + QB * j + qb
                if not (isinstance(n, int) and n < 2):
                    pe.wait_ge(sm["max_used"], n - 1)
                nc.tensor.matmul(ps[:, 4 + qb % 2, :], qs[:, g, j, P * qb:P * (qb + 1)], ks[:, g, j, :],
                                 start=True, stop=True).then_inc(sm["max_ok"], 1)

            def scores(s, g, kc, j):
                n = 2 * QB * s + 2 * kc + j // 2
                if j % 2 == 0 and not (isinstance(n, int) and n < 2):
                    pe.wait_ge(sm["exp_ok"], n - 1)
                last = nc.tensor.matmul(ps[:, j, :], ks[:, g, j, P * kc:P * (kc + 1)], qs[:, g, j, :],
                                        start=True, stop=True)
                if j % 2:
                    last.then_inc(sm["pair_ok"], 1)

            def pv(s, g, kc):
                if kc == 0:
                    pe.wait_ge(sm["vs_ok"], s + 2)
                    if not (isinstance(s, int) and s == 0):
                        pe.wait_ge(sm["pv_copied"], s)
                pe.wait_ge(sm["exp_ok"], 2 * QB * s + 2 * kc + 2)
                for j in range(GRP):
                    last = nc.tensor.matmul(ps[HW * j:HW * (j + 1), 6, :], vs[:, g, kc, j, :],
                                            probs[:, GRP * (kc % 2) + j, :], start=(kc == 0), stop=(kc == QB - 1))
                last.then_inc(sm["pv_ok"], 1)

            def maxima_to_rows(v):
                pe.wait_ge(sm["nm_ok"], v + 1)
                for qb in range(QB):
                    last = nc.tensor.matmul(ps[0:PARTS * GRP, 7, P * qb:P * (qb + 1)],
                                            negm_p[:, qb].rearrange("p a j -> p (a j)"), ident_b[:, :],
                                            start=True, stop=True)
                last.then_inc(sm["mT_ok"], 1)

            def to_tokens(ob, qb):
                pe.wait_ge(sm["pv_copied"], NG * (ob + 1))
                if qb > 0:
                    pe.wait_ge(sm["norm_ok"], QB * ob + qb)
                for g in range(NG):
                    last = nc.tensor.transpose(ps[:, 7, P * g:P * (g + 1)], oT[:, g, P * qb:P * (qb + 1)],
                                               ident[:, :])
                last.then_inc(sm["tr_ok"], 1)

            def to_channels(ob, qb):
                pe.wait_ge(sm["norm_ok"], QB * (ob + 1))
                if qb > 0:
                    pe.wait_ge(sm["y_ok"], QB * ob + qb)
                nc.tensor.transpose(ps[:, 7, 0:P], o_sb[:, qb, :], ident[:, :]).then_inc(sm["oT_ok"], 1)

            def project(ob, qb):
                pe.wait_ge(sm["oT_copied"], QB * ob + qb + 1)
                nc.tensor.matmul(ps[:, 7, P:2 * P], oT_sb[:, :], wp_sb[:, :], start=True, stop=True)\
                  .then_inc(sm["proj_ok"], 1)

            def slots(b, first, last):
                for g in range(NG):
                    s = NG * b + g
                    pe.wait_ge(mrow_in[g], 48 * (b + 1))
                    if not (last and g >= 2):
                        pe.wait_ge(loaded[(g + 2) % NG], LOAD * (b + (g + 2) // NG + 1))
                    for kc in range(QB):
                        for j in range(GRP):
                            scores(s, g, kc, j)
                            if not (last and g >= 2):
                                maximum_scores(s + 2, (g + 2) % NG, kc, j)
                        if not first and (g, kc) in PROJ_AT:
                            if not (last and g == NG - 1):
                                pe.wait_ge(sm["mrow_ok"], s + 2)
                            to_channels(b - 1, PROJ_AT[g, kc])
                        if not first and g == 0 and kc > 0:
                            pe.wait_ge(sm["mrow_ok"], s + 2)
                            to_tokens(b - 1, kc - 1)
                        if kc > 0:
                            pv(s, g, kc - 1)
                        elif not (first and g == 0):
                            pv(s - 1, (g - 1) % NG, QB - 1)
                        if kc == 0 and not (last and g == NG - 1):
                            if not (first and g == 0):
                                pe.wait_ge(sm["mrow_ok"], s + 1)
                            maxima_to_rows(s + 1)
                        if not first and (g, kc) in PROJ_AT:
                            project(b - 1, PROJ_AT[g, kc])
                        if not first and g == 0 and kc == QB - 1:
                            to_tokens(b - 1, QB - 1)

            for v in range(2):
                pe.wait_ge(loaded[v], LOAD)
                for j in range(GRP):
                    for qb in range(QB):
                        maximum_scores(v, v, j, qb)
            maxima_to_rows(0)
            pe.wait_ge(sm["mrow_ok"], 1)
            slots(0, True, False)
            with pe.Fori(1, B - 1) as b:
                slots(b, False, False)
            slots(B - 1, False, True)
            pv(UNITS - 1, NG - 1, QB - 1)
            pe.wait_ge(sm["y_ok"], QB * (B - 1))
            for qb in range(QB):
                to_tokens(B - 1, qb)
            for qb in range(QB):
                to_channels(B - 1, qb)
                project(B - 1, qb)

            def x1_transposes(b):
                pe.wait_ge(sm["x1_ok"], b + 1)
                if b >= 2:
                    pe.wait_ge(sm["x1T_copied"], b - 1)
                for t in range(QB):
                    last = nc.tensor.transpose(ps[:, b % 2, P * t:P * (t + 1)], x_sb[:, QB * b + t, 0:D],
                                               ident[:, :])
                last.then_inc(sm["x1T_ok"], 1)

            x1_transposes(0)
            for b in range(B):
                if b + 1 < B:
                    x1_transposes(b + 1)
                pe.wait_ge(sm["x1T_copied"], b + 1)
                for t in range(QB):
                    at = (QB * b + t) * E
                    last = nc.tensor.matmul(ps[:, 2, at:at + E], znT[:, b % 2, P * t:P * (t + 1)], gw_sb[:, :],
                                            start=True, stop=True)
                last.then_inc(sm["logits_ok"], 1)
            pe.wait_ge(sm["onehot_ok"], 1)
            nc.tensor.matmul(ps[:, 3, 0:TILES * E], below[:, :], onehot[:, :, :].rearrange("p t e -> p (t e)"),
                             start=True, stop=True)
            nc.tensor.matmul(ps[:, 4, 0:TILES * E], ones_b[:, :], onehot[:, :, :].rearrange("p t e -> p (t e)"),
                             start=True, stop=True).then_inc(sm["ranks_ok"], 1)
            pe.wait_ge(sm["table_ok"], 1)
            pe.wait_ge(sm["moe_weights"], 64)

            def transpose_rows(i, k, r):
                pe.wait_ge(rows_in[k], 16 * (r + 1))
                if not (isinstance(i, int) and i == 0):
                    pe.wait_ge(sm["xTc_ok"], i)
                nc.tensor.transpose(ps[:, 0, 0:P], rows[:, k, 0:D], ident[:, :]).then_inc(sm["xT_ok"], 1)

            def up(i, k):
                e = pe.value_load(table[0:1, 1, bass.ds(i, 1)], min_val=0, max_val=E - 1)
                pe.wait_ge(sm["xTc_ok"], i + 1)
                if not (isinstance(i, int) and i < 2):
                    pe.wait_ge(sm["add_ok"], i - 1)
                nc.tensor.matmul(ps[:, 1 + k % 2, :], xT[:, k % 2, :], w1_sb[:, bass.ds(e * FF, FF)],
                                 start=True, stop=True).then_inc(sm["mm1_ok"], 1)

            def transpose_hidden(i, k):
                pe.wait_ge(sm["gelu_ok"], i + 1)
                if not (isinstance(i, int) and i == 0):
                    pe.wait_ge(sm["hTc_ok"], i)
                for c in range(FC):
                    last = nc.tensor.transpose(ps[:, 3, P * c:P * (c + 1)], hid[:, k % 2, P * c:P * (c + 1)],
                                               ident[:, :])
                last.then_inc(sm["hT_ok"], 1)

            def down(i, k):
                e = pe.value_load(table[0:1, 1, bass.ds(i, 1)], min_val=0, max_val=E - 1)
                pe.wait_ge(sm["hTc_ok"], i + 1)
                if not (isinstance(i, int) and i < 2):
                    pe.wait_ge(sm["y1_ok"], i - 1)
                for c in range(FC):
                    last = nc.tensor.matmul(ps[:, 4 + k % 2, 0:D], hidT[:, k % 2, P * c:P * (c + 1)],
                                            w2_sb[:, bass.ds(e * (FC * D) + c * D, D)],
                                            start=(c == 0), stop=(c == FC - 1))
                last.then_inc(sm["mm2_ok"], 1)

            def steps(r, last):
                for k in range(STEP):
                    i = STEP * r + k
                    transpose_hidden(i, k)
                    if not (last and k == STEP - 1):
                        up(i + 1, (k + 1) % STEP)
                    if not (last and k >= STEP - 2):
                        transpose_rows(i + 2, (k + 2) % STEP, r + (k + 2) // STEP)
                    down(i, k)

            transpose_rows(0, 0, 0)
            up(0, 0)
            transpose_rows(1, 1, 0)
            steps(0, False)
            with pe.Fori(1, NT // STEP - 1) as r:
                steps(r, False)
            steps(NT // STEP - 1, True)


_INS = ["z", "ln_w", "ln_b", "w_qk", "w_v", "b_qk", "b_v", "w_proj", "b_proj", "gate_w", "gate_b",
        "w1", "b1", "w2", "b2"]


def kernel(**inputs):
    import numpy as np
    import concourse.bacc as bacc
    from concourse.bass_utils import run_bass_kernel_spmd

    def given(name):
        return np.asarray(inputs[name])

    z = given("L0_attn_z")
    w_qkv, b_qkv = given("L0_attn_W_qkv"), given("L0_attn_b_qkv")
    by_channel = np.arange(D).reshape(H, DH).T.ravel()
    qk = np.concatenate([by_channel, D + by_channel])
    arrays = {
        "z": z.reshape(B * S, D), "ln_w": given("L0_attn_ln_w"), "ln_b": given("L0_attn_ln_b"),
        "w_qk": w_qkv[:, qk], "w_v": w_qkv[:, 2 * D:], "b_qk": b_qkv[qk], "b_v": b_qkv[2 * D:],
        "w_proj": given("L0_attn_W_proj"), "b_proj": given("L0_attn_b_proj"),
        "gate_w": given("L0_ffn_gate_w"), "gate_b": given("L0_ffn_gate_b"),
        "w1": given("L0_ffn_w1"), "b1": given("L0_ffn_b1").reshape(E * FF),
        "w2": given("L0_ffn_w2"), "b2": given("L0_ffn_b2").reshape(E * D),
    }
    arrays = {n: np.ascontiguousarray(arrays[n]) for n in _INS}
    nc = bacc.Bacc("TRN2", target_bir_lowering=False, num_devices=1)
    args = [nc.dram_tensor(n, arrays[n].shape, mybir.dt.from_np(arrays[n].dtype), kind="ExternalInput").ap()
            for n in _INS]
    out = nc.dram_tensor("out", (B * S, D), F32, kind="ExternalOutput").ap()
    build(nc, *args, out)
    r = run_bass_kernel_spmd(nc, [arrays], core_ids=[0])
    return r.results[0]["out"].reshape(B, S, D)
```

```python
import concourse.bass as bass
from concourse import mybir
from contextlib import ExitStack

F32 = mybir.dt.float32
BF16 = mybir.dt.bfloat16
I32 = mybir.dt.int32
U32 = mybir.dt.uint32
ALU = mybir.AluOpType
ACT = mybir.ActivationFunctionType
AX = mybir.AxisListType

P = 128
B, S, D = 8, 512, 128
H, DH = 16, 8
E, FF = 8, 512
QB = S // P
TILES = B * QB
GRP = 4
NG = H // GRP
UNITS = B * NG
PARTS = 3
ROWS = PARTS * PARTS * DH
KROWS = 96
HW = 32
EPS = 1e-5
SCALE = DH ** -0.5
ROW = D + 2
CAP = TILES * P + P
STEP = 8
NT = -(-(TILES + E - 1) // STEP) * STEP
GROUP = 4
FC = FF // P
B1 = FF
B2 = B1 + FC
WCOLS = B2 + D
GATE_AT = {(3, 2, 0): (0, 1), (3, 2, 1): (2,), (3, 2, 2): (3,), (3, 2, 3): (4,), (3, 3, 0): (5,), (3, 3, 1): (6,),
           (3, 3, 2): (7,)}
PROJECT_AT = {(1, 1): 0, (1, 2): 1, (1, 3): 2, (2, 1): 3}
TOKENS_AT = {(0, 1): 0, (0, 2): 1, (0, 3): 2, (1, 0): 3}
RESIDUAL_AT = {(1, 2): 0, (1, 3): 1, (2, 0): 2, (2, 2): 3}
FAR = 1 << 20
IN_RANGE = "the table is made of these values"
ROUND = 1.5 * 2.0 ** 23


def build(nc, z, ln_w, ln_b, w_qk, w_v, b_qk, b_v, w_proj, b_proj, gate_w, gate_b, w1, b1t, w2, b2, out):
    ctx = ExitStack()
    with ctx:
        def sb(name, shape, dt=F32):
            return ctx.enter_context(nc.sbuf_tensor(name, shape, dt))

        def sem(name):
            return ctx.enter_context(nc.semaphore(name))

        q_parts = nc.dram_tensor("q_parts", (B, PARTS * DH, H, S), BF16).ap()
        k_parts = nc.dram_tensor("k_parts", (B, 5 * DH, H, S), BF16).ap()
        routed = nc.dram_tensor("routed", (E * CAP, ROW), F32).ap()

        ident = sb("ident", [P, P])
        ident_b = sb("ident_b", [P, P], BF16)
        below = sb("below", [P, P], BF16)
        ones_b = sb("ones_b", [P, P], BF16)
        zero_rows = sb("zero_rows", [PARTS, S], BF16)
        one_rows = sb("one_rows", [PARTS, S], BF16)
        half = sb("half", [P, QB])
        ln_wc, ln_bc = sb("ln_wc", [P, 1]), sb("ln_bc", [P, 1])
        b_qkc = sb("b_qkc", [P, 2])
        wqk_sb = sb("wqk_sb", [P, 2 * D])
        wv_sb = sb("wv_sb", [P, D])
        bv_col = sb("bv_col", [P, 1])
        bv_rep = sb("bv_rep", [P, P])
        wp_sb = sb("wp_sb", [P, D])
        bp_sb = sb("bp_sb", [P, D])
        gw_sb = sb("gw_sb", [P, E])
        gb_sb = sb("gb_sb", [P, E])
        w1_sb = sb("w1_sb", [P, E * WCOLS])
        w2_sb = sb("w2_sb", [P, E * FC * D])

        x_sb = sb("x_sb", [P, TILES, D])
        v_all = sb("v_all", [P, TILES, D])

        mv = sb("mv", [P, TILES, 2])
        ve = sb("ve", [P, TILES])
        rstd = sb("rstd", [P, TILES])
        zstats = sb("zstats", [P, TILES, 6])
        zn = sb("zn", [P, 2, QB, D])
        znT = sb("znT", [P, 2, S])
        rest = sb("rest", [P, 2, 2, S])
        parts = sb("parts", [P, 2, 2, PARTS, S], BF16)

        qs = sb("qs", [KROWS, NG, GRP, S], BF16)
        ks = sb("ks", [KROWS, NG, GRP, S], BF16)
        vs = sb("vs", [P, NG, QB, GRP, HW])
        negm = sb("negm", [P, 2, QB, GRP])
        negm_r = sb("negm_r", [P, QB, GRP])
        negm_p = sb("negm_p", [P, QB, PARTS, GRP], BF16)
        mrow = sb("mrow", [PARTS * GRP, S], BF16)
        probs = sb("probs", [P, 2 * GRP, S])
        oT = sb("oT", [P, NG, S])
        rec = sb("rec", [P, QB, H])
        o_sb = sb("o_sb", [P, QB, D])
        oT_sb = sb("oT_sb", [P, P])

        y_sb = sb("y_sb", [P, QB, ROW])
        y_last = zn[:, :, :, :].rearrange("p k t d -> p (k t d)")[:, 0:QB * ROW].rearrange("p (t r) -> p t r", r=ROW)
        ystats = sb("ystats", [P, QB, 6])
        y_mv = sb("y_mv", [P, QB, 2])
        ymean, yvar, yrstd = (sb(n, [P, QB]) for n in ("ymean", "yvar", "yrstd"))
        mom = sb("mom", [P, 4, QB])
        x1T = sb("x1T", [P, S])
        logits, shifted, ex, is_top, cand = (sb(n, [P, QB, E]) for n in
                                             ("logits", "shifted", "ex", "is_top", "cand"))
        top, total, found = (sb(n, [P, QB]) for n in ("top", "total", "found"))
        onehot = sb("onehot", [P, QB, E], BF16)
        ranks = sb("ranks", [P, 2, QB, E])
        base = sb("base", [P, QB + 1, E])
        place = sb("place", [P, QB, E])
        slot = sb("slot", [P, 2, QB], U32)
        token = sb("token", [P, QB])
        pad_at = sb("pad_at", [1, E], I32)
        numbers = sb("numbers", [P, 2 * E + 1 + 2 * NT], I32)
        numbers_f = sb("numbers_f", [P, 2 * E + 1 + 2 * NT])
        token_i = sb("token_i", [P, QB], I32)
        pad_row = sb("pad_row", [P, ROW])
        count, tiles_of, ends0, ends1, weight_of = (sb(n, [1, E]) for n in
                                                    ("count", "tiles_of", "ends0", "ends1", "weight_of"))
        after, after_w = sb("after", [1, NT, E - 1]), sb("after_w", [1, NT, E - 1])
        table_f, table = sb("table_f", [1, 2, NT]), sb("table", [1, 2, NT], I32)
        limit = sb("limit", [1, 1])

        spare = probs[:, :, :].rearrange("p k n -> p (k n)")
        chosen = spare[:, 0:GROUP * WCOLS].rearrange("p (k c) -> p k c", c=WCOLS)
        rows = spare[:, GROUP * WCOLS:GROUP * WCOLS + STEP * ROW].rearrange("p (k r) -> p k r", r=ROW)
        hidT = rest[:, 0]
        xT = rest[:, 1, 0, 0:2 * P].rearrange("p (k n) -> p k n", n=P)
        yb = rest[:, 1, 1, 0:2 * D].rearrange("p (k d) -> p k d", d=D)
        res = oT[:, 0:2].rearrange("p h (k d) -> p h k d", d=D)
        final = oT[:, 2:4].rearrange("p h (k d) -> p h k d", d=D)
        fstats = sb("fstats", [P, 2, GROUP, 6])
        fmean, fvar, frstd, fshift = (sb(n, [P, GROUP]) for n in ("fmean", "fvar", "frstd", "fshift"))
        res_number = sb("res_number", [P, GROUP], I32)
        out_number = sb("out_number", [P, 2, GROUP], I32)

        ps = ctx.enter_context(nc.psum_tensor("ps", [P, 8, 512], F32))
        MISC = 7

        names = """consts consts2 cleared qk_weights weights moe_weights ident_ok stat_link stat_ok ve_ok rstd_ok ones_in bv_ok
            bias_ok bias_added
            max_ok max_used nm_link nm_ok mT_ok mrow_ok pair_ok exp_ok vs_ok pv_ok pv_copied
            tr_ok rec_ok norm_ok oT_ok oT_copied proj_ok y_ok ystat_ok mom_link yrstd_ok x1_ok last_aggr last_var_ok last_x1_ok
            x1T_ok x1T_copied logits_ok lg_ok top_ok shifted_ok is_top_ok cand_ok found_ok onehot_ok ex_ok
            total_ok weight_ok ranks_ok ranks_copied place_link token_link token_ok pads_ok pads_out
            link numbers_ok route_link table_ok routed_out
            later_zn later_twice later_zb later_zT later_znT later_q later_k later_qk_copied later_hi later_rest
            later_mid later_lo later_v
            chosen_ok xT_ok xTc_ok mm1_ok gelu_ok mm2_ok yb_ok res_ok number_ok fstat_ok
            fmom_link frstd_ok final_ok""".split()
        sm = {n: sem(n) for n in names}
        pr = {n: [sem(f"{n}{k}") for k in range(2)] for n in
              "zn_ok zT_ok znT_ok q_ok k_ok v_ok hi_ok rest_ok mid_ok lo_ok v_all_ok".split()}
        z_in = [sem(f"z_in{b}") for b in range(B)]
        rows_in = [sem(f"rows_in{k}") for k in range(STEP)]
        loaded = [sem(f"unit_loaded{g}") for g in range(NG)]
        mrow_in = [sem(f"mrow_in{g}") for g in range(NG)]
        parts_out = [sem(f"parts_out{k}") for k in range(2)]
        stored = [sem(f"stored{h}") for h in range(2)]
        LOAD = 16 * 7
        STORE = 16 * 3

        block = ctx.enter_context(nc.Block())

        def is_last(ob):
            return isinstance(ob, int) and ob == B - 1

        def wait_x1(eng, ob):
            if is_last(ob):
                eng.wait_ge(sm["last_x1_ok"], 1)
            else:
                eng.wait_ge(sm["x1_ok"], ob + 1)

        def rows_of(ob):
            return y_last if is_last(ob) else y_sb

        def store_pads(eng, engine, experts):
            eng.wait_ge(sm["pads_ok"], 1)
            eng.wait_ge(sm["numbers_ok"], 3)
            for e in experts:
                at = nc.values_load(pad_at[0:1, e:e + 1], engines=(engine,), min_val=0, max_val=E * CAP - P,
                                    skip_runtime_bounds_check_because=IN_RANGE)
                eng.dma_start(routed[bass.ds(at, P), :], pad_row[:, :]).then_inc(sm["pads_out"], 16)

        def heads(rows_):
            return rows_[:, :].rearrange("p (o n) -> p o n", o=1).to_broadcast([PARTS, GRP, S])

        def moments(eng, st, mean, var, sem_, before):
            sq, dif, dd, both = (mom[:, k, :] for k in range(4))
            eng.tensor_tensor(sq, st[:, :, 2], st[:, :, 5], ALU.add).then_inc(sem_, 1)
            eng.tensor_tensor(dif, st[:, :, 1], st[:, :, 4], ALU.subtract).then_inc(sem_, 1)
            eng.tensor_tensor(both, st[:, :, 1], st[:, :, 4], ALU.add).then_inc(sem_, 1)
            eng.wait_ge(sem_, before + 3)
            eng.tensor_scalar(mean, both, 0.5, None, ALU.mult).then_inc(sem_, 1)
            eng.tensor_tensor(dd, dif, dif, ALU.mult).then_inc(sem_, 1)
            eng.wait_ge(sem_, before + 5)
            eng.tensor_scalar(dd, dd, 0.25, EPS, ALU.mult, ALU.add).then_inc(sem_, 1)
            eng.wait_ge(sem_, before + 6)
            eng.tensor_scalar(sq, sq, 1.0 / D, None, ALU.mult).then_inc(sem_, 1)
            eng.wait_ge(sem_, before + 7)
            eng.tensor_tensor(var, dd, sq, ALU.add).then_inc(sem_, 1)

        MOMENTS = 8

        @block.sync
        def _(sp):
            zt = z.rearrange("(t p) d -> p t d", p=P)
            col = lambda a: a.rearrange("(p o) -> p o", o=1)
            row = lambda a: a.rearrange("(o n) -> o n", o=1).to_broadcast([P, a.shape[0]])
            def load_z(b):
                sp.dma_start(x_sb[:, QB * b:QB * (b + 1), :], zt[:, QB * b:QB * (b + 1), :]).then_inc(z_in[b], 16)

            load_z(0)
            with nc.allow_non_contiguous_dma(reason="a few columns of parameters"):
                for dst, src in ((ln_wc[:, :], col(ln_w)), (ln_bc[:, :], col(ln_b)),
                                 (b_qkc[:, :], b_qk.rearrange("(s p) -> p s", p=P)), (wqk_sb[:, :], w_qk)):
                    sp.dma_start(dst, src).then_inc(sm["qk_weights"], 16)
                load_z(1)
                for dst, src in ((wv_sb[:, :], w_v), (bv_col[:, :], col(b_v)), (wp_sb[:, :], w_proj),
                                 (bp_sb[:, :], row(b_proj)), (gw_sb[:, :], gate_w), (gb_sb[:, :], row(gate_b))):
                    sp.dma_start(dst, src).then_inc(sm["weights"], 16)
            for b in range(2, B):
                load_z(b)

            def store_parts(b, par):
                sp.dma_start(q_parts[bass.ds(b, 1)].rearrange("o (t d) h n -> (o d h) t n", t=PARTS),
                             parts[:, par, 0]).then_inc(parts_out[par], 16)
                kd = k_parts[bass.ds(b, 1)].rearrange("o (t d) h n -> (o d h) t n", t=5)
                sp.dma_start(kd[:, 0:PARTS, :], parts[:, par, 1]).then_inc(parts_out[par], 16)
                sp.dma_start(kd[:, PARTS:5, :], parts[:, par, 1, 0:2]).then_inc(parts_out[par], 16)

            def zeros(g):
                sp.dma_start(qs[ROWS:ROWS + PARTS, g, :, :], heads(zero_rows)).then_inc(loaded[g], 16)

            def ones(g):
                sp.dma_start(ks[ROWS:ROWS + PARTS, g, :, :], heads(one_rows)).then_inc(sm["ones_in"], 16)

            def load(b, g):
                for s in range(PARTS):
                    r = slice(s * PARTS * DH, (s + 1) * PARTS * DH)
                    sp.dma_start(qs[r, g], q_parts[bass.ds(b, 1), :, GRP * g:GRP * (g + 1), :]
                                 .rearrange("o r j n -> (o r) j n")).then_inc(loaded[g], 16)
                    sp.dma_start(ks[r, g], k_parts[bass.ds(b, 1), s * DH:(s + PARTS) * DH,
                                                   GRP * g:GRP * (g + 1), :]
                                 .rearrange("o r j n -> (o r) j n")).then_inc(loaded[g], 16)

            def mrow_out(v, g):
                sp.wait_ge(sm["mrow_ok"], v + 1)
                for a in range(PARTS):
                    sp.dma_start(qs[ROWS + a:ROWS + a + 1, g, :, :], mrow[GRP * a:GRP * (a + 1), :])\
                      .then_inc(mrow_in[g], 16)

            sp.wait_ge(sm["consts"], 4)
            ones(0)
            zeros(0)
            sp.wait_ge(pr["lo_ok"][0], 2)
            store_parts(0, 0)
            sp.wait_ge(parts_out[0], STORE)
            load(0, 0)
            sp.wait_ge(sm["cleared"], 2)
            for g in range(1, NG):
                ones(g)
                if g < 3:
                    zeros(g)
                    load(0, g)
            sp.wait_ge(pr["lo_ok"][1], 2)
            store_parts(1, 1)
            mrow_out(0, 0)

            def slots(b, first, last, later, stored):
                for g in range(NG):
                    s = NG * b + g
                    if not (last and g > 0):
                        if not (first and g == 0):
                            sp.wait_ge(sm["pair_ok"], 2 * QB * s)
                        zeros((g + 3) % NG)
                        if g == 1:
                            if first:
                                sp.wait_ge(parts_out[1], STORE)
                            else:
                                sp.wait_ge(parts_out[0], STORE * (b + 1))
                        load(b + (g + 3) // NG, (g + 3) % NG)
                    if not (last and g == NG - 1):
                        mrow_out(s + 1, (g + 1) % NG)
                    if g == 0 and stored:
                        sp.wait_ge(sm["later_lo"], 2 * b)
                        store_parts(b + 1, 0)

            slots(0, True, False, True, False)
            w1e = w1_sb[:, :].rearrange("p (e c) -> p e c", e=E)
            sp.dma_start(w1e[:, :, 0:FF], w1.rearrange("e d f -> d e f"))\
              .then_inc(sm["moe_weights"], 16)
            sp.dma_start(w2_sb[:, :].rearrange("p (e c d) -> p (e c) d", e=E, d=D),
                         w2.rearrange("e (c f) d -> f (e c) d", f=P)).then_inc(sm["moe_weights"], 16)
            sp.dma_start(w1e[:, :, B1:B2], b1t).then_inc(sm["moe_weights"], 16)
            sp.dma_start(w1e[:, :, B2:WCOLS], b2.rearrange("(o e) d -> o e d", o=1).to_broadcast([P, E, D]))\
              .then_inc(sm["moe_weights"], 16)
            with sp.Fori(1, B - 2) as b:
                slots(b, False, False, True, True)
            slots(B - 2, False, False, False, True)
            slots(B - 1, False, True, False, False)

            def first_row(i):
                return nc.values_load(table[0:1, 0, bass.ds(i, 1)], engines=(mybir.EngineType.SP,), min_val=0,
                                      max_val=E * CAP - P, skip_runtime_bounds_check_because=IN_RANGE)

            def load_rows(k, at):
                sp.dma_start(rows[:, k, :], routed[bass.ds(at, P), :]).then_inc(rows_in[k], 16)

            store_pads(sp, mybir.EngineType.SP, range(E // 2))
            sp.wait_ge(sm["table_ok"], 1)
            sp.wait_ge(sm["routed_out"], 16 * TILES)
            sp.wait_ge(sm["pads_out"], 16 * E)
            for k in range(STEP):
                load_rows(k, first_row(k))
            with sp.Fori(0, NT // STEP - 1) as r:
                for k in range(STEP):
                    at = first_row(STEP * (r + 1) + k)
                    sp.wait_ge(sm["fstat_ok"], STEP * r + k + 1)
                    load_rows(k, at)
            for h in range(2):
                sp.wait_ge(stored[h], 16 * NT // 2)

        @block.gpsimd
        def _(pool):
            pool.memset(ident[:, :], 0.0).then_inc(sm["ident_ok"], 1)
            pool.memset(ones_b[:, :], 1.0).then_inc(sm["ident_ok"], 1)
            pool.memset(half[:, :], -0.5)
            pool.wait_ge(sm["ident_ok"], 2)
            pool.affine_select(out=ident[:, :], in_=ident[:, :], compare_op=ALU.not_equal, fill=1.0, base=0,
                               pattern=[[-1, P]], channel_multiplier=1).then_inc(sm["ident_ok"], 1)
            pool.affine_select(out=below[:, :], in_=ones_b[:, :], compare_op=ALU.is_gt, fill=0.0, base=0,
                               pattern=[[1, P]], channel_multiplier=-1).then_inc(sm["ident_ok"], 1)

            def rstd_of(b):
                r = slice(QB * b, QB * (b + 1))
                pool.wait_ge(sm["stat_ok"], b + 1)
                pool.tensor_scalar(ve[:, r], mv[:, r, 1], EPS, None, ALU.add).then_inc(sm["ve_ok"], 1)
                pool.wait_ge(sm["ve_ok"], b + 1)
                pool.tensor_tensor(rstd[:, r], ve[:, r], half[:, :], ALU.pow).then_inc(sm["rstd_ok"], 1)

            rstd_of(0)
            rstd_of(1)
            pool.wait_ge(sm["rstd_ok"], 2)
            for t in (qs, ks):
                pool.memset(t[64:KROWS, 1:NG, :, :].rearrange("p g j n -> p (g j n)").bitcast(U32), 0)\
                    .then_inc(sm["cleared"], 1)
            pool.wait_ge(sm["cleared"], 2)
            pool.memset(vs[:, :, :, :, :], 0.0).then_inc(sm["cleared"], 1)
            pool.wait_ge(sm["cleared"], 3)
            pool.memset(vs[:, :, :, :, DH:DH + 1], 1.0).then_inc(sm["cleared"], 1)
            for side in range(2):
                pool.wait_ge(pr["mid_ok"][1], side + 1)
                pool.tensor_tensor(parts[:, 1, side, 2], rest[:, 1, side], parts[:, 1, side, 1],
                                   ALU.subtract).then_inc(pr["lo_ok"][1], 1)
            pool.memset(token[:, :], 0.0)
            for at, pat, start, ch in ((0, [[CAP, E]], 0, 0), (E, [[-1, E]], E, 0), (2 * E, [[0, 1]], 0, 1),
                                       (2 * E + 1, [[P, NT]], 0, 0), (2 * E + 1 + NT, [[1, NT]], 0, 0)):
                pool.iota(numbers[:, at:at + pat[0][1]], pattern=pat, base=start, channel_multiplier=ch)\
                    .then_inc(sm["consts2"], 1)
            pool.iota(token_i[:, :], pattern=[[P, QB]], base=0, channel_multiplier=1).then_inc(sm["consts2"], 1)
            pool.wait_ge(sm["consts2"], 6)
            pool.tensor_copy(numbers_f[:, :], numbers[:, :]).then_inc(sm["numbers_ok"], 1)
            pool.tensor_copy(token[:, :], token_i[:, :]).then_inc(sm["numbers_ok"], 1)
            pool.memset(pad_row[:, 0:D + 1], 0.0)
            pool.memset(pad_row[:, D + 1:ROW].bitcast(I32), FAR).then_inc(sm["numbers_ok"], 1)
            pool.wait_ge(sm["numbers_ok"], 3)
            pool.tensor_copy(base[:, QB, :], numbers_f[:, 0:E]).then_inc(sm["ranks_copied"], 1)
            pool.tensor_copy(y_sb[:, :, D + 1].bitcast(I32), token[:, :]).then_inc(sm["token_ok"], 1)

            def values(b, g):
                src = v_all[:, QB * b:QB * (b + 1), GRP * DH * g:GRP * DH * (g + 1)]
                pool.tensor_copy(vs[:, g, :, :, 0:DH], src.rearrange("p c (j d) -> p c j d", d=DH))\
                    .then_inc(sm["vs_ok"], 1)

            pool.wait_ge(sm["cleared"], 4)
            pool.wait_ge(pr["v_all_ok"][0], 1)
            for g in range(NG):
                values(0, g)
            pool.wait_ge(pr["v_all_ok"][1], 1)
            for b in range(2, B):
                rstd_of(b)

            def later_zn(a):
                if a > 0:
                    pool.wait_ge(sm["later_zT"], a)
                for t in range(QB):
                    n = QB * (a + 2) + t
                    last = pool.tensor_scalar(zn[:, 0, t, :], x_sb[:, n, :], mv[:, n, 0:1], rstd[:, n:n + 1],
                                              ALU.subtract, ALU.mult)
                last.then_inc(sm["later_zn"], 1)

            def twice(a):
                xb = x_sb[:, QB * (a + 2):QB * (a + 3), :]
                pool.wait_ge(sm["later_zn"], a + 1)
                pool.tensor_tensor(xb, xb, xb, ALU.add).then_inc(sm["later_twice"], 1)
                pool.wait_ge(sm["later_twice"], a + 1)
                pool.tensor_tensor(xb, xb, bp_sb[:, :].rearrange("p (o d) -> p o d", o=1)
                                   .to_broadcast([P, QB, D]), ALU.add).then_inc(sm["later_zb"], 1)

            def later_rests(a):
                for side in range(2):
                    pool.wait_ge(sm["later_hi"], 2 * a + side + 1)
                    pool.tensor_tensor(rest[:, 1, side], rest[:, 0, side], parts[:, 0, side, 0],
                                       ALU.subtract).then_inc(sm["later_rest"], 1)

            def later_lows(a):
                for side in range(2):
                    pool.wait_ge(sm["later_mid"], 2 * a + side + 1)
                    pool.tensor_tensor(parts[:, 0, side, 2], rest[:, 1, side], parts[:, 0, side, 1],
                                       ALU.subtract).then_inc(sm["later_lo"], 1)

            def x1_of(ob):
                y = rows_of(ob)
                pool.wait_ge(sm["yrstd_ok"], ob + 1)
                for t in range(QB):
                    last = pool.tensor_scalar(y[:, t, 0:D], y[:, t, 0:D], ymean[:, t:t + 1],
                                              yrstd[:, t:t + 1], ALU.subtract, ALU.mult)
                last.then_inc(sm["x1_ok"], 1)

            def split_maxima(v):
                m = negm[:, v % 2]
                pool.wait_ge(sm["max_used"], GRP * QB * (v + 1))
                if v > 0:
                    pool.wait_ge(sm["mT_ok"], v)
                hi, mid, lo = (negm_p[:, :, a, :] for a in range(PARTS))
                pool.tensor_copy(hi, m).then_inc(sm["nm_link"], 1)
                pool.wait_ge(sm["nm_link"], 3 * v + 1)
                pool.tensor_tensor(negm_r[:, :, :], m, hi, ALU.subtract).then_inc(sm["nm_link"], 1)
                pool.wait_ge(sm["nm_link"], 3 * v + 2)
                pool.tensor_copy(mid, negm_r[:, :, :]).then_inc(sm["nm_link"], 1)
                pool.wait_ge(sm["nm_link"], 3 * v + 3)
                pool.tensor_tensor(lo, negm_r[:, :, :], mid, ALU.subtract).then_inc(sm["nm_ok"], 1)

            def last_rstd():
                pool.wait_ge(sm["last_var_ok"], 1)
                pool.tensor_tensor(yrstd[:, :], yvar[:, :], half[:, :], ALU.pow).then_inc(sm["yrstd_ok"], 1)

            def norm_of(ob):
                pool.wait_ge(sm["ystat_ok"], QB * (ob + 1))
                moments(pool, ystats, ymean[:, :], yvar[:, :], sm["mom_link"], MOMENTS * ob)
                pool.wait_ge(sm["mom_link"], MOMENTS * (ob + 1))
                pool.tensor_tensor(yrstd[:, :], yvar[:, :], half[:, :], ALU.pow).then_inc(sm["yrstd_ok"], 1)

            def slots_of(ob):
                PL = QB + 7

                def link(op, n):
                    op.then_inc(sm["place_link"], 1)
                    pool.wait_ge(sm["place_link"], PL * ob + n)

                pool.wait_ge(sm["ranks_copied"], ob + 2)
                link(pool.tensor_copy(base[:, 0, :], base[:, QB, :]), 1)
                for t in range(QB):
                    link(pool.tensor_tensor(base[:, t + 1, :], base[:, t, :], ranks[:, 1, t, :], ALU.add), t + 2)
                link(pool.tensor_tensor(place[:, :, :], base[:, 0:QB, :], ranks[:, 0, :, :], ALU.add), QB + 2)
                link(pool.tensor_tensor(place[:, :, :], place[:, :, :], onehot[:, :, :], ALU.mult), QB + 3)
                for n, w in ((4, 4), (5, 2), (6, 1)):
                    link(pool.tensor_tensor(place[:, :, 0:w], place[:, :, 0:w], place[:, :, w:2 * w], ALU.add),
                         QB + n)
                link(pool.tensor_copy(slot[:, ob % 2, :], place[:, :, 0]), PL)

            def scatter(ob):
                pool.wait_ge(sm["weight_ok"], ob + 1)
                wait_x1(pool, ob)
                for t in range(QB):
                    pool.indirect_dma_start(routed[:, :],
                                            bass.IndirectOffsetOnAxis(ap=slot[:, ob % 2, t:t + 1], axis=0),
                                            rows_of(ob)[:, t, :], None).then_inc(sm["routed_out"], 16)

            def next_numbers(nb):
                pool.tensor_scalar(token[:, :], token[:, :], float(S), None, ALU.add)\
                    .then_inc(sm["token_link"], 1)
                if nb < B - 1:
                    pool.wait_ge(sm["routed_out"], 16 * QB * nb)
                pool.wait_ge(sm["token_link"], nb)
                pool.tensor_copy(rows_of(nb)[:, :, D + 1].bitcast(I32), token[:, :]).then_inc(sm["token_ok"], 1)

            def slots(b, first, last, later):
                for g in range(NG):
                    if not (last and g == NG - 1):
                        split_maxima(NG * b + g + 1)
                    if g == 0 and 0 < b < B - 1:
                        later_lows(b - 1)
                    if g == 3 and not first:
                        x1_of(b - 1)
                    if not (first and g == 0) and not (last and g > 0):
                        pool.wait_ge(sm["pv_ok"], QB * (NG * b + g))
                        values(b if g == 0 else b + 1, (g - 1) % NG)
                    if g == 0 and b > 1:
                        slots_of(b - 2)
                        scatter(b - 2)
                        next_numbers(b - 1)
                    if g == 1 and later:
                        later_zn(b)
                        twice(b)
                    if g == 2 and not first:
                        norm_of(b - 1)
                    if g == 3 and later:
                        later_rests(b)

            split_maxima(0)
            for b in range(B):
                slots(b, b == 0, b == B - 1, b < B - 2)
            next_numbers(B - 1)
            slots_of(B - 2)
            last_rstd()
            scatter(B - 2)
            slots_of(B - 1)
            scatter(B - 1)

            def store(n):
                h = n % 2
                pool.wait_ge(sm["fstat_ok"], GROUP * (n + 1))
                moments(pool, fstats[:, h], fmean[:, :], fvar[:, :], sm["fmom_link"], (MOMENTS + 2) * n)
                pool.wait_ge(sm["fmom_link"], (MOMENTS + 2) * n + MOMENTS)
                pool.tensor_tensor(frstd[:, :], fvar[:, :], half[:, :], ALU.pow).then_inc(sm["fmom_link"], 1)
                pool.wait_ge(sm["fmom_link"], (MOMENTS + 2) * n + MOMENTS + 1)
                pool.tensor_tensor(fshift[:, :], fmean[:, :], frstd[:, :], ALU.mult).then_inc(sm["fmom_link"], 1)
                pool.wait_ge(sm["fmom_link"], (MOMENTS + 2) * (n + 1))
                pool.tensor_scalar(fshift[:, :], fshift[:, :], -1.0, None, ALU.mult).then_inc(sm["frstd_ok"], 1)
                for k in range(GROUP):
                    pool.wait_ge(sm["final_ok"], GROUP * n + k + 1)
                    pool.indirect_dma_start(
                        out[:, :], bass.IndirectOffsetOnAxis(ap=out_number[:, h, k:k + 1].bitcast(U32), axis=0),
                        final[:, h, k, :], None, bounds_check=TILES * P - 1, oob_is_err=False)\
                        .then_inc(stored[h], 16)

            for n in range(NT // GROUP):
                store(n)

        @block.vector
        def _(dve):
            V = nc.vector

            def z_stats(b):
                dve.wait_ge(z_in[b], 16)
                for t in range(QB):
                    V.bn_stats(zstats[:, QB * b + t, :], x_sb[:, QB * b + t, :]).then_inc(sm["stat_link"], 1)
                dve.wait_ge(sm["stat_link"], QB * b + QB)
                for t in range(QB):
                    last = V.bn_aggr(mv[:, QB * b + t, :], zstats[:, QB * b + t, :])
                last.then_inc(sm["stat_ok"], 1)

            def zn_of(b):
                for t in range(QB):
                    n = QB * b + t
                    last = V.tensor_scalar(zn[:, b, t, :], x_sb[:, n, :], mv[:, n, 0:1], rstd[:, n:n + 1],
                                           ALU.subtract, ALU.mult)
                return last

            V.memset(zero_rows[:, :], 0.0).then_inc(sm["consts"], 1)
            V.memset(one_rows[:, :], 1.0).then_inc(sm["consts"], 1)
            for t in (qs, ks):
                V.memset(t[64:KROWS, 0, :, :].rearrange("p j n -> p (j n)").bitcast(U32), 0)\
                 .then_inc(sm["consts"], 1)
            z_stats(0)
            z_stats(1)
            for b in range(2):
                dve.wait_ge(sm["rstd_ok"], b + 1)
                zn_of(b).then_inc(pr["zn_ok"][b], 1)
            dve.wait_ge(sm["weights"], 16 * 6)
            V.tensor_copy(bv_rep[:, :], bv_col[:, :].to_broadcast([P, P])).then_inc(sm["bv_ok"], 1)
            for par in range(2):
                for side, name in ((0, "q_ok"), (1, "k_ok")):
                    dve.wait_ge(pr[name][par], 1)
                    dve.wait_ge(pr["hi_ok"][par], side + 1)
                    V.scalar_tensor_tensor(
                        out=rest[:, par, side], in0=ps[:, 2 + 2 * side + par, :], scalar=b_qkc[:, side:side + 1],
                        in1=parts[:, par, side, 0], op0=ALU.add, op1=ALU.subtract).then_inc(pr["rest_ok"][par], 1)
                if par == 0:
                    for side in range(2):
                        dve.wait_ge(pr["mid_ok"][par], side + 1)
                        V.tensor_tensor(parts[:, par, side, 2], rest[:, par, side], parts[:, par, side, 1],
                                        ALU.subtract).then_inc(pr["lo_ok"][par], 1)
            dve.wait_ge(sm["bias_ok"], 1)
            V.tensor_tensor(bp_sb[:, :], ps[:, 0, 0:D], bp_sb[:, :], ALU.add).then_inc(sm["bias_added"], 1)
            dve.wait_ge(sm["bias_added"], 1)
            for b in range(2):
                xb = x_sb[:, QB * b:QB * (b + 1), :]
                V.scalar_tensor_tensor(out=xb, in0=xb, scalar=2.0, in1=bp_sb[:, :]
                                       .rearrange("p (o d) -> p o d", o=1).to_broadcast([P, QB, D]),
                                       op0=ALU.mult, op1=ALU.add)
            for b in range(2, B):
                z_stats(b)

            def maximum(v, par, j, qb):
                n = GRP * QB * v + QB * j + qb
                if j == 0 and qb == 0 and not (isinstance(v, int) and v < 2):
                    dve.wait_ge(sm["nm_ok"], v - 1)
                dve.wait_ge(sm["max_ok"], n + 1)
                V.tensor_reduce(negm[:, par, qb, j:j + 1], ps[:, 4 + qb % 2, :], AX.X, ALU.max, negate=True)\
                 .then_inc(sm["max_used"], 1)

            def by_head(ob, qb):
                return ps[:, qb if is_last(ob) else MISC, :].rearrange("p (h c) -> p h c", c=HW)

            def row_sums(ob, qb):
                dve.wait_ge(sm["tr_ok"], QB * ob + qb + 1)
                V.reciprocal(rec[:, qb, :], by_head(ob, qb)[:, :, DH]).then_inc(sm["rec_ok"], 1)

            def normalise(ob, qb):
                dve.wait_ge(sm["rec_ok"], QB * ob + qb + 1)
                V.tensor_tensor(o_sb[:, qb, :].rearrange("p (h d) -> p h d", d=DH), by_head(ob, qb)[:, :, 0:DH],
                                rec[:, qb, :].rearrange("p (h o) -> p h o", o=1).to_broadcast([P, H, DH]),
                                ALU.mult).then_inc(sm["norm_ok"], 1)

            def residual(ob, qb, y):
                t = QB * ob + qb
                dve.wait_ge(sm["proj_ok"], t + 1)
                V.tensor_tensor(y[:, qb, 0:D], ps[:, 4 + qb if is_last(ob) else MISC, P:2 * P], x_sb[:, bass.ds(t, 1), :]
                                .rearrange("p o d -> p (o d)"), ALU.add).then_inc(sm["y_ok"], 1)

            def y_stats(ob, qb, y):
                dve.wait_ge(sm["y_ok"], QB * ob + qb + 1)
                V.bn_stats(ystats[:, qb, :], y[:, qb, 0:D]).then_inc(sm["ystat_ok"], 1)

            def over_tiles(a):
                return a.rearrange("p (o e) -> p o e", o=1).to_broadcast([P, QB, E])

            def over_experts(a):
                return a[:, :].rearrange("p (t o) -> p t o", o=1).to_broadcast([P, QB, E])

            rev = numbers_f[:, E:2 * E]

            def gate(ob, step):
                n = ob + 1
                if step == 0:
                    dve.wait_ge(sm["logits_ok"], n)
                    V.tensor_tensor(logits[:, :, :], ps[:, MISC, 0:QB * E].rearrange("p (t e) -> p t e", e=E),
                                    over_tiles(gb_sb[:, :]), ALU.add).then_inc(sm["lg_ok"], 1)
                if step == 1:
                    dve.wait_ge(sm["lg_ok"], n)
                    V.tensor_reduce(top[:, :], logits[:, :, :], AX.X, ALU.max).then_inc(sm["top_ok"], 1)
                if step == 2:
                    dve.wait_ge(sm["top_ok"], n)
                    V.tensor_tensor(shifted[:, :, :], logits[:, :, :], over_experts(top), ALU.subtract)\
                     .then_inc(sm["shifted_ok"], 1)
                    V.tensor_tensor(is_top[:, :, :], logits[:, :, :], over_experts(top), ALU.is_equal)\
                     .then_inc(sm["is_top_ok"], 1)
                if step == 3:
                    dve.wait_ge(sm["is_top_ok"], n)
                    V.tensor_tensor(cand[:, :, :], is_top[:, :, :], over_tiles(rev), ALU.mult)\
                     .then_inc(sm["cand_ok"], 1)
                if step == 4:
                    dve.wait_ge(sm["cand_ok"], n)
                    V.tensor_reduce(found[:, :], cand[:, :, :], AX.X, ALU.max).then_inc(sm["found_ok"], 1)
                if step == 5:
                    dve.wait_ge(sm["found_ok"], n)
                    V.tensor_tensor(onehot[:, :, :], cand[:, :, :], over_experts(found), ALU.is_equal)\
                     .then_inc(sm["onehot_ok"], 1)

                if step == 6:
                    dve.wait_ge(sm["ex_ok"], n)
                    V.tensor_reduce(total[:, :], ex[:, :, :], AX.X, ALU.add).then_inc(sm["total_ok"], 1)
                if step == 7:
                    dve.wait_ge(sm["ranks_ok"], n)
                    V.tensor_copy(ranks[:, :, :, :], ps[:, MISC, 0:2 * QB * E]
                                  .rearrange("p (k t e) -> p k t e", k=2, e=E)).then_inc(sm["ranks_copied"], 1)
                    dve.wait_ge(sm["total_ok"], n)
                    V.reciprocal(rows_of(ob)[:, :, D], total[:, :]).then_inc(sm["weight_ok"], 1)

            def slots(b, first, last, later):
                for g in range(NG):
                    s = NG * b + g
                    more = not (last and g >= 2)
                    for kc in range(QB):
                        for qb in range(QB):
                            if more:
                                maximum(s + 2, g % 2, kc, qb)
                            if first:
                                continue
                            if (g, kc) in RESIDUAL_AT:
                                t = RESIDUAL_AT[g, kc]
                                if qb == 0:
                                    if t == 0:
                                        dve.wait_ge(sm["token_ok"], b)
                                        dve.wait_ge(sm["later_zb"], b if not last else b - 1)
                                    residual(b - 1, t, y_sb)
                                if qb == 2:
                                    y_stats(b - 1, t, y_sb)
                            if (g, kc) in TOKENS_AT:
                                t = TOKENS_AT[g, kc]
                                if qb == 0 and t > 0:
                                    normalise(b - 1, t - 1)
                                if qb == 2:
                                    if t == 0:
                                        dve.wait_ge(sm["max_used"], GRP * QB * (s + 2) + QB * kc + qb + 1)
                                    row_sums(b - 1, t)
                                    if t == QB - 1:
                                        normalise(b - 1, t)
                            for step in GATE_AT.get((g, kc, qb), ()):
                                gate(b - 1, step)

            for v in range(2):
                for j in range(GRP):
                    for qb in range(QB):
                        maximum(v, v, j, qb)
            slots(0, True, False, True)
            with dve.Fori(1, B - 2) as b:
                slots(b, False, False, True)
            slots(B - 2, False, False, False)
            slots(B - 1, False, True, False)
            ob = B - 1
            for qb in range(QB):
                row_sums(ob, qb)
            for qb in range(QB):
                normalise(ob, qb)
            for qb in range(QB):
                residual(ob, qb, y_last)
                y_stats(ob, qb, y_last)
            dve.wait_ge(sm["ystat_ok"], TILES)
            for t in range(QB):
                last = V.bn_aggr(y_mv[:, t, :], ystats[:, t, :])
            last.then_inc(sm["last_aggr"], 1)
            dve.wait_ge(sm["last_aggr"], 1)
            V.tensor_scalar(yvar[:, :], y_mv[:, :, 1], EPS, None, ALU.add).then_inc(sm["last_var_ok"], 1)
            dve.wait_ge(sm["yrstd_ok"], B)
            for t in range(QB):
                last = V.tensor_scalar(y_last[:, t, 0:D], y_last[:, t, 0:D], y_mv[:, t, 0:1],
                                       yrstd[:, t:t + 1], ALU.subtract, ALU.mult)
            last.then_inc(sm["last_x1_ok"], 1)
            for step in range(8):
                gate(ob, step)

            links = [0]

            def link(op):
                links[0] += 1
                op.then_inc(sm["route_link"], 1)
                dve.wait_ge(sm["route_link"], links[0])

            first_row = numbers_f[0:1, 2 * E + 1:2 * E + 1 + NT]
            tile_no = numbers_f[0:1, 2 * E + 1 + NT:]
            dve.wait_ge(sm["place_link"], (QB + 7) * (B - 1) + QB + 1)
            V.tensor_copy(pad_at[:, :], base[0:1, QB, :]).then_inc(sm["pads_ok"], 1)
            link(V.tensor_tensor(count[:, :], base[0:1, QB, :], numbers_f[0:1, 0:E], ALU.subtract))
            c0 = count[:, :]
            link(V.tensor_scalar(ends0[:, :], c0, 1.0 / P, (P - 1) / (2.0 * P), ALU.mult, ALU.add))
            link(V.tensor_scalar(ends1[:, :], ends0[:, :], ROUND, None, ALU.add))
            link(V.tensor_scalar(tiles_of[:, :], ends1[:, :], -ROUND, None, ALU.add))
            a, b_ = tiles_of, ends0
            for n in (1, 2, 4):
                V.tensor_copy(b_[:, 0:n], a[:, 0:n])
                link(V.tensor_tensor(b_[:, n:], a[:, n:], a[:, 0:E - n], ALU.add))
                a, b_ = b_, (ends1 if b_ is ends0 else ends0)
            ends = a
            shape = [1, NT, E - 1]
            link(V.tensor_tensor(after[:, :, :], tile_no.rearrange("p (i o) -> p i o", o=1).to_broadcast(shape),
                                 ends[:, 0:E - 1].rearrange("p (o e) -> p o e", o=1).to_broadcast(shape),
                                 ALU.is_ge))
            link(V.tensor_scalar(weight_of[:, :], tiles_of[:, :], -float(P), float(CAP), ALU.mult, ALU.add))
            link(V.tensor_tensor(after_w[:, :, :], after[:, :, :],
                                 weight_of[:, 0:E - 1].rearrange("p (o e) -> p o e", o=1).to_broadcast(shape),
                                 ALU.mult))
            link(V.tensor_reduce(table_f[:, 1, :], after[:, :, :], AX.X, ALU.add))
            link(V.tensor_reduce(table_f[:, 0, :], after_w[:, :, :], AX.X, ALU.add))
            link(V.tensor_tensor(table_f[:, 0, :], table_f[:, 0, :], first_row, ALU.add))
            link(V.tensor_scalar(limit[:, :], c0[:, E - 1:E], float((E - 1) * CAP), None, ALU.add))
            link(V.tensor_scalar(table_f[:, 0, :], table_f[:, 0, :], limit[:, :], None, ALU.min))
            V.tensor_copy(table[:, :, :], table_f[:, :, :]).then_inc(sm["table_ok"], 1)
            dve.wait_ge(sm["table_ok"], 1)
            dve.wait_ge(sm["moe_weights"], 64)

            def choose(i, k):
                e = nc.values_load(table[0:1, 1, bass.ds(i, 1)], engines=(mybir.EngineType.DVE,), min_val=0,
                                   max_val=E - 1, skip_runtime_bounds_check_because=IN_RANGE)
                if not (isinstance(i, int) and i < GROUP):
                    dve.wait_ge(sm["gelu_ok"], i - GROUP + 1)
                    dve.wait_ge(sm["yb_ok"], i - GROUP + 1)
                V.tensor_copy(chosen[:, k % GROUP, :], w1_sb[:, bass.ds(e * WCOLS, WCOLS)])\
                 .then_inc(sm["chosen_ok"], 1)

            def add_bias(i, k, r):
                dve.wait_ge(rows_in[k], 16 * (r + 1))
                dve.wait_ge(sm["mm2_ok"], i + 1)
                V.tensor_tensor(yb[:, k % 2, :], ps[:, 4 + k % 2, 0:D], chosen[:, k % GROUP, B2:WCOLS], ALU.add)\
                 .then_inc(sm["yb_ok"], 1)

            def combine(i, k, r):
                h, c = k // GROUP, k % GROUP
                if c == 0 and not (isinstance(r, int) and r == 0):
                    dve.wait_ge(sm["final_ok"], GROUP * ((STEP // GROUP) * r + h - 1))
                dve.wait_ge(sm["yb_ok"], i + 1)
                V.scalar_tensor_tensor(out=res[:, h, c, :], in0=yb[:, k % 2, :], scalar=rows[:, k, D:D + 1],
                                       in1=rows[:, k, 0:D], op0=ALU.mult, op1=ALU.add).then_inc(sm["res_ok"], 1)
                V.tensor_copy(res_number[:, c:c + 1], rows[:, k, D + 1:ROW].bitcast(I32)).then_inc(sm["number_ok"], 1)
                if c == GROUP - 1:
                    if not (isinstance(r, int) and r == 0):
                        dve.wait_ge(stored[h], 16 * GROUP * r)
                    dve.wait_ge(sm["number_ok"], i + 1)
                    V.tensor_copy(out_number[:, h, :], res_number[:, :])
                dve.wait_ge(sm["res_ok"], i + 1)
                V.bn_stats(fstats[:, h, c, :], res[:, h, c, :]).then_inc(sm["fstat_ok"], 1)

            def steps(r, first, last):
                for k in range(STEP):
                    i = STEP * r + k
                    before = (i - 1, (k - 1) % STEP, r if k > 0 else r - 1)
                    if not (first and k == 0):
                        add_bias(*before)
                    if not (last and k >= STEP - 2):
                        choose(i + 2, (k + 2) % STEP)
                    if not (first and k == 0):
                        combine(*before)

            choose(0, 0)
            choose(1, 1)
            steps(0, True, False)
            with dve.Fori(1, NT // STEP - 1) as r:
                steps(r, False, False)
            steps(NT // STEP - 1, False, True)
            add_bias(NT - 1, STEP - 1, NT // STEP - 1)
            combine(NT - 1, STEP - 1, NT // STEP - 1)

        @block.scalar
        def _(act):
            A = nc.scalar
            act.wait_ge(sm["ident_ok"], 4)
            A.activation(ident_b[:, :], ident[:, :], ACT.Copy).then_inc(sm["ident_ok"], 1)
            act.wait_ge(sm["qk_weights"], 16 * 4)

            def first_znT(par):
                act.wait_ge(pr["zT_ok"][par], 1)
                A.activation(znT[:, par, :], ps[:, par, :], ACT.Identity, bias=ln_bc[:, 0:1],
                             scale=ln_wc[:, 0:1]).then_inc(pr["znT_ok"][par], 1)

            def first_hi(par, side):
                act.wait_ge(pr[("q_ok", "k_ok")[side]][par], 1)
                A.activation(parts[:, par, side, 0], ps[:, 2 + 2 * side + par, :], ACT.Identity,
                             bias=b_qkc[:, side:side + 1]).then_inc(pr["hi_ok"][par], 1)

            def first_mid(par, side):
                act.wait_ge(pr["rest_ok"][par], side + 1)
                A.activation(parts[:, par, side, 1], rest[:, par, side], ACT.Copy).then_inc(pr["mid_ok"][par], 1)

            def first_values(par):
                act.wait_ge(pr["v_ok"][par], 1)
                A.activation(v_all[:, QB * par:QB * (par + 1), :].rearrange("p c d -> p (c d)"),
                             ps[:, 6 + par, :], ACT.Copy).then_inc(pr["v_all_ok"][par], 1)

            first_znT(0)
            first_znT(1)
            first_hi(0, 0)
            first_hi(0, 1)
            first_mid(0, 0)
            first_mid(0, 1)
            first_hi(1, 0)
            first_hi(1, 1)
            first_mid(1, 0)
            first_mid(1, 1)
            first_values(0)
            first_values(1)

            def exps(s, kc, jp):
                n = 2 * QB * s + 2 * kc + jp
                act.wait_ge(sm["pair_ok"], n + 1)
                if not (isinstance(s, int) and s == 0 and kc < 2):
                    act.wait_ge(sm["pv_ok"], QB * s + kc - 1)
                k = GRP * (kc % 2) + 2 * jp
                A.activation(probs[:, k:k + 2, :], ps[:, 2 * jp:2 * jp + 2, :], ACT.Exp, scale=SCALE)\
                 .then_inc(sm["exp_ok"], 1)

            def copy_pv(s, g, b=None):
                act.wait_ge(sm["pv_ok"], QB * (s + 1))
                if g == 0 and b is not None:
                    act.wait_ge(sm["tr_ok"], QB * b)
                A.activation(oT[:, g, :], ps[:, 6, :], ACT.Copy).then_inc(sm["pv_copied"], 1)

            def copy_mrow(v):
                act.wait_ge(sm["mT_ok"], v + 1)
                A.activation(mrow[:, :], ps[0:PARTS * GRP, MISC, :], ACT.Copy).then_inc(sm["mrow_ok"], 1)

            def copy_oT(ob, qb):
                act.wait_ge(sm["oT_ok"], QB * ob + qb + 1)
                bank, oT_ = (4 + qb, x1T[:, P * qb:P * (qb + 1)]) if is_last(ob) else (MISC, oT_sb[:, :])
                A.activation(oT_, ps[:, bank, 0:P], ACT.Copy).then_inc(sm["oT_copied"], 1)

            def copy_x1T(ob):
                act.wait_ge(sm["x1T_ok"], ob + 1)
                A.activation(x1T[:, :], ps[:, MISC, :], ACT.Copy).then_inc(sm["x1T_copied"], 1)

            def gate_exp(ob):
                act.wait_ge(sm["shifted_ok"], ob + 1)
                A.activation(ex[:, :, :], shifted[:, :, :], ACT.Exp).then_inc(sm["ex_ok"], 1)

            def later_znT(a):
                act.wait_ge(sm["later_zT"], a + 1)
                A.activation(znT[:, 0, :], ps[:, MISC, :], ACT.Identity, bias=ln_bc[:, 0:1],
                             scale=ln_wc[:, 0:1]).then_inc(sm["later_znT"], 1)

            def later_copy(a, side, first):
                act.wait_ge(sm[("later_q", "later_k")[side]], a + 1)
                if side == 0 and not first:
                    act.wait_ge(sm["later_rest"], 2 * a)
                A.activation(rest[:, 0, side], ps[:, MISC, :], ACT.Identity, bias=b_qkc[:, side:side + 1])\
                 .then_inc(sm["later_qk_copied"], 1)

            def later_his(a):
                act.wait_ge(parts_out[0], STORE * (a + 1))
                for side in range(2):
                    act.wait_ge(sm["later_qk_copied"], 2 * a + side + 1)
                    A.activation(parts[:, 0, side, 0], rest[:, 0, side], ACT.Copy).then_inc(sm["later_hi"], 1)

            def later_mids(a):
                for side in range(2):
                    act.wait_ge(sm["later_rest"], 2 * a + side + 1)
                    A.activation(parts[:, 0, side, 1], rest[:, 1, side], ACT.Copy).then_inc(sm["later_mid"], 1)

            def later_values(a):
                act.wait_ge(sm["later_v"], a + 1)
                A.activation(v_all[:, bass.ds(QB * (a + 2), QB), :].rearrange("p c d -> p (c d)"),
                             ps[:, MISC, :], ACT.Copy).then_inc(pr["v_all_ok"][0], 1)

            def slots(b, first, last, later):
                for g in range(NG):
                    s = NG * b + g
                    for kc in range(QB):
                        if kc == 1 and not (last and g == NG - 1):
                            act.wait_ge(mrow_in[g], 48 * (b + 1))
                            copy_mrow(s + 1)
                        exps(s, kc, 0)
                        if not first:
                            if (g, kc) in PROJECT_AT:
                                copy_oT(b - 1, PROJECT_AT[g, kc])
                            if (g, kc) == (3, 1):
                                copy_x1T(b - 1)
                        exps(s, kc, 1)
                        if later:
                            if (g, kc) == (2, 2):
                                later_znT(b)
                            if (g, kc) == (2, 3):
                                later_copy(b, 0, first)
                            if (g, kc) == (3, 0):
                                later_copy(b, 1, first)
                            if (g, kc) == (3, 1):
                                later_his(b)
                            if (g, kc) == (3, 2):
                                later_values(b)
                            if (g, kc) == (3, 3):
                                later_mids(b)
                        if kc == 0 and not (first and g == 0):
                            copy_pv(s - 1, (g - 1) % NG, None if first else b)
                        if not first and (g, kc) == (3, 2):
                            gate_exp(b - 1)

            copy_mrow(0)
            slots(0, True, False, True)
            with act.Fori(1, B - 2) as b:
                slots(b, False, False, True)
            slots(B - 2, False, False, False)
            slots(B - 1, False, True, False)
            copy_pv(UNITS - 1, NG - 1)
            for qb in range(QB):
                copy_oT(B - 1, qb)
            copy_x1T(B - 1)
            gate_exp(B - 1)
            store_pads(act, mybir.EngineType.Activation, range(E // 2, E))

            def copy_xT(i, k):
                act.wait_ge(sm["xT_ok"], i + 1)
                if not (isinstance(i, int) and i < 2):
                    act.wait_ge(sm["mm1_ok"], i - 1)
                A.activation(xT[:, k % 2, :], ps[:, 0, 0:P], ACT.Copy).then_inc(sm["xTc_ok"], 1)

            def gelu(i, k):
                act.wait_ge(sm["mm1_ok"], i + 1)
                if not (isinstance(i, int) and i < 2):
                    act.wait_ge(sm["mm2_ok"], i - 1)
                for c in range(FC):
                    last = A.activation(hidT[:, k % 2, P * c:P * (c + 1)], ps[:, 1 + k % 2, P * c:P * (c + 1)],
                                        ACT.Gelu, bias=chosen[:, k % GROUP, B1 + c:B1 + c + 1])
                last.then_inc(sm["gelu_ok"], 1)

            def finish(n, h):
                act.wait_ge(sm["frstd_ok"], n + 1)
                for k in range(GROUP):
                    A.activation(final[:, h, k, :], res[:, h, k, :], ACT.Identity, scale=frstd[:, k:k + 1],
                                 bias=fshift[:, k:k + 1]).then_inc(sm["final_ok"], 1)

            def steps(r, first, last):
                for k in range(STEP):
                    i = STEP * r + k
                    if not (last and k >= STEP - 2):
                        copy_xT(i + 2, (k + 2) % STEP)
                    if not (last and k == STEP - 1):
                        gelu(i + 1, (k + 1) % STEP)
                    if k % GROUP == GROUP - 1 and not (first and k < GROUP):
                        n = (STEP // GROUP) * r + k // GROUP - 1
                        finish(n, (k // GROUP - 1) % 2)

            copy_xT(0, 0)
            copy_xT(1, 1)
            gelu(0, 0)
            steps(0, True, False)
            with act.Fori(1, NT // STEP - 1) as r:
                steps(r, False, False)
            steps(NT // STEP - 1, False, True)
            finish(NT // GROUP - 1, 1)

        @block.tensor
        def _(pe):
            T = nc.tensor
            pe.wait_ge(sm["ident_ok"], 5)
            for par in range(2):
                pe.wait_ge(pr["zn_ok"][par], 1)
                for t in range(QB):
                    last = T.transpose(ps[:, par, P * t:P * (t + 1)], zn[:, par, t, :], ident[:, :])
                last.then_inc(pr["zT_ok"][par], 1)
            pe.wait_ge(sm["qk_weights"], 16 * 4)
            for par in range(2):
                pe.wait_ge(pr["znT_ok"][par], 1)
                for side, name in ((0, "q_ok"), (1, "k_ok")):
                    T.matmul(ps[:, 2 + 2 * side + par, :], wqk_sb[:, D * side:D * (side + 1)],
                             znT[:, par, :], start=True, stop=True).then_inc(pr[name][par], 1)
            pe.wait_ge(sm["weights"], 16 * 6)
            for par in range(2):
                for t in range(QB):
                    last = T.matmul(ps[:, 6 + par, P * t:P * (t + 1)], znT[:, par, P * t:P * (t + 1)],
                                    wv_sb[:, :], start=True, stop=True)
                last.then_inc(pr["v_ok"][par], 1)
            pe.wait_ge(sm["bv_ok"], 1)
            T.matmul(ps[:, 0, 0:D], bv_rep[:, :], wp_sb[:, :], start=True, stop=True).then_inc(sm["bias_ok"], 1)
            for par in range(2):
                pe.wait_ge(pr["rest_ok"][par], 2)
                pe.wait_ge(pr["hi_ok"][par], 2)
                pe.wait_ge(pr["v_all_ok"][par], 1)
            pe.wait_ge(sm["consts"], 4)

            def maximum_scores(v, g, j, qb):
                n = GRP * QB * v + QB * j + qb
                if not (isinstance(n, int) and n < 2):
                    pe.wait_ge(sm["max_used"], n - 1)
                T.matmul(ps[:, 4 + qb % 2, :], qs[:, g, j, P * qb:P * (qb + 1)], ks[:, g, j, :],
                         start=True, stop=True).then_inc(sm["max_ok"], 1)

            def scores(s, g, kc, j):
                n = 2 * QB * s + 2 * kc + j // 2
                if j % 2 == 0 and not (isinstance(n, int) and n < 2):
                    pe.wait_ge(sm["exp_ok"], n - 1)
                last = T.matmul(ps[:, j, :], ks[:, g, j, P * kc:P * (kc + 1)], qs[:, g, j, :],
                                start=True, stop=True)
                if j % 2:
                    last.then_inc(sm["pair_ok"], 1)

            def pv(s, g, kc):
                if kc == 0:
                    pe.wait_ge(sm["vs_ok"], s + 1)
                    if not (isinstance(s, int) and s == 0):
                        pe.wait_ge(sm["pv_copied"], s)
                pe.wait_ge(sm["exp_ok"], 2 * QB * s + 2 * kc + 2)
                for j in range(GRP):
                    last = T.matmul(ps[HW * j:HW * (j + 1), 6, :], vs[:, g, kc, j, :],
                                    probs[:, GRP * (kc % 2) + j, :], start=(kc == 0), stop=(kc == QB - 1))
                last.then_inc(sm["pv_ok"], 1)

            def maxima_to_rows(v):
                pe.wait_ge(sm["nm_ok"], v + 1)
                for qb in range(QB):
                    last = T.matmul(ps[0:PARTS * GRP, MISC, P * qb:P * (qb + 1)],
                                    negm_p[:, qb].rearrange("p a j -> p (a j)"), ident_b[:, :],
                                    start=True, stop=True)
                last.then_inc(sm["mT_ok"], 1)

            def to_tokens(ob, qb):
                pe.wait_ge(sm["pv_copied"], NG * (ob + 1))
                if qb > 0 and not is_last(ob):
                    pe.wait_ge(sm["norm_ok"], QB * ob + qb)
                bank = qb if is_last(ob) else MISC
                for g in range(NG):
                    last = T.transpose(ps[:, bank, P * g:P * (g + 1)], oT[:, g, P * qb:P * (qb + 1)],
                                       ident[:, :])
                last.then_inc(sm["tr_ok"], 1)

            def to_channels(ob, qb):
                if is_last(ob):
                    pe.wait_ge(sm["norm_ok"], QB * ob + qb + 1)
                else:
                    pe.wait_ge(sm["norm_ok"], QB * (ob + 1))
                    if qb > 0:
                        pe.wait_ge(sm["y_ok"], QB * ob + qb)
                bank = 4 + qb if is_last(ob) else MISC
                T.transpose(ps[:, bank, 0:P], o_sb[:, qb, :], ident[:, :]).then_inc(sm["oT_ok"], 1)

            def project(ob, qb):
                pe.wait_ge(sm["oT_copied"], QB * ob + qb + 1)
                bank, oT_ = (4 + qb, x1T[:, P * qb:P * (qb + 1)]) if is_last(ob) else (MISC, oT_sb[:, :])
                T.matmul(ps[:, bank, P:2 * P], oT_, wp_sb[:, :], start=True, stop=True)\
                 .then_inc(sm["proj_ok"], 1)

            def x1_transposes(ob):
                y = rows_of(ob)
                wait_x1(pe, ob)
                for t in range(QB):
                    last = T.transpose(ps[:, MISC, P * t:P * (t + 1)], y[:, t, 0:D], ident[:, :])
                last.then_inc(sm["x1T_ok"], 1)

            def gate_logits(ob):
                pe.wait_ge(sm["x1T_copied"], ob + 1)
                for t in range(QB):
                    last = T.matmul(ps[:, MISC, E * t:E * (t + 1)], x1T[:, P * t:P * (t + 1)], gw_sb[:, :],
                                    start=True, stop=True)
                last.then_inc(sm["logits_ok"], 1)

            def expert_ranks(ob):
                pe.wait_ge(sm["onehot_ok"], ob + 1)
                oh = onehot[:, :, :].rearrange("p t e -> p (t e)")
                T.matmul(ps[:, MISC, 0:QB * E], below[:, :], oh, start=True, stop=True)
                T.matmul(ps[:, MISC, QB * E:2 * QB * E], ones_b[:, :], oh, start=True, stop=True)\
                 .then_inc(sm["ranks_ok"], 1)

            def later_transposes(a):
                pe.wait_ge(sm["later_zn"], a + 1)
                for t in range(QB):
                    last = T.transpose(ps[:, MISC, P * t:P * (t + 1)], zn[:, 0, t, :], ident[:, :])
                last.then_inc(sm["later_zT"], 1)

            def later_qk(a, side):
                if side == 0:
                    pe.wait_ge(sm["later_znT"], a + 1)
                else:
                    pe.wait_ge(sm["later_qk_copied"], 2 * a + 1)
                T.matmul(ps[:, MISC, :], wqk_sb[:, D * side:D * (side + 1)], znT[:, 0, :], start=True, stop=True)\
                 .then_inc(sm[("later_q", "later_k")[side]], 1)

            def later_v(a):
                for t in range(QB):
                    last = T.matmul(ps[:, MISC, P * t:P * (t + 1)], znT[:, 0, P * t:P * (t + 1)], wv_sb[:, :],
                                    start=True, stop=True)
                last.then_inc(sm["later_v"], 1)

            def before_pv(b, g, kc, first, last, later):
                s = NG * b + g
                if not first:
                    if (g, kc) in TOKENS_AT:
                        if kc == 1:
                            pe.wait_ge(sm["mrow_ok"], s + 2)
                        to_tokens(b - 1, TOKENS_AT[g, kc])
                    if (g, kc) in PROJECT_AT:
                        if (g, kc) in ((1, 1), (2, 1)):
                            pe.wait_ge(sm["mrow_ok"], s + 2)
                        to_channels(b - 1, PROJECT_AT[g, kc])
                    if (g, kc) == (3, 1):
                        if last:
                            pe.wait_ge(sm["y_ok"], QB * b)
                        else:
                            pe.wait_ge(sm["mrow_ok"], s + 2)
                        x1_transposes(b - 1)
                    if (g, kc) == (3, 3):
                        if later:
                            pe.wait_ge(pr["v_all_ok"][0], b + 2)
                        expert_ranks(b - 1)
                if later:
                    if (g, kc) == (2, 2):
                        if first:
                            pe.wait_ge(sm["mrow_ok"], s + 2)
                        else:
                            pe.wait_ge(sm["y_ok"], QB * b)
                        later_transposes(b)
                    if (g, kc) == (2, 3):
                        later_qk(b, 0)
                    if (g, kc) == (3, 0):
                        later_qk(b, 1)
                    if (g, kc) == (3, 2):
                        if first:
                            pe.wait_ge(sm["mrow_ok"], s + 2)
                        else:
                            pe.wait_ge(sm["lg_ok"], b)
                        later_v(b)

            def after_pv(b, g, kc, first, last, later):
                s = NG * b + g
                if kc == 0 and not (last and g == NG - 1):
                    if not (first and g == 0):
                        pe.wait_ge(sm["mrow_ok"], s + 1)
                    if not first and g == 0:
                        pe.wait_ge(sm["ranks_copied"], b)
                    if not first and g == 1:
                        pe.wait_ge(sm["norm_ok"], QB * b)
                    if not first and g == 2:
                        pe.wait_ge(sm["y_ok"], QB * (b - 1) + 3)
                    if not first and g == 3 and not later:
                        pe.wait_ge(sm["y_ok"], QB * b)
                    if later and g == 3:
                        pe.wait_ge(sm["later_qk_copied"], 2 * b + 2)
                    maxima_to_rows(s + 1)
                if not first:
                    if (g, kc) in PROJECT_AT:
                        project(b - 1, PROJECT_AT[g, kc])
                    if (g, kc) == (3, 1):
                        gate_logits(b - 1)
                elif (g, kc) == (3, 3):
                    pe.wait_ge(pr["v_all_ok"][0], 2)

            def slots(b, first, last, later):
                for g in range(NG):
                    s = NG * b + g
                    pe.wait_ge(mrow_in[g], 48 * (b + 1))
                    more = not (last and g >= 2)
                    if more:
                        pe.wait_ge(loaded[(g + 2) % NG], LOAD * (b + (g + 2) // NG + 1))

                    def ahead(kc, qb):
                        if more:
                            maximum_scores(s + 2, (g + 2) % NG, kc, qb)

                    for kc in range(QB):
                        ahead(kc, 0)
                        scores(s, g, kc, 0)
                        scores(s, g, kc, 1)
                        ahead(kc, 1)
                        scores(s, g, kc, 2)
                        scores(s, g, kc, 3)
                        ahead(kc, 2)
                        before_pv(b, g, kc, first, last, later)
                        if kc > 0:
                            pv(s, g, kc - 1)
                        elif not (first and g == 0):
                            pv(s - 1, (g - 1) % NG, QB - 1)
                        ahead(kc, 3)
                        after_pv(b, g, kc, first, last, later)

            for v in range(2):
                pe.wait_ge(loaded[v], LOAD)
                if v == 1:
                    pe.wait_ge(sm["cleared"], 2)
                for j in range(GRP):
                    for qb in range(QB):
                        maximum_scores(v, v, j, qb)
                    if (v, j) == (1, 0):
                        pe.wait_ge(sm["bias_added"], 1)
                        maxima_to_rows(0)
            pe.wait_ge(sm["ones_in"], 16 * NG)
            slots(0, True, False, True)
            with pe.Fori(1, B - 2) as b:
                slots(b, False, False, True)
            slots(B - 2, False, False, False)
            slots(B - 1, False, True, False)
            ob = B - 1
            pv(UNITS - 1, NG - 1, QB - 1)
            pe.wait_ge(sm["ranks_copied"], ob + 1)
            pe.wait_ge(sm["exp_ok"], 2 * QB * UNITS)
            pe.wait_ge(sm["max_used"], GRP * QB * UNITS)
            for qb in range(QB):
                to_tokens(ob, qb)
            for qb in range(QB):
                to_channels(ob, qb)
            for qb in range(QB):
                project(ob, qb)
            pe.wait_ge(sm["y_ok"], TILES)
            x1_transposes(ob)
            gate_logits(ob)
            expert_ranks(ob)

            pe.wait_ge(sm["table_ok"], 1)
            pe.wait_ge(sm["moe_weights"], 64)

            def expert_of(i):
                return nc.values_load(table[0:1, 1, bass.ds(i, 1)], engines=(mybir.EngineType.PE,), min_val=0,
                                      max_val=E - 1, skip_runtime_bounds_check_because=IN_RANGE)

            def transpose_rows(i, k, r):
                pe.wait_ge(rows_in[k], 16 * (r + 1))
                if not (isinstance(i, int) and i == 0):
                    pe.wait_ge(sm["xTc_ok"], i)
                T.transpose(ps[:, 0, 0:P], rows[:, k, 0:D], ident[:, :]).then_inc(sm["xT_ok"], 1)

            def up(i, k):
                pe.wait_ge(sm["xTc_ok"], i + 1)
                pe.wait_ge(sm["chosen_ok"], i + 1)
                if not (isinstance(i, int) and i < 2):
                    pe.wait_ge(sm["gelu_ok"], i - 1)
                for c in range(FC):
                    last = T.matmul(ps[:, 1 + k % 2, P * c:P * (c + 1)], chosen[:, k % GROUP, P * c:P * (c + 1)],
                                    xT[:, k % 2, :], start=True, stop=True)
                last.then_inc(sm["mm1_ok"], 1)

            def down(i, k, e):
                pe.wait_ge(sm["gelu_ok"], i + 1)
                if not (isinstance(i, int) and i < 2):
                    pe.wait_ge(sm["yb_ok"], i - 1)
                for c in range(FC):
                    last = T.matmul(ps[:, 4 + k % 2, 0:D], hidT[:, k % 2, P * c:P * (c + 1)],
                                    w2_sb[:, bass.ds(e * (FC * D) + c * D, D)],
                                    start=(c == 0), stop=(c == FC - 1))
                last.then_inc(sm["mm2_ok"], 1)

            def steps(r, last):
                for k in range(STEP):
                    i = STEP * r + k
                    e = expert_of(i)
                    if not (last and k >= STEP - 2):
                        transpose_rows(i + 2, (k + 2) % STEP, r + (k + 2) // STEP)
                    if not (last and k == STEP - 1):
                        up(i + 1, (k + 1) % STEP)
                    down(i, k, e)

            transpose_rows(0, 0, 0)
            transpose_rows(1, 1, 0)
            up(0, 0)
            steps(0, False)
            with pe.Fori(1, NT // STEP - 1) as r:
                steps(r, False)
            steps(NT // STEP - 1, True)


_INS = ["z", "ln_w", "ln_b", "w_qk", "w_v", "b_qk", "b_v", "w_proj", "b_proj", "gate_w", "gate_b",
        "w1", "b1t", "w2", "b2"]


def kernel(**inputs):
    import numpy as np
    import concourse.bacc as bacc
    from concourse.bass_utils import run_bass_kernel_spmd

    def given(name):
        return np.asarray(inputs[name])

    z = given("L0_attn_z")
    w_qkv, b_qkv = given("L0_attn_W_qkv"), given("L0_attn_b_qkv")
    by_channel = np.arange(D).reshape(H, DH).T.ravel()
    qk = np.concatenate([by_channel, D + by_channel])
    arrays = {
        "z": z.reshape(B * S, D), "ln_w": given("L0_attn_ln_w"), "ln_b": given("L0_attn_ln_b"),
        "w_qk": w_qkv[:, qk], "w_v": w_qkv[:, 2 * D:], "b_qk": b_qkv[qk], "b_v": b_qkv[2 * D:],
        "w_proj": given("L0_attn_W_proj"), "b_proj": given("L0_attn_b_proj"),
        "gate_w": given("L0_ffn_gate_w"), "gate_b": given("L0_ffn_gate_b"),
        "w1": given("L0_ffn_w1"), "b1t": given("L0_ffn_b1").reshape(E, FC, P).transpose(2, 0, 1),
        "w2": given("L0_ffn_w2"), "b2": given("L0_ffn_b2"),
    }
    arrays = {n: np.ascontiguousarray(arrays[n]) for n in _INS}
    nc = bacc.Bacc("TRN2", target_bir_lowering=False, num_devices=1)
    args = [nc.dram_tensor(n, arrays[n].shape, mybir.dt.from_np(arrays[n].dtype), kind="ExternalInput").ap()
            for n in _INS]
    out = nc.dram_tensor("out", (B * S, D), F32, kind="ExternalOutput").ap()
    build(nc, *args, out)
    r = run_bass_kernel_spmd(nc, [arrays], core_ids=[0])
    return r.results[0]["out"].reshape(B, S, D)
```

```python
import concourse.bass as bass
from concourse import mybir
from contextlib import ExitStack

F32 = mybir.dt.float32
BF16 = mybir.dt.bfloat16
I32 = mybir.dt.int32
U32 = mybir.dt.uint32
ALU = mybir.AluOpType
ACT = mybir.ActivationFunctionType
AX = mybir.AxisListType

P = 128
B, S, D = 8, 512, 128
H, DH = 16, 8
E, FF = 8, 512
QB = S // P
TILES = B * QB
GRP = 4
NG = H // GRP
UNITS = B * NG
PARTS = 3
ROWS = PARTS * PARTS * DH
KROWS = 96
HW = 32
EPS = 1e-5
SCALE = DH ** -0.5
ROW = D + 2
CAP = TILES * P + P
STEP = 8
NT = TILES + E - 1
PASSES = -(-NT // STEP)
GROUP = 4
GROUPS = NT // GROUP
FINISH_AT = {2: (-4, -3), 3: (-2, -1), 6: (0, 1), 7: (2, 3)}
FC = FF // P
B1 = FF
B2 = B1 + FC
WCOLS = B2 + D
BEFORE_PV = {(0, 1), (0, 2), (0, 3), (2, 2), (2, 3), (3, 0), (3, 1), (3, 2)}
GATE_AT = {(3, 2, 0): (0, 1), (3, 2, 1): (2,), (3, 2, 2): (3,), (3, 2, 3): (4,), (3, 3, 0): (5,), (3, 3, 1): (6,),
           (3, 3, 2): (7,)}
PROJECT_AT = {(1, 1): 0, (1, 2): 1, (1, 3): 2, (2, 1): 3}
TOKENS_AT = {(0, 1): 0, (0, 2): 1, (0, 3): 2, (1, 0): 3}
RESIDUAL_AT = {(1, 2): 0, (1, 3): 1, (2, 0): 2, (2, 2): 3}
FAR = 1 << 20
IN_RANGE = "the table is made of these values"
ROUND = 1.5 * 2.0 ** 23


def build(nc, z, ln_w, ln_b, w_qk, w_v, b_qk, b_v, w_proj, b_proj, gate_w, gate_b, w1, b1t, w2, b2, out):
    ctx = ExitStack()
    with ctx:
        def sb(name, shape, dt=F32):
            return ctx.enter_context(nc.sbuf_tensor(name, shape, dt))

        def sem(name):
            return ctx.enter_context(nc.semaphore(name))

        q_parts = nc.dram_tensor("q_parts", (B, NG, PARTS, GRP * DH, S), BF16).ap()
        k_parts = nc.dram_tensor("k_parts", (B, NG, PARTS, GRP * DH, S), BF16).ap()
        routed = nc.dram_tensor("routed", (E * CAP, ROW), F32).ap()

        ident = sb("ident", [P, P])
        ident_b = sb("ident_b", [P, P], BF16)
        below = sb("below", [P, P], BF16)
        ones_b = sb("ones_b", [P, P], BF16)
        zero_rows = sb("zero_rows", [PARTS, S], BF16)
        one_rows = sb("one_rows", [PARTS, S], BF16)
        half = sb("half", [P, QB])
        ln_wc, ln_bc = sb("ln_wc", [P, 1]), sb("ln_bc", [P, 1])
        b_qkc = sb("b_qkc", [P, 2])
        wqk_sb = sb("wqk_sb", [P, 2 * D])
        wv_sb = sb("wv_sb", [P, D])
        bv_col = sb("bv_col", [P, 1])
        bv_rep = sb("bv_rep", [P, P])
        wp_sb = sb("wp_sb", [P, D])
        bp_sb = sb("bp_sb", [P, D])
        gw_sb = sb("gw_sb", [P, E])
        gb_sb = sb("gb_sb", [P, E])
        w1_sb = sb("w1_sb", [P, E * WCOLS])
        w2_sb = sb("w2_sb", [P, E * FC * D])

        x_sb = sb("x_sb", [P, TILES, D])
        v_all = sb("v_all", [P, TILES, D])

        mv = sb("mv", [P, TILES, 2])
        ve = sb("ve", [P, TILES])
        rstd = sb("rstd", [P, TILES])
        zstats = sb("zstats", [P, TILES, 6])
        zn = sb("zn", [P, 2, QB, D])
        znT = sb("znT", [P, 2, S])
        rest = sb("rest", [P, 2, 2, S])
        parts = sb("parts", [P, 2, 2, PARTS, S], BF16)

        qs = sb("qs", [KROWS, NG, GRP, S], BF16)
        ks = sb("ks", [KROWS, NG, GRP, S], BF16)
        vs = sb("vs", [P, NG, QB, GRP, HW])
        negm = sb("negm", [P, 2, QB, GRP])
        negm_r = sb("negm_r", [P, QB, GRP])
        negm_p = sb("negm_p", [P, QB, PARTS, GRP], BF16)
        mrow = sb("mrow", [PARTS * GRP, S], BF16)
        probs = sb("probs", [P, 2 * GRP, S])
        oT = sb("oT", [P, NG, S])
        rec = sb("rec", [P, QB, H])
        o_sb = sb("o_sb", [P, QB, D])
        oT_sb = sb("oT_sb", [P, P])

        y_sb = sb("y_sb", [P, QB, ROW])
        y_last = zn[:, :, :, :].rearrange("p k t d -> p (k t d)")[:, 0:QB * ROW].rearrange("p (t r) -> p t r", r=ROW)
        ystats = sb("ystats", [P, QB, 6])
        y_mv = sb("y_mv", [P, QB, 2])
        ymean, yvar, yrstd = (sb(n, [P, QB]) for n in ("ymean", "yvar", "yrstd"))
        mom = sb("mom", [P, 4, QB])
        x1T = sb("x1T", [P, S])
        logits, shifted, ex, is_top, cand = (sb(n, [P, QB, E]) for n in
                                             ("logits", "shifted", "ex", "is_top", "cand"))
        top, total, found = (sb(n, [P, QB]) for n in ("top", "total", "found"))
        onehot = sb("onehot", [P, QB, E], BF16)
        ranks = sb("ranks", [P, QB + 1, E])
        base = sb("base", [P, E])
        place = sb("place", [P, QB, E])
        slot = sb("slot", [P, 2, QB], U32)
        token = sb("token", [P, QB])
        pad_at = sb("pad_at", [1, E], I32)
        numbers = sb("numbers", [P, 2 * E + 1 + 2 * NT], I32)
        numbers_f = sb("numbers_f", [P, 2 * E + 1 + 2 * NT])
        token_i = sb("token_i", [P, QB], I32)
        pad_row = sb("pad_row", [P, ROW])
        count, tiles_of, ends0, ends1, weight_of = (sb(n, [1, E]) for n in
                                                    ("count", "tiles_of", "ends0", "ends1", "weight_of"))
        after, after_w = sb("after", [1, NT, E - 1]), sb("after_w", [1, NT, E - 1])
        table_f, table = sb("table_f", [1, 2, NT]), sb("table", [1, 2, NT], I32)
        limit = sb("limit", [1, 1])

        spare = probs[:, :, :].rearrange("p k n -> p (k n)")
        chosen = spare[:, 0:GROUP * WCOLS].rearrange("p (k c) -> p k c", c=WCOLS)
        rows = spare[:, GROUP * WCOLS:GROUP * WCOLS + STEP * ROW].rearrange("p (k r) -> p k r", r=ROW)
        hidT = rest[:, 0]
        xT = rest[:, 1, 0, 0:2 * P].rearrange("p (k n) -> p k n", n=P)
        yb = rest[:, 1, 1, 0:2 * D].rearrange("p (k d) -> p k d", d=D)
        res = oT[:, 0:2].rearrange("p h (k d) -> p h k d", d=D)
        final = oT[:, 2:4].rearrange("p h (k d) -> p h k d", d=D)
        fstats = sb("fstats", [P, 2, GROUP, 6])
        f_mv = sb("f_mv", [P, 2, GROUP, 2])
        fvar, frstd, fshift = (sb(n, [P, 2, GROUP]) for n in ("fvar", "frstd", "fshift"))
        res_number = sb("res_number", [P, GROUP], I32)
        LAST = NT - GROUP * GROUPS
        final_last = o_sb
        fvar_last, frstd_last = sb("fvar_last", [P, LAST]), sb("frstd_last", [P, LAST])
        number_last = sb("number_last", [P, LAST], I32)
        out_number = sb("out_number", [P, 2, GROUP], I32)

        ps = ctx.enter_context(nc.psum_tensor("ps", [P, 8, 512], F32))
        MISC = 7

        names = """consts consts2 cleared qk_weights weights moe_weights ident_ok stat_link stat_ok ve_ok rstd_ok ones_in first_out
            bv_ok
            bias_ok bias_added max_ok max_used nm_link nm_ok mT_ok mrow_ok pair_ok exp_ok vs_ok pv_ok pv_copied
            tr_ok rec_ok norm_ok oT_ok oT_copied proj_ok y_ok ystat_ok mom_link yrstd_ok
            x1_ok last_aggr last_var_ok last_x1_ok
            x1T_ok x1T_copied logits_ok lg_ok top_ok shifted_ok is_top_ok cand_ok found_ok onehot_ok ex_ok
            total_ok weight_ok ranks_ok ranks_copied place_link token_link token_ok pads_ok pads_out
            numbers_ok route_link table_ok routed_out
            later_zn later_twice later_zb later_zT later_znT later_q later_k later_qk_copied later_hi later_rest
            later_mid later_lo later_v
            chosen_ok xT_ok xTc_ok mm1_ok gelu_ok mm2_ok yb_ok res_ok number_ok fstat_ok
            fmom_link frstd_ok final_ok faggr_ok last_fvar_ok last_frstd_ok last_final_ok last_stored""".split()
        sm = {n: sem(n) for n in names}
        pr = {n: [sem(f"{n}{k}") for k in range(2)] for n in
              "zn_ok zT_ok znT_ok q_ok k_ok v_ok hi_ok rest_ok mid_ok lo_ok v_all_ok".split()}
        z_in = [sem(f"z_in{b}") for b in range(B)]
        rows_in = [sem(f"rows_in{k}") for k in range(STEP)]
        loaded = [sem(f"unit_loaded{g}") for g in range(NG)]
        mrow_in = [sem(f"mrow_in{g}") for g in range(NG)]
        parts_out = [sem(f"parts_out{k}") for k in range(2)]
        stored = [sem(f"stored{h}") for h in range(2)]
        LOAD = 16 * 5
        FIRST = 16 * 2
        STORE = FIRST * NG
        MROWS = 16 * PARTS
        QK_WEIGHTS, WEIGHTS, MOE_WEIGHTS = 16 * 4, 16 * 6, 16 * 4

        block = ctx.enter_context(nc.Block())

        def is_last(ob):
            return isinstance(ob, int) and ob == B - 1

        def wait_x1(eng, ob):
            if is_last(ob):
                eng.wait_ge(sm["last_x1_ok"], 1)
            else:
                eng.wait_ge(sm["x1_ok"], ob + 1)

        def rows_of(ob):
            return y_last if is_last(ob) else y_sb

        def store_pads(eng, engine, experts):
            eng.wait_ge(sm["pads_ok"], 1)
            eng.wait_ge(sm["numbers_ok"], 3)
            for e in experts:
                at = nc.values_load(pad_at[0:1, e:e + 1], engines=(engine,), min_val=0, max_val=E * CAP - P,
                                    skip_runtime_bounds_check_because=IN_RANGE)
                eng.dma_start(routed[bass.ds(at, P), :], pad_row[:, :]).then_inc(sm["pads_out"], 16)

        def heads(rows_):
            return rows_[:, :].rearrange("p (o n) -> p o n", o=1).to_broadcast([PARTS, GRP, S])

        def moments(eng, st, mean, var, sem_, before):
            sq, dif, dd, both = (mom[:, k, :] for k in range(4))
            eng.tensor_tensor(sq, st[:, :, 2], st[:, :, 5], ALU.add).then_inc(sem_, 1)
            eng.tensor_tensor(dif, st[:, :, 1], st[:, :, 4], ALU.subtract).then_inc(sem_, 1)
            eng.tensor_tensor(both, st[:, :, 1], st[:, :, 4], ALU.add).then_inc(sem_, 1)
            eng.wait_ge(sem_, before + 3)
            eng.tensor_scalar(mean, both, 0.5, None, ALU.mult).then_inc(sem_, 1)
            eng.tensor_tensor(dd, dif, dif, ALU.mult).then_inc(sem_, 1)
            eng.wait_ge(sem_, before + 5)
            eng.tensor_scalar(dd, dd, 0.25, EPS, ALU.mult, ALU.add).then_inc(sem_, 1)
            eng.wait_ge(sem_, before + 6)
            eng.tensor_scalar(sq, sq, 1.0 / D, None, ALU.mult).then_inc(sem_, 1)
            eng.wait_ge(sem_, before + 7)
            eng.tensor_tensor(var, dd, sq, ALU.add).then_inc(sem_, 1)

        MOMENTS = 8
        PLACES = 7

        @block.sync
        def _(sp):
            zt = z.rearrange("(t p) d -> p t d", p=P)
            col = lambda a: a.rearrange("(p o) -> p o", o=1)
            row = lambda a: a.rearrange("(o n) -> o n", o=1).to_broadcast([P, a.shape[0]])
            def load_z(b):
                sp.dma_start(x_sb[:, QB * b:QB * (b + 1), :], zt[:, QB * b:QB * (b + 1), :]).then_inc(z_in[b], 16)

            load_z(0)
            with nc.allow_non_contiguous_dma(reason="a few columns of parameters"):
                for dst, src in ((ln_wc[:, :], col(ln_w)), (ln_bc[:, :], col(ln_b)),
                                 (b_qkc[:, :], b_qk.rearrange("(s p) -> p s", p=P)), (wqk_sb[:, :], w_qk)):
                    sp.dma_start(dst, src).then_inc(sm["qk_weights"], 16)
                load_z(1)
                for dst, src in ((wv_sb[:, :], w_v), (bv_col[:, :], col(b_v)), (wp_sb[:, :], w_proj),
                                 (bp_sb[:, :], row(b_proj)), (gw_sb[:, :], gate_w), (gb_sb[:, :], row(gate_b))):
                    sp.dma_start(dst, src).then_inc(sm["weights"], 16)
            for b in range(2, B):
                load_z(b)

            def store_parts(b, par, units, signal):
                for g in units:
                    for side, to in ((0, q_parts), (1, k_parts)):
                        sp.dma_start(to[bass.ds(b, 1), g].rearrange("o t c n -> c (o t) n"),
                                     parts[GRP * DH * g:GRP * DH * (g + 1), par, side]).then_inc(signal, 16)

            def zeros(g):
                sp.dma_start(qs[ROWS:ROWS + PARTS, g, :, :], heads(zero_rows)).then_inc(loaded[g], 16)

            def ones(g):
                sp.dma_start(ks[ROWS:ROWS + PARTS, g, :, :], heads(one_rows)).then_inc(sm["ones_in"], 16)

            def load(b, g):
                for t in range(PARTS):
                    r = slice(t * PARTS * DH, (t + 1) * PARTS * DH)
                    sp.dma_start(qs[r, g].rearrange("r j n -> r (j n)"),
                                 q_parts[bass.ds(b, 1), g, t].rearrange("o (d j) n -> o d (j n)", d=DH)
                                 .to_broadcast([PARTS, DH, GRP * S])).then_inc(loaded[g], 16)
                sp.dma_start(ks[0:ROWS, g].rearrange("r j n -> r (j n)"),
                             k_parts[bass.ds(b, 1), g].rearrange("o u (d j) n -> o (u d) (j n)", d=DH)
                             .to_broadcast([PARTS, PARTS * DH, GRP * S])).then_inc(loaded[g], 16)

            def mrow_out(v, g):
                sp.wait_ge(sm["mrow_ok"], v + 1)
                for a in range(PARTS):
                    sp.dma_start(qs[ROWS + a:ROWS + a + 1, g, :, :], mrow[GRP * a:GRP * (a + 1), :])\
                      .then_inc(mrow_in[g], 16)

            sp.wait_ge(sm["consts"], 4)
            ones(0)
            zeros(0)
            sp.wait_ge(pr["lo_ok"][0], 2)
            store_parts(0, 0, (0,), sm["first_out"])
            store_parts(0, 0, (1, 2), parts_out[0])
            sp.wait_ge(sm["first_out"], FIRST)
            load(0, 0)
            store_parts(0, 0, (3,), parts_out[0])
            sp.wait_ge(parts_out[0], STORE - FIRST)
            sp.wait_ge(sm["cleared"], 2)
            for g in range(1, NG):
                ones(g)
                if g < 3:
                    zeros(g)
                    load(0, g)
            mrow_out(0, 0)
            sp.wait_ge(pr["lo_ok"][1], 2)
            store_parts(1, 1, range(NG), parts_out[1])

            def slots(b, first, last, later, stored):
                for g in range(NG):
                    s = NG * b + g
                    if not (last and g > 0):
                        if not (first and g == 0):
                            sp.wait_ge(sm["pair_ok"], 2 * QB * s)
                        zeros((g + 3) % NG)
                        if g == 1:
                            if first:
                                sp.wait_ge(parts_out[1], STORE)
                            else:
                                sp.wait_ge(parts_out[0], STORE * (b + 1) - FIRST)
                        load(b + (g + 3) // NG, (g + 3) % NG)
                    if not (last and g == NG - 1):
                        mrow_out(s + 1, (g + 1) % NG)
                    if g == 0 and stored:
                        sp.wait_ge(sm["later_lo"], 2 * b)
                        store_parts(b + 1, 0, range(NG), parts_out[0])

            slots(0, True, False, True, False)
            w1e = w1_sb[:, :].rearrange("p (e c) -> p e c", e=E)
            sp.dma_start(w1e[:, :, 0:FF], w1.rearrange("e d f -> d e f"))\
              .then_inc(sm["moe_weights"], 16)
            sp.dma_start(w2_sb[:, :].rearrange("p (e c d) -> p (e c) d", e=E, d=D),
                         w2.rearrange("e (c f) d -> f (e c) d", f=P)).then_inc(sm["moe_weights"], 16)
            sp.dma_start(w1e[:, :, B1:B2], b1t).then_inc(sm["moe_weights"], 16)
            sp.dma_start(w1e[:, :, B2:WCOLS], b2.rearrange("(o e) d -> o e d", o=1).to_broadcast([P, E, D]))\
              .then_inc(sm["moe_weights"], 16)
            with sp.Fori(1, B - 2) as b:
                slots(b, False, False, True, True)
            slots(B - 2, False, False, False, True)
            slots(B - 1, False, True, False, False)

            def first_row(i):
                return nc.values_load(table[0:1, 0, bass.ds(i, 1)], engines=(mybir.EngineType.SP,), min_val=0,
                                      max_val=E * CAP - P, skip_runtime_bounds_check_because=IN_RANGE)

            def load_rows(k, at):
                sp.dma_start(rows[:, k, :], routed[bass.ds(at, P), :]).then_inc(rows_in[k], 16)

            store_pads(sp, mybir.EngineType.SP, range(E // 2))
            sp.wait_ge(sm["table_ok"], 1)
            ready = [first_row(k) for k in range(2)]
            sp.wait_ge(sm["routed_out"], 16 * TILES)
            sp.wait_ge(sm["pads_out"], 16 * E)
            for k in range(STEP):
                load_rows(k, ready[k] if k < len(ready) else first_row(k))

            def reload(r, tiles):
                for k in range(tiles):
                    at = first_row(STEP * (r + 1) + k)
                    sp.wait_ge(sm["fstat_ok"], STEP * r + k + 1)
                    load_rows(k, at)

            with sp.Fori(0, PASSES - 2) as r:
                reload(r, STEP)
            reload(PASSES - 2, NT - STEP * (PASSES - 1))
            for h in range(2):
                sp.wait_ge(stored[h], 16 * GROUP * ((GROUPS + 1 - h) // 2))
            sp.wait_ge(sm["last_stored"], 16 * (NT - GROUP * GROUPS))

        @block.gpsimd
        def _(pool):
            pool.memset(ident[:, :], 0.0).then_inc(sm["ident_ok"], 1)
            pool.memset(ones_b[:, :], 1.0).then_inc(sm["ident_ok"], 1)
            pool.memset(half[:, :], -0.5)
            pool.wait_ge(sm["ident_ok"], 2)
            pool.affine_select(out=ident[:, :], in_=ident[:, :], compare_op=ALU.not_equal, fill=1.0, base=0,
                               pattern=[[-1, P]], channel_multiplier=1).then_inc(sm["ident_ok"], 1)
            pool.affine_select(out=below[:, :], in_=ones_b[:, :], compare_op=ALU.is_gt, fill=0.0, base=0,
                               pattern=[[1, P]], channel_multiplier=-1).then_inc(sm["ident_ok"], 1)

            def rstd_of(b):
                r = slice(QB * b, QB * (b + 1))
                pool.wait_ge(sm["stat_ok"], b + 1)
                pool.tensor_scalar(ve[:, r], mv[:, r, 1], EPS, None, ALU.add).then_inc(sm["ve_ok"], 1)
                pool.wait_ge(sm["ve_ok"], b + 1)
                pool.tensor_tensor(rstd[:, r], ve[:, r], half[:, :], ALU.pow).then_inc(sm["rstd_ok"], 1)

            rstd_of(0)
            rstd_of(1)
            pool.wait_ge(sm["rstd_ok"], 2)
            for t in (qs, ks):
                pool.memset(t[64:KROWS, 1:NG, :, :].rearrange("p g j n -> p (g j n)").bitcast(U32), 0)\
                    .then_inc(sm["cleared"], 1)
            pool.wait_ge(sm["cleared"], 2)
            pool.memset(vs[:, :, :, :, :], 0.0).then_inc(sm["cleared"], 1)
            pool.wait_ge(sm["cleared"], 3)
            pool.memset(vs[:, :, :, :, DH:DH + 1], 1.0).then_inc(sm["cleared"], 1)
            for side in range(2):
                pool.wait_ge(pr["mid_ok"][1], side + 1)
                pool.tensor_tensor(parts[:, 1, side, 2], rest[:, 1, side], parts[:, 1, side, 1],
                                   ALU.subtract).then_inc(pr["lo_ok"][1], 1)
            pool.memset(token[:, :], 0.0)
            for at, pat, start, ch in ((0, [[CAP, E]], 0, 0), (E, [[-1, E]], E, 0), (2 * E, [[0, 1]], 0, 1),
                                       (2 * E + 1, [[P, NT]], 0, 0), (2 * E + 1 + NT, [[1, NT]], 0, 0)):
                pool.iota(numbers[:, at:at + pat[0][1]], pattern=pat, base=start, channel_multiplier=ch)\
                    .then_inc(sm["consts2"], 1)
            pool.iota(token_i[:, :], pattern=[[P, QB]], base=0, channel_multiplier=1).then_inc(sm["consts2"], 1)
            pool.wait_ge(sm["consts2"], 6)
            pool.tensor_copy(numbers_f[:, :], numbers[:, :]).then_inc(sm["numbers_ok"], 1)
            pool.tensor_copy(token[:, :], token_i[:, :]).then_inc(sm["numbers_ok"], 1)
            pool.memset(pad_row[:, 0:D + 1], 0.0)
            pool.memset(pad_row[:, D + 1:ROW].bitcast(I32), FAR).then_inc(sm["numbers_ok"], 1)
            pool.wait_ge(sm["numbers_ok"], 3)
            pool.tensor_copy(base[:, :], numbers_f[:, 0:E]).then_inc(sm["ranks_copied"], 1)
            pool.tensor_copy(y_sb[:, :, D + 1].bitcast(I32), token[:, :]).then_inc(sm["token_ok"], 1)

            def values(b, g):
                src = v_all[:, QB * b:QB * (b + 1), GRP * DH * g:GRP * DH * (g + 1)]
                pool.tensor_copy(vs[:, g, :, :, 0:DH], src.rearrange("p c (j d) -> p c j d", d=DH))\
                    .then_inc(sm["vs_ok"], 1)

            pool.wait_ge(sm["cleared"], 4)
            pool.wait_ge(pr["v_all_ok"][0], 1)
            for g in range(NG):
                values(0, g)
            pool.wait_ge(pr["v_all_ok"][1], 1)

            def later_zn(a):
                if a > 0:
                    pool.wait_ge(sm["later_zT"], a)
                pool.wait_ge(sm["rstd_ok"], a + 3)
                for t in range(QB):
                    n = QB * (a + 2) + t
                    last = pool.tensor_scalar(zn[:, 0, t, :], x_sb[:, n, :], mv[:, n, 0:1], rstd[:, n:n + 1],
                                              ALU.subtract, ALU.mult)
                last.then_inc(sm["later_zn"], 1)

            def twice(a):
                xb = x_sb[:, QB * (a + 2):QB * (a + 3), :]
                pool.wait_ge(sm["later_zn"], a + 1)
                pool.tensor_tensor(xb, xb, xb, ALU.add).then_inc(sm["later_twice"], 1)
                pool.wait_ge(sm["later_twice"], a + 1)
                pool.tensor_tensor(xb, xb, bp_sb[:, :].rearrange("p (o d) -> p o d", o=1)
                                   .to_broadcast([P, QB, D]), ALU.add).then_inc(sm["later_zb"], 1)

            def later_rests(a):
                for side in range(2):
                    pool.wait_ge(sm["later_hi"], 2 * a + side + 1)
                    pool.tensor_tensor(rest[:, 1, side], rest[:, 0, side], parts[:, 0, side, 0],
                                       ALU.subtract).then_inc(sm["later_rest"], 1)

            def later_lows(a):
                for side in range(2):
                    pool.wait_ge(sm["later_mid"], 2 * a + side + 1)
                    pool.tensor_tensor(parts[:, 0, side, 2], rest[:, 1, side], parts[:, 0, side, 1],
                                       ALU.subtract).then_inc(sm["later_lo"], 1)

            def x1_of(ob, tiles):
                y = rows_of(ob)
                pool.wait_ge(sm["yrstd_ok"], ob + 1)
                for t in tiles:
                    last = pool.tensor_scalar(y[:, t, 0:D], y[:, t, 0:D], ymean[:, t:t + 1],
                                              yrstd[:, t:t + 1], ALU.subtract, ALU.mult)
                if t == QB - 1:
                    last.then_inc(sm["x1_ok"], 1)

            def split_maxima(v):
                m = negm[:, v % 2]
                pool.wait_ge(sm["max_used"], GRP * QB * (v + 1))
                if v > 0:
                    pool.wait_ge(sm["mT_ok"], v)
                hi, mid, lo = (negm_p[:, :, a, :] for a in range(PARTS))
                pool.tensor_copy(hi, m).then_inc(sm["nm_link"], 1)
                pool.wait_ge(sm["nm_link"], 3 * v + 1)
                pool.tensor_tensor(negm_r[:, :, :], m, hi, ALU.subtract).then_inc(sm["nm_link"], 1)
                pool.wait_ge(sm["nm_link"], 3 * v + 2)
                pool.tensor_copy(mid, negm_r[:, :, :]).then_inc(sm["nm_link"], 1)
                pool.wait_ge(sm["nm_link"], 3 * v + 3)
                pool.tensor_tensor(lo, negm_r[:, :, :], mid, ALU.subtract).then_inc(sm["nm_ok"], 1)

            def last_rstd():
                pool.wait_ge(sm["last_var_ok"], 1)
                pool.tensor_tensor(yrstd[:, :], yvar[:, :], half[:, :], ALU.pow).then_inc(sm["yrstd_ok"], 1)

            def norm_of(ob):
                pool.wait_ge(sm["ystat_ok"], QB * (ob + 1))
                moments(pool, ystats, ymean[:, :], yvar[:, :], sm["mom_link"], MOMENTS * ob)
                pool.wait_ge(sm["mom_link"], MOMENTS * (ob + 1))
                pool.tensor_tensor(yrstd[:, :], yvar[:, :], half[:, :], ALU.pow).then_inc(sm["yrstd_ok"], 1)

            def slots_of(ob):
                def link(op, n):
                    op.then_inc(sm["place_link"], 1)
                    pool.wait_ge(sm["place_link"], PLACES * ob + n)

                pool.wait_ge(sm["ranks_copied"], ob + 2)
                link(pool.tensor_tensor(place[:, :, :], base[:, :].rearrange("p (o e) -> p o e", o=1)
                                        .to_broadcast([P, QB, E]), ranks[:, 0:QB, :], ALU.add), 1)
                link(pool.tensor_tensor(base[:, :], base[:, :], ranks[:, QB, :], ALU.add), 2)
                link(pool.tensor_tensor(place[:, :, :], place[:, :, :], onehot[:, :, :], ALU.mult), 3)
                for n, w in ((4, 4), (5, 2), (6, 1)):
                    link(pool.tensor_tensor(place[:, :, 0:w], place[:, :, 0:w], place[:, :, w:2 * w], ALU.add), n)
                link(pool.tensor_copy(slot[:, ob % 2, :], place[:, :, 0]), PLACES)

            def scatter(ob):
                pool.wait_ge(sm["weight_ok"], ob + 1)
                wait_x1(pool, ob)
                for t in range(QB):
                    pool.indirect_dma_start(routed[:, :],
                                            bass.IndirectOffsetOnAxis(ap=slot[:, ob % 2, t:t + 1], axis=0),
                                            rows_of(ob)[:, t, :], None).then_inc(sm["routed_out"], 16)

            def next_numbers(nb):
                pool.tensor_scalar(token[:, :], token[:, :], float(S), None, ALU.add)\
                    .then_inc(sm["token_link"], 1)
                if nb < B - 1:
                    pool.wait_ge(sm["routed_out"], 16 * QB * nb)
                pool.wait_ge(sm["token_link"], nb)
                pool.tensor_copy(rows_of(nb)[:, :, D + 1].bitcast(I32), token[:, :]).then_inc(sm["token_ok"], 1)

            def slots(b, first, last, later):
                for g in range(NG):
                    if not (last and g == NG - 1):
                        split_maxima(NG * b + g + 1)
                    if g == 0 and 0 < b < B - 1:
                        later_lows(b - 1)
                    if g == 3 and not first:
                        x1_of(b - 1, (2, 3))
                    if not (first and g == 0) and not (last and g > 0):
                        pool.wait_ge(sm["pv_ok"], QB * (NG * b + g))
                        values(b if g == 0 else b + 1, (g - 1) % NG)
                    if g == 0 and b > 1:
                        slots_of(b - 2)
                        scatter(b - 2)
                        next_numbers(b - 1)
                    if g == 1 and later:
                        rstd_of(b + 2)
                        later_zn(b)
                        twice(b)
                    if g == 2 and not first:
                        norm_of(b - 1)
                        x1_of(b - 1, (0, 1))
                    if g == 3 and later:
                        later_rests(b)

            split_maxima(0)
            for b in range(B):
                slots(b, b == 0, b == B - 1, b < B - 2)
            next_numbers(B - 1)
            slots_of(B - 2)
            last_rstd()
            scatter(B - 2)
            slots_of(B - 1)
            scatter(B - 1)

            def scale_of(n):
                h = n % 2
                pool.wait_ge(sm["faggr_ok"], GROUP * (n + 1))
                pool.tensor_scalar(fvar[:, h], f_mv[:, h, :, 1], EPS, None, ALU.add).then_inc(sm["fmom_link"], 1)
                pool.wait_ge(sm["fmom_link"], 3 * n + 1)
                pool.tensor_tensor(frstd[:, h], fvar[:, h], half[:, :], ALU.pow).then_inc(sm["fmom_link"], 1)
                pool.wait_ge(sm["fmom_link"], 3 * n + 2)
                pool.tensor_tensor(fshift[:, h], f_mv[:, h, :, 0], frstd[:, h], ALU.mult)\
                    .then_inc(sm["fmom_link"], 1)
                pool.wait_ge(sm["fmom_link"], 3 * (n + 1))
                pool.tensor_scalar(fshift[:, h], fshift[:, h], -1.0, None, ALU.mult).then_inc(sm["frstd_ok"], 1)

            def store(n, tiles):
                h = n % 2
                for k in tiles:
                    pool.wait_ge(sm["final_ok"], GROUP * n + k + 1)
                    pool.indirect_dma_start(
                        out[:, :], bass.IndirectOffsetOnAxis(ap=out_number[:, h, k:k + 1].bitcast(U32), axis=0),
                        final[:, h, k, :], None, bounds_check=TILES * P - 1, oob_is_err=False)\
                        .then_inc(stored[h], 16)

            def last_rstds(a, z_):
                pool.wait_ge(sm["last_fvar_ok"], z_)
                pool.tensor_tensor(frstd_last[:, a:z_], fvar_last[:, a:z_], half[:, a:z_], ALU.pow)\
                    .then_inc(sm["last_frstd_ok"], z_ - a)

            for n in range(GROUPS):
                if n == GROUPS - 1:
                    store(n - 1, (2, 3))
                scale_of(n)
                if 0 < n < GROUPS - 1:
                    store(n - 1, (2, 3))
                if n < GROUPS - 1:
                    store(n, (0, 1))
            store(GROUPS - 1, (0,))
            last_rstds(0, LAST)
            store(GROUPS - 1, (1, 2, 3))
            for c in range(LAST):
                pool.wait_ge(sm["last_final_ok"], c + 1)
                pool.indirect_dma_start(
                    out[:, :], bass.IndirectOffsetOnAxis(ap=number_last[:, c:c + 1].bitcast(U32), axis=0),
                    final_last[:, c, :], None, bounds_check=TILES * P - 1, oob_is_err=False)\
                    .then_inc(sm["last_stored"], 16)

        @block.vector
        def _(dve):
            V = nc.vector

            def z_stat(b, t):
                dve.wait_ge(z_in[b], 16)
                V.bn_stats(zstats[:, QB * b + t, :], x_sb[:, QB * b + t, :]).then_inc(sm["stat_link"], 1)

            def z_stats(b):
                for t in range(QB):
                    z_stat(b, t)
                z_aggregates(b)

            def z_aggregates(b):
                dve.wait_ge(sm["stat_link"], QB * b + QB)
                for t in range(QB):
                    last = V.bn_aggr(mv[:, QB * b + t, :], zstats[:, QB * b + t, :])
                last.then_inc(sm["stat_ok"], 1)

            def zn_of(b):
                for t in range(QB):
                    n = QB * b + t
                    last = V.tensor_scalar(zn[:, b, t, :], x_sb[:, n, :], mv[:, n, 0:1], rstd[:, n:n + 1],
                                           ALU.subtract, ALU.mult)
                return last

            V.memset(zero_rows[:, :], 0.0).then_inc(sm["consts"], 1)
            V.memset(one_rows[:, :], 1.0).then_inc(sm["consts"], 1)
            for t in (qs, ks):
                V.memset(t[64:KROWS, 0, :, :].rearrange("p j n -> p (j n)").bitcast(U32), 0)\
                 .then_inc(sm["consts"], 1)
            z_stats(0)
            z_stats(1)
            for b in range(2):
                dve.wait_ge(sm["rstd_ok"], b + 1)
                zn_of(b).then_inc(pr["zn_ok"][b], 1)
            dve.wait_ge(sm["weights"], WEIGHTS)
            V.tensor_copy(bv_rep[:, :], bv_col[:, :].to_broadcast([P, P])).then_inc(sm["bv_ok"], 1)
            for par in range(2):
                for side, name in ((0, "q_ok"), (1, "k_ok")):
                    dve.wait_ge(pr[name][par], 1)
                    dve.wait_ge(pr["hi_ok"][par], side + 1)
                    V.scalar_tensor_tensor(
                        out=rest[:, par, side], in0=ps[:, 2 + 2 * side + par, :], scalar=b_qkc[:, side:side + 1],
                        in1=parts[:, par, side, 0], op0=ALU.add, op1=ALU.subtract).then_inc(pr["rest_ok"][par], 1)
                if par == 0:
                    for side in range(2):
                        dve.wait_ge(pr["mid_ok"][par], side + 1)
                        V.tensor_tensor(parts[:, par, side, 2], rest[:, par, side], parts[:, par, side, 1],
                                        ALU.subtract).then_inc(pr["lo_ok"][par], 1)
            dve.wait_ge(sm["bias_ok"], 1)
            V.tensor_tensor(bp_sb[:, :], ps[:, 0, 0:D], bp_sb[:, :], ALU.add).then_inc(sm["bias_added"], 1)
            dve.wait_ge(sm["bias_added"], 1)
            for b in range(2):
                xb = x_sb[:, QB * b:QB * (b + 1), :]
                V.scalar_tensor_tensor(out=xb, in0=xb, scalar=2.0, in1=bp_sb[:, :]
                                       .rearrange("p (o d) -> p o d", o=1).to_broadcast([P, QB, D]),
                                       op0=ALU.mult, op1=ALU.add)
            for b in range(2, 4):
                z_stats(b)

            def maximum(v, par, j, qb):
                n = GRP * QB * v + QB * j + qb
                if j == 0 and qb == 0 and not (isinstance(v, int) and v < 2):
                    dve.wait_ge(sm["nm_ok"], v - 1)
                dve.wait_ge(sm["max_ok"], n + 1)
                V.tensor_reduce(negm[:, par, qb, j:j + 1], ps[:, 4 + qb % 2, :], AX.X, ALU.max, negate=True)\
                 .then_inc(sm["max_used"], 1)

            def by_head(ob, qb):
                return ps[:, qb if is_last(ob) else MISC, :].rearrange("p (h c) -> p h c", c=HW)

            def row_sums(ob, qb):
                dve.wait_ge(sm["tr_ok"], QB * ob + qb + 1)
                V.reciprocal(rec[:, qb, :], by_head(ob, qb)[:, :, DH]).then_inc(sm["rec_ok"], 1)

            def normalise(ob, qb):
                dve.wait_ge(sm["rec_ok"], QB * ob + qb + 1)
                V.tensor_tensor(o_sb[:, qb, :].rearrange("p (h d) -> p h d", d=DH), by_head(ob, qb)[:, :, 0:DH],
                                rec[:, qb, :].rearrange("p (h o) -> p h o", o=1).to_broadcast([P, H, DH]),
                                ALU.mult).then_inc(sm["norm_ok"], 1)

            def residual(ob, qb, y):
                t = QB * ob + qb
                dve.wait_ge(sm["proj_ok"], t + 1)
                bank = 4 + qb if is_last(ob) else MISC
                V.tensor_tensor(y[:, qb, 0:D], ps[:, bank, P:2 * P], x_sb[:, bass.ds(t, 1), :]
                                .rearrange("p o d -> p (o d)"), ALU.add).then_inc(sm["y_ok"], 1)

            def y_stats(ob, qb, y):
                dve.wait_ge(sm["y_ok"], QB * ob + qb + 1)
                V.bn_stats(ystats[:, qb, :], y[:, qb, 0:D]).then_inc(sm["ystat_ok"], 1)

            def over_tiles(a):
                return a.rearrange("p (o e) -> p o e", o=1).to_broadcast([P, QB, E])

            def over_experts(a):
                return a[:, :].rearrange("p (t o) -> p t o", o=1).to_broadcast([P, QB, E])

            rev = numbers_f[:, E:2 * E]

            def gate(ob, step):
                n = ob + 1
                if step == 0:
                    dve.wait_ge(sm["logits_ok"], n)
                    V.tensor_tensor(logits[:, :, :], ps[:, MISC, 0:QB * E].rearrange("p (t e) -> p t e", e=E),
                                    over_tiles(gb_sb[:, :]), ALU.add).then_inc(sm["lg_ok"], 1)
                if step == 1:
                    dve.wait_ge(sm["lg_ok"], n)
                    V.tensor_reduce(top[:, :], logits[:, :, :], AX.X, ALU.max).then_inc(sm["top_ok"], 1)
                if step == 2:
                    dve.wait_ge(sm["top_ok"], n)
                    V.tensor_tensor(shifted[:, :, :], logits[:, :, :], over_experts(top), ALU.subtract)\
                     .then_inc(sm["shifted_ok"], 1)
                    V.tensor_tensor(is_top[:, :, :], logits[:, :, :], over_experts(top), ALU.is_equal)\
                     .then_inc(sm["is_top_ok"], 1)
                if step == 3:
                    dve.wait_ge(sm["is_top_ok"], n)
                    V.tensor_tensor(cand[:, :, :], is_top[:, :, :], over_tiles(rev), ALU.mult)\
                     .then_inc(sm["cand_ok"], 1)
                if step == 4:
                    dve.wait_ge(sm["cand_ok"], n)
                    V.tensor_reduce(found[:, :], cand[:, :, :], AX.X, ALU.max).then_inc(sm["found_ok"], 1)
                if step == 5:
                    dve.wait_ge(sm["found_ok"], n)
                    V.tensor_tensor(onehot[:, :, :], cand[:, :, :], over_experts(found), ALU.is_equal)\
                     .then_inc(sm["onehot_ok"], 1)

                if step == 6:
                    dve.wait_ge(sm["ex_ok"], n)
                    V.tensor_reduce(total[:, :], ex[:, :, :], AX.X, ALU.add).then_inc(sm["total_ok"], 1)
                if step == 7:
                    dve.wait_ge(sm["ranks_ok"], n)
                    V.tensor_copy(ranks[:, :, :], ps[:, MISC, 0:(QB + 1) * E]
                                  .rearrange("p (t e) -> p t e", e=E)).then_inc(sm["ranks_copied"], 1)
                    dve.wait_ge(sm["total_ok"], n)
                    V.reciprocal(rows_of(ob)[:, :, D], total[:, :]).then_inc(sm["weight_ok"], 1)

            def slots(b, first, last, later):
                for g in range(NG):
                    s = NG * b + g
                    more = not (last and g >= 2)
                    for kc in range(QB):
                        for qb in range(QB):
                            if more:
                                maximum(s + 2, g % 2, kc, qb)
                            if first:
                                if qb == 2:
                                    z_stat(4 + g, kc)
                                if kc == QB - 1 and qb == QB - 1:
                                    z_aggregates(4 + g)
                                continue
                            if (g, kc) in RESIDUAL_AT:
                                t = RESIDUAL_AT[g, kc]
                                if qb == 0:
                                    if t == 0:
                                        dve.wait_ge(sm["token_ok"], b)
                                        dve.wait_ge(sm["later_zb"], b if not last else b - 1)
                                    residual(b - 1, t, y_sb)
                                if qb == 2:
                                    y_stats(b - 1, t, y_sb)
                            if (g, kc) in TOKENS_AT:
                                t = TOKENS_AT[g, kc]
                                if qb == (3 if (g, kc) in BEFORE_PV else 2):
                                    if t == 0:
                                        dve.wait_ge(sm["max_used"], GRP * QB * (s + 2) + QB * kc + qb + 1)
                                    row_sums(b - 1, t)
                                    normalise(b - 1, t)
                            for step in GATE_AT.get((g, kc, qb), ()):
                                gate(b - 1, step)

            for v in range(2):
                for j in range(GRP):
                    for half_ in range(2):
                        n = GRP * QB * v + QB * j + 2 * half_
                        dve.wait_ge(sm["max_ok"], n + 2)
                        bank = n % 6
                        V.tensor_reduce(negm[:, v, 2 * half_:2 * half_ + 2, j], ps[:, bank:bank + 2, :],
                                        AX.X, ALU.max, negate=True).then_inc(sm["max_used"], 2)
            slots(0, True, False, True)
            with dve.Fori(1, B - 2) as b:
                slots(b, False, False, True)
            slots(B - 2, False, False, False)
            slots(B - 1, False, True, False)
            ob = B - 1
            for qb in range(QB):
                row_sums(ob, qb)
            for qb in range(QB):
                normalise(ob, qb)
            for qb in range(QB):
                residual(ob, qb, y_last)
                y_stats(ob, qb, y_last)
            dve.wait_ge(sm["ystat_ok"], TILES)
            for t in range(QB):
                last = V.bn_aggr(y_mv[:, t, :], ystats[:, t, :])
            last.then_inc(sm["last_aggr"], 1)
            dve.wait_ge(sm["last_aggr"], 1)
            V.tensor_scalar(yvar[:, :], y_mv[:, :, 1], EPS, None, ALU.add).then_inc(sm["last_var_ok"], 1)
            dve.wait_ge(sm["yrstd_ok"], B)
            for t in range(QB):
                last = V.tensor_scalar(y_last[:, t, 0:D], y_last[:, t, 0:D], y_mv[:, t, 0:1],
                                       yrstd[:, t:t + 1], ALU.subtract, ALU.mult)
            last.then_inc(sm["last_x1_ok"], 1)
            for step in range(8):
                gate(ob, step)

            links = [0]

            def link(op):
                links[0] += 1
                op.then_inc(sm["route_link"], 1)
                dve.wait_ge(sm["route_link"], links[0])

            first_row = numbers_f[0:1, 2 * E + 1:2 * E + 1 + NT]
            tile_no = numbers_f[0:1, 2 * E + 1 + NT:]
            dve.wait_ge(sm["place_link"], PLACES * (B - 1) + 2)
            V.tensor_copy(pad_at[:, :], base[0:1, :]).then_inc(sm["pads_ok"], 1)
            link(V.tensor_tensor(count[:, :], base[0:1, :], numbers_f[0:1, 0:E], ALU.subtract))
            c0 = count[:, :]
            link(V.tensor_scalar(ends0[:, :], c0, 1.0 / P, (P - 1) / (2.0 * P), ALU.mult, ALU.add))
            link(V.tensor_scalar(ends1[:, :], ends0[:, :], ROUND, None, ALU.add))
            link(V.tensor_scalar(tiles_of[:, :], ends1[:, :], -ROUND, None, ALU.add))
            a, b_ = tiles_of, ends0
            for n in (1, 2, 4):
                V.tensor_copy(b_[:, 0:n], a[:, 0:n])
                link(V.tensor_tensor(b_[:, n:], a[:, n:], a[:, 0:E - n], ALU.add))
                a, b_ = b_, (ends1 if b_ is ends0 else ends0)
            ends = a
            shape = [1, NT, E - 1]
            link(V.tensor_tensor(after[:, :, :], tile_no.rearrange("p (i o) -> p i o", o=1).to_broadcast(shape),
                                 ends[:, 0:E - 1].rearrange("p (o e) -> p o e", o=1).to_broadcast(shape),
                                 ALU.is_ge))
            link(V.tensor_scalar(weight_of[:, :], tiles_of[:, :], -float(P), float(CAP), ALU.mult, ALU.add))
            link(V.tensor_tensor(after_w[:, :, :], after[:, :, :],
                                 weight_of[:, 0:E - 1].rearrange("p (o e) -> p o e", o=1).to_broadcast(shape),
                                 ALU.mult))
            link(V.tensor_reduce(table_f[:, 1, :], after[:, :, :], AX.X, ALU.add))
            link(V.tensor_reduce(table_f[:, 0, :], after_w[:, :, :], AX.X, ALU.add))
            link(V.tensor_tensor(table_f[:, 0, :], table_f[:, 0, :], first_row, ALU.add))
            link(V.tensor_scalar(limit[:, :], c0[:, E - 1:E], float((E - 1) * CAP), None, ALU.add))
            link(V.tensor_scalar(table_f[:, 0, :], table_f[:, 0, :], limit[:, :], None, ALU.min))
            V.tensor_copy(table[:, :, :], table_f[:, :, :]).then_inc(sm["table_ok"], 1)
            dve.wait_ge(sm["table_ok"], 1)
            dve.wait_ge(sm["moe_weights"], MOE_WEIGHTS)

            def choose(i, k):
                e = nc.values_load(table[0:1, 1, bass.ds(i, 1)], engines=(mybir.EngineType.DVE,), min_val=0,
                                   max_val=E - 1, skip_runtime_bounds_check_because=IN_RANGE)
                if not (isinstance(i, int) and i < GROUP):
                    dve.wait_ge(sm["gelu_ok"], i - GROUP + 1)
                    dve.wait_ge(sm["yb_ok"], i - GROUP + 1)
                V.tensor_copy(chosen[:, k % GROUP, :], w1_sb[:, bass.ds(e * WCOLS, WCOLS)])\
                 .then_inc(sm["chosen_ok"], 1)

            def aggregate(k):
                V.bn_aggr(f_mv[:, k // GROUP, k % GROUP, :], fstats[:, k // GROUP, k % GROUP, :])\
                 .then_inc(sm["faggr_ok"], 1)

            def add_bias(i, k, r):
                if not (isinstance(i, int) and i == 0):
                    dve.wait_ge(sm["fstat_ok"], i)
                dve.wait_ge(rows_in[k], 16 * (r + 1))
                dve.wait_ge(sm["mm2_ok"], i + 1)
                V.tensor_tensor(yb[:, k % 2, :], ps[:, 4 + k % 2, 0:D], chosen[:, k % GROUP, B2:WCOLS], ALU.add)\
                 .then_inc(sm["yb_ok"], 1)
                if not (isinstance(i, int) and i == 0):
                    aggregate((k - 1) % STEP)

            def i_is_last(i):
                return isinstance(i, int) and i >= GROUP * GROUPS

            def combine(i, k, r):
                h, c = k // GROUP, k % GROUP
                if not (isinstance(r, int) and r == 0):
                    dve.wait_ge(sm["final_ok"], i - STEP + 1)
                if i_is_last(i):
                    V.tensor_copy(number_last[:, c:c + 1], rows[:, k, D + 1:ROW].bitcast(I32))
                else:
                    V.tensor_copy(res_number[:, c:c + 1], rows[:, k, D + 1:ROW].bitcast(I32))\
                     .then_inc(sm["number_ok"], 1)
                dve.wait_ge(sm["yb_ok"], i + 1)
                V.scalar_tensor_tensor(out=res[:, h, c, :], in0=yb[:, k % 2, :], scalar=rows[:, k, D:D + 1],
                                       in1=rows[:, k, 0:D], op0=ALU.mult, op1=ALU.add).then_inc(sm["res_ok"], 1)
                if c == GROUP - 1:
                    if not (isinstance(r, int) and r == 0):
                        dve.wait_ge(stored[h], 16 * GROUP * r)
                    dve.wait_ge(sm["number_ok"], i + 1)
                    V.tensor_copy(out_number[:, h, :], res_number[:, :])
                dve.wait_ge(sm["res_ok"], i + 1)
                V.bn_stats(fstats[:, h, c, :], res[:, h, c, :]).then_inc(sm["fstat_ok"], 1)

            def last_variance(c):
                dve.wait_ge(sm["faggr_ok"], GROUP * GROUPS + c + 1)
                V.tensor_scalar(fvar_last[:, c:c + 1], f_mv[:, GROUPS % 2, c, 1:2], EPS, None, ALU.add)\
                 .then_inc(sm["last_fvar_ok"], 1)

            def last_final(c):
                dve.wait_ge(sm["last_frstd_ok"], c + 1)
                V.tensor_scalar(final_last[:, c, :], res[:, GROUPS % 2, c, :], f_mv[:, GROUPS % 2, c, 0:1],
                                frstd_last[:, c:c + 1], ALU.subtract, ALU.mult).then_inc(sm["last_final_ok"], 1)

            def steps(r, first, last):
                for k in range(NT - STEP * r if last else STEP):
                    i = STEP * r + k
                    before = (i - 1, (k - 1) % STEP, r if k > 0 else r - 1)
                    if not (last and i + 2 >= NT):
                        choose(i + 2, (k + 2) % STEP)
                    if not (first and k == 0):
                        add_bias(*before)
                        combine(*before)
                    if last and i_is_last(i - 2):
                        last_variance(i - 2 - GROUP * GROUPS)

            choose(0, 0)
            choose(1, 1)
            steps(0, True, False)
            with dve.Fori(1, PASSES - 1) as r:
                steps(r, False, False)
            steps(PASSES - 1, False, True)
            add_bias(NT - 1, (NT - 1) % STEP, PASSES - 1)
            last_variance(LAST - 2)
            combine(NT - 1, (NT - 1) % STEP, PASSES - 1)
            dve.wait_ge(sm["fstat_ok"], NT)
            aggregate((NT - 1) % STEP)
            last_variance(LAST - 1)
            for c in range(LAST):
                last_final(c)

        @block.scalar
        def _(act):
            A = nc.scalar
            act.wait_ge(sm["ident_ok"], 4)
            A.activation(ident_b[:, :], ident[:, :], ACT.Copy).then_inc(sm["ident_ok"], 1)
            act.wait_ge(sm["qk_weights"], QK_WEIGHTS)

            def first_znT(par):
                act.wait_ge(pr["zT_ok"][par], 1)
                A.activation(znT[:, par, :], ps[:, par, :], ACT.Identity, bias=ln_bc[:, 0:1],
                             scale=ln_wc[:, 0:1]).then_inc(pr["znT_ok"][par], 1)

            def first_hi(par, side):
                act.wait_ge(pr[("q_ok", "k_ok")[side]][par], 1)
                A.activation(parts[:, par, side, 0], ps[:, 2 + 2 * side + par, :], ACT.Identity,
                             bias=b_qkc[:, side:side + 1]).then_inc(pr["hi_ok"][par], 1)

            def first_mid(par, side):
                act.wait_ge(pr["rest_ok"][par], side + 1)
                A.activation(parts[:, par, side, 1], rest[:, par, side], ACT.Copy).then_inc(pr["mid_ok"][par], 1)

            def first_values(par):
                act.wait_ge(pr["v_ok"][par], 1)
                A.activation(v_all[:, QB * par:QB * (par + 1), :].rearrange("p c d -> p (c d)"),
                             ps[:, 6 + par, :], ACT.Copy).then_inc(pr["v_all_ok"][par], 1)

            first_znT(0)
            first_hi(0, 0)
            first_hi(0, 1)
            first_mid(0, 0)
            first_znT(1)
            first_mid(0, 1)
            first_hi(1, 0)
            first_hi(1, 1)
            first_mid(1, 0)
            first_mid(1, 1)
            first_values(0)
            first_values(1)

            def exps(s, kc, jp):
                n = 2 * QB * s + 2 * kc + jp
                act.wait_ge(sm["pair_ok"], n + 1)
                if not (isinstance(s, int) and s == 0 and kc < 2):
                    act.wait_ge(sm["pv_ok"], QB * s + kc - 1)
                k = GRP * (kc % 2) + 2 * jp
                A.activation(probs[:, k:k + 2, :], ps[:, 2 * jp:2 * jp + 2, :], ACT.Exp, scale=SCALE)\
                 .then_inc(sm["exp_ok"], 1)

            def copy_pv(s, g, b=None):
                act.wait_ge(sm["pv_ok"], QB * (s + 1))
                if g == 0 and b is not None:
                    act.wait_ge(sm["tr_ok"], QB * b)
                A.activation(oT[:, g, :], ps[:, 6, :], ACT.Copy).then_inc(sm["pv_copied"], 1)

            def copy_mrow(v):
                act.wait_ge(sm["mT_ok"], v + 1)
                A.activation(mrow[:, :], ps[0:PARTS * GRP, MISC, :], ACT.Copy).then_inc(sm["mrow_ok"], 1)

            def copy_oT(ob, qb):
                act.wait_ge(sm["oT_ok"], QB * ob + qb + 1)
                bank, oT_ = (4 + qb, x1T[:, P * qb:P * (qb + 1)]) if is_last(ob) else (MISC, oT_sb[:, :])
                A.activation(oT_, ps[:, bank, 0:P], ACT.Copy).then_inc(sm["oT_copied"], 1)

            def copy_x1T(ob):
                act.wait_ge(sm["x1T_ok"], ob + 1)
                A.activation(x1T[:, :], ps[:, MISC, :], ACT.Copy).then_inc(sm["x1T_copied"], 1)

            def gate_exp(ob):
                act.wait_ge(sm["shifted_ok"], ob + 1)
                A.activation(ex[:, :, :], shifted[:, :, :], ACT.Exp).then_inc(sm["ex_ok"], 1)

            def later_znT(a):
                act.wait_ge(sm["later_zT"], a + 1)
                A.activation(znT[:, 0, :], ps[:, MISC, :], ACT.Identity, bias=ln_bc[:, 0:1],
                             scale=ln_wc[:, 0:1]).then_inc(sm["later_znT"], 1)

            def later_copy(a, side, first):
                act.wait_ge(sm[("later_q", "later_k")[side]], a + 1)
                if side == 0 and not first:
                    act.wait_ge(sm["later_rest"], 2 * a)
                A.activation(rest[:, 0, side], ps[:, MISC, :], ACT.Identity, bias=b_qkc[:, side:side + 1])\
                 .then_inc(sm["later_qk_copied"], 1)

            def later_his(a):
                act.wait_ge(parts_out[0], STORE * (a + 1) - FIRST)
                for side in range(2):
                    act.wait_ge(sm["later_qk_copied"], 2 * a + side + 1)
                    A.activation(parts[:, 0, side, 0], rest[:, 0, side], ACT.Copy).then_inc(sm["later_hi"], 1)

            def later_mids(a):
                for side in range(2):
                    act.wait_ge(sm["later_rest"], 2 * a + side + 1)
                    A.activation(parts[:, 0, side, 1], rest[:, 1, side], ACT.Copy).then_inc(sm["later_mid"], 1)

            def later_values(a):
                act.wait_ge(sm["later_v"], a + 1)
                A.activation(v_all[:, bass.ds(QB * (a + 2), QB), :].rearrange("p c d -> p (c d)"),
                             ps[:, MISC, :], ACT.Copy).then_inc(pr["v_all_ok"][0], 1)

            def slots(b, first, last, later):
                for g in range(NG):
                    s = NG * b + g
                    for kc in range(QB):
                        if kc == 1 and not (last and g == NG - 1):
                            act.wait_ge(mrow_in[g], MROWS * (b + 1))
                            copy_mrow(s + 1)
                        exps(s, kc, 0)
                        if not first:
                            if (g, kc) in PROJECT_AT:
                                copy_oT(b - 1, PROJECT_AT[g, kc])
                            if (g, kc) == (3, 1):
                                copy_x1T(b - 1)
                        exps(s, kc, 1)
                        if later:
                            if (g, kc) == (2, 2):
                                later_znT(b)
                            if (g, kc) == (2, 3):
                                later_copy(b, 0, first)
                            if (g, kc) == (3, 0):
                                later_copy(b, 1, first)
                            if (g, kc) == (3, 1):
                                later_his(b)
                            if (g, kc) == (3, 2):
                                later_values(b)
                            if (g, kc) == (3, 3):
                                later_mids(b)
                        if kc == 0 and not (first and g == 0):
                            copy_pv(s - 1, (g - 1) % NG, None if first else b)
                        if not first and (g, kc) == (3, 2):
                            gate_exp(b - 1)

            copy_mrow(0)
            slots(0, True, False, True)
            with act.Fori(1, B - 2) as b:
                slots(b, False, False, True)
            slots(B - 2, False, False, False)
            slots(B - 1, False, True, False)
            copy_pv(UNITS - 1, NG - 1)
            for qb in range(QB):
                copy_oT(B - 1, qb)
            copy_x1T(B - 1)
            gate_exp(B - 1)
            store_pads(act, mybir.EngineType.Activation, range(E // 2, E))

            def copy_xT(i, k):
                act.wait_ge(sm["xT_ok"], i + 1)
                if not (isinstance(i, int) and i < 2):
                    act.wait_ge(sm["mm1_ok"], i - 1)
                A.activation(xT[:, k % 2, :], ps[:, 0, 0:P], ACT.Copy).then_inc(sm["xTc_ok"], 1)

            def gelu(i, k):
                act.wait_ge(sm["mm1_ok"], i + 1)
                if not (isinstance(i, int) and i < 2):
                    act.wait_ge(sm["mm2_ok"], i - 1)
                for c in range(FC):
                    last = A.activation(hidT[:, k % 2, P * c:P * (c + 1)], ps[:, 1 + k % 2, P * c:P * (c + 1)],
                                        ACT.Gelu, bias=chosen[:, k % GROUP, B1 + c:B1 + c + 1])
                last.then_inc(sm["gelu_ok"], 1)

            def finish(n, k):
                h, c = k // GROUP, k % GROUP
                if c == 0:
                    act.wait_ge(sm["frstd_ok"], n + 1)
                A.activation(final[:, h, c, :], res[:, h, c, :], ACT.Identity, scale=frstd[:, h, c:c + 1],
                             bias=fshift[:, h, c:c + 1]).then_inc(sm["final_ok"], 1)

            def steps(r, first, last):
                for k in range(NT - STEP * r if last else STEP):
                    i = STEP * r + k
                    if not (last and i + 2 >= NT):
                        copy_xT(i + 2, (k + 2) % STEP)
                    if not (last and i + 1 >= NT):
                        gelu(i + 1, (k + 1) % STEP)
                    for f in FINISH_AT.get(k, ()):
                        if not (first and f < 0) and not (last and f >= 0):
                            finish((STEP // GROUP) * r + f // GROUP, f % STEP)

            copy_xT(0, 0)
            copy_xT(1, 1)
            gelu(0, 0)
            steps(0, True, False)
            with act.Fori(1, PASSES - 1) as r:
                steps(r, False, False)
            steps(PASSES - 1, False, True)
            for f in range(STEP * (PASSES - 1), GROUP * GROUPS):
                finish(f // GROUP, f % STEP)

        @block.tensor
        def _(pe):
            T = nc.tensor
            pe.wait_ge(sm["ident_ok"], 5)
            for par in range(2):
                pe.wait_ge(pr["zn_ok"][par], 1)
                for t in range(QB):
                    last = T.transpose(ps[:, par, P * t:P * (t + 1)], zn[:, par, t, :], ident[:, :])
                last.then_inc(pr["zT_ok"][par], 1)
                if par == 0:
                    pe.wait_ge(sm["qk_weights"], QK_WEIGHTS)
                pe.wait_ge(pr["znT_ok"][par], 1)
                for side, name in ((0, "q_ok"), (1, "k_ok")):
                    T.matmul(ps[:, 2 + 2 * side + par, :], wqk_sb[:, D * side:D * (side + 1)],
                             znT[:, par, :], start=True, stop=True).then_inc(pr[name][par], 1)
            pe.wait_ge(sm["weights"], WEIGHTS)
            for par in range(2):
                for t in range(QB):
                    last = T.matmul(ps[:, 6 + par, P * t:P * (t + 1)], znT[:, par, P * t:P * (t + 1)],
                                    wv_sb[:, :], start=True, stop=True)
                last.then_inc(pr["v_ok"][par], 1)
            pe.wait_ge(sm["bv_ok"], 1)
            T.matmul(ps[:, 0, 0:D], bv_rep[:, :], wp_sb[:, :], start=True, stop=True).then_inc(sm["bias_ok"], 1)
            for par in range(2):
                pe.wait_ge(pr["rest_ok"][par], 2)
                pe.wait_ge(pr["hi_ok"][par], 2)
                pe.wait_ge(pr["v_all_ok"][par], 1)
            pe.wait_ge(sm["bias_added"], 1)
            pe.wait_ge(sm["consts"], 4)

            def maximum_scores(v, g, j, qb):
                n = GRP * QB * v + QB * j + qb
                if not (isinstance(n, int) and n < 2):
                    pe.wait_ge(sm["max_used"], n - 1)
                T.matmul(ps[:, 4 + qb % 2, :], qs[:, g, j, P * qb:P * (qb + 1)], ks[:, g, j, :],
                         start=True, stop=True).then_inc(sm["max_ok"], 1)

            def scores(s, g, kc, j):
                n = 2 * QB * s + 2 * kc + j // 2
                if j % 2 == 0 and not (isinstance(n, int) and n < 2):
                    pe.wait_ge(sm["exp_ok"], n - 1)
                last = T.matmul(ps[:, j, :], ks[:, g, j, P * kc:P * (kc + 1)], qs[:, g, j, :],
                                start=True, stop=True)
                if j % 2:
                    last.then_inc(sm["pair_ok"], 1)

            def pv(s, g, kc):
                if kc == 0:
                    pe.wait_ge(sm["vs_ok"], s + 1)
                    if not (isinstance(s, int) and s == 0):
                        pe.wait_ge(sm["pv_copied"], s)
                pe.wait_ge(sm["exp_ok"], 2 * QB * s + 2 * kc + 2)
                for j in range(GRP):
                    last = T.matmul(ps[HW * j:HW * (j + 1), 6, :], vs[:, g, kc, j, :],
                                    probs[:, GRP * (kc % 2) + j, :], start=(kc == 0), stop=(kc == QB - 1))
                last.then_inc(sm["pv_ok"], 1)

            def maxima_to_rows(v):
                pe.wait_ge(sm["nm_ok"], v + 1)
                for qb in range(QB):
                    last = T.matmul(ps[0:PARTS * GRP, MISC, P * qb:P * (qb + 1)],
                                    negm_p[:, qb].rearrange("p a j -> p (a j)"), ident_b[:, :],
                                    start=True, stop=True)
                last.then_inc(sm["mT_ok"], 1)

            def to_tokens(ob, qb):
                pe.wait_ge(sm["pv_copied"], NG * (ob + 1))
                if qb > 0 and not is_last(ob):
                    pe.wait_ge(sm["norm_ok"], QB * ob + qb)
                bank = qb if is_last(ob) else MISC
                for g in range(NG):
                    last = T.transpose(ps[:, bank, P * g:P * (g + 1)], oT[:, g, P * qb:P * (qb + 1)],
                                       ident[:, :])
                last.then_inc(sm["tr_ok"], 1)

            def to_channels(ob, qb):
                if is_last(ob):
                    pe.wait_ge(sm["norm_ok"], QB * ob + qb + 1)
                else:
                    pe.wait_ge(sm["norm_ok"], QB * (ob + 1))
                    if qb > 0:
                        pe.wait_ge(sm["y_ok"], QB * ob + qb)
                bank = 4 + qb if is_last(ob) else MISC
                T.transpose(ps[:, bank, 0:P], o_sb[:, qb, :], ident[:, :]).then_inc(sm["oT_ok"], 1)

            def project(ob, qb):
                pe.wait_ge(sm["oT_copied"], QB * ob + qb + 1)
                bank, oT_ = (4 + qb, x1T[:, P * qb:P * (qb + 1)]) if is_last(ob) else (MISC, oT_sb[:, :])
                T.matmul(ps[:, bank, P:2 * P], oT_, wp_sb[:, :], start=True, stop=True)\
                 .then_inc(sm["proj_ok"], 1)

            def x1_transposes(ob):
                y = rows_of(ob)
                wait_x1(pe, ob)
                for t in range(QB):
                    last = T.transpose(ps[:, MISC, P * t:P * (t + 1)], y[:, t, 0:D], ident[:, :])
                last.then_inc(sm["x1T_ok"], 1)

            def gate_logits(ob):
                pe.wait_ge(sm["x1T_copied"], ob + 1)
                for t in range(QB):
                    last = T.matmul(ps[:, MISC, E * t:E * (t + 1)], x1T[:, P * t:P * (t + 1)], gw_sb[:, :],
                                    start=True, stop=True)
                last.then_inc(sm["logits_ok"], 1)

            def expert_ranks(ob):
                pe.wait_ge(sm["onehot_ok"], ob + 1)
                oh = onehot[:, :, :].rearrange("p t e -> p (t e)")
                T.matmul(ps[:, MISC, 0:QB * E], below[:, :], oh, start=True, stop=False)
                for t in range(1, QB):
                    T.matmul(ps[:, MISC, t * E:QB * E], ones_b[:, :], oh[:, 0:(QB - t) * E],
                             start=False, stop=(t == QB - 1))
                for t in range(QB):
                    last = T.matmul(ps[:, MISC, QB * E:(QB + 1) * E], ones_b[:, :], oh[:, t * E:(t + 1) * E],
                                    start=(t == 0), stop=(t == QB - 1))
                last.then_inc(sm["ranks_ok"], 1)

            def later_transposes(a):
                pe.wait_ge(sm["later_zn"], a + 1)
                for t in range(QB):
                    last = T.transpose(ps[:, MISC, P * t:P * (t + 1)], zn[:, 0, t, :], ident[:, :])
                last.then_inc(sm["later_zT"], 1)

            def later_qk(a, side):
                if side == 0:
                    pe.wait_ge(sm["later_znT"], a + 1)
                else:
                    pe.wait_ge(sm["later_qk_copied"], 2 * a + 1)
                T.matmul(ps[:, MISC, :], wqk_sb[:, D * side:D * (side + 1)], znT[:, 0, :], start=True, stop=True)\
                 .then_inc(sm[("later_q", "later_k")[side]], 1)

            def later_v(a):
                for t in range(QB):
                    last = T.matmul(ps[:, MISC, P * t:P * (t + 1)], znT[:, 0, P * t:P * (t + 1)], wv_sb[:, :],
                                    start=True, stop=True)
                last.then_inc(sm["later_v"], 1)

            def before_pv(b, g, kc, first, last, later):
                s = NG * b + g
                if not first:
                    if (g, kc) in TOKENS_AT:
                        if kc == 1:
                            pe.wait_ge(sm["mrow_ok"], s + 2)
                        to_tokens(b - 1, TOKENS_AT[g, kc])
                    if (g, kc) in PROJECT_AT:
                        if (g, kc) in ((1, 1), (2, 1)):
                            pe.wait_ge(sm["mrow_ok"], s + 2)
                        to_channels(b - 1, PROJECT_AT[g, kc])
                    if (g, kc) == (3, 1):
                        if last:
                            pe.wait_ge(sm["y_ok"], QB * b)
                        else:
                            pe.wait_ge(sm["mrow_ok"], s + 2)
                        x1_transposes(b - 1)
                    if (g, kc) == (3, 3):
                        if later:
                            pe.wait_ge(pr["v_all_ok"][0], b + 2)
                        expert_ranks(b - 1)
                if later:
                    if (g, kc) == (2, 2):
                        if first:
                            pe.wait_ge(sm["mrow_ok"], s + 2)
                        else:
                            pe.wait_ge(sm["y_ok"], QB * b)
                        later_transposes(b)
                    if (g, kc) == (2, 3):
                        later_qk(b, 0)
                    if (g, kc) == (3, 0):
                        later_qk(b, 1)
                    if (g, kc) == (3, 2):
                        if first:
                            pe.wait_ge(sm["mrow_ok"], s + 2)
                        else:
                            pe.wait_ge(sm["lg_ok"], b)
                        later_v(b)

            def after_pv(b, g, kc, first, last, later):
                s = NG * b + g
                if kc == 0 and not (last and g == NG - 1):
                    if not (first and g == 0):
                        pe.wait_ge(sm["mrow_ok"], s + 1)
                    if not first and g == 0:
                        pe.wait_ge(sm["ranks_copied"], b)
                    if not first and g == 1:
                        pe.wait_ge(sm["norm_ok"], QB * b)
                    if not first and g == 2:
                        pe.wait_ge(sm["y_ok"], QB * (b - 1) + 3)
                    if not first and g == 3 and not later:
                        pe.wait_ge(sm["y_ok"], QB * b)
                    if later and g == 3:
                        pe.wait_ge(sm["later_qk_copied"], 2 * b + 2)
                    maxima_to_rows(s + 1)
                if not first:
                    if (g, kc) in PROJECT_AT:
                        project(b - 1, PROJECT_AT[g, kc])
                    if (g, kc) == (3, 1):
                        gate_logits(b - 1)
                elif (g, kc) == (3, 3):
                    pe.wait_ge(pr["v_all_ok"][0], 2)

            def slots(b, first, last, later):
                for g in range(NG):
                    s = NG * b + g
                    pe.wait_ge(mrow_in[g], MROWS * (b + 1))
                    more = not (last and g >= 2)
                    if more:
                        pe.wait_ge(loaded[(g + 2) % NG], LOAD * (b + (g + 2) // NG + 1))

                    def ahead(kc, qb):
                        if more:
                            maximum_scores(s + 2, (g + 2) % NG, kc, qb)

                    for kc in range(QB):
                        ahead(kc, 0)
                        scores(s, g, kc, 0)
                        scores(s, g, kc, 1)
                        ahead(kc, 1)
                        scores(s, g, kc, 2)
                        scores(s, g, kc, 3)
                        ahead(kc, 2)
                        before_pv(b, g, kc, first, last, later)
                        if (g, kc) in BEFORE_PV:
                            ahead(kc, 3)
                        if kc > 0:
                            pv(s, g, kc - 1)
                        elif not (first and g == 0):
                            pv(s - 1, (g - 1) % NG, QB - 1)
                        if (g, kc) not in BEFORE_PV:
                            ahead(kc, 3)
                        after_pv(b, g, kc, first, last, later)

            for v in range(2):
                pe.wait_ge(loaded[v], LOAD)
                if v == 1:
                    pe.wait_ge(sm["cleared"], 2)
                for j in range(GRP):
                    for qb in range(QB):
                        n = GRP * QB * v + QB * j + qb
                        if n >= 6 and qb % 2 == 0:
                            pe.wait_ge(sm["max_used"], n - 4)
                        T.matmul(ps[:, n % 6, :], qs[:, v, j, P * qb:P * (qb + 1)], ks[:, v, j, :],
                                 start=True, stop=True).then_inc(sm["max_ok"], 1)
                    if (v, j) == (1, 0):
                        maxima_to_rows(0)
            pe.wait_ge(sm["max_used"], 2 * GRP * QB)
            pe.wait_ge(sm["ones_in"], 16 * NG)
            slots(0, True, False, True)
            with pe.Fori(1, B - 2) as b:
                slots(b, False, False, True)
            slots(B - 2, False, False, False)
            slots(B - 1, False, True, False)
            ob = B - 1
            pv(UNITS - 1, NG - 1, QB - 1)
            pe.wait_ge(sm["ranks_copied"], ob + 1)
            pe.wait_ge(sm["exp_ok"], 2 * QB * UNITS)
            pe.wait_ge(sm["max_used"], GRP * QB * UNITS)
            for qb in range(QB):
                to_tokens(ob, qb)
            for qb in range(QB):
                to_channels(ob, qb)
            for qb in range(QB):
                project(ob, qb)
            pe.wait_ge(sm["y_ok"], TILES)
            x1_transposes(ob)
            gate_logits(ob)
            expert_ranks(ob)

            pe.wait_ge(sm["table_ok"], 1)
            pe.wait_ge(sm["moe_weights"], MOE_WEIGHTS)

            def expert_of(i):
                return nc.values_load(table[0:1, 1, bass.ds(i, 1)], engines=(mybir.EngineType.PE,), min_val=0,
                                      max_val=E - 1, skip_runtime_bounds_check_because=IN_RANGE)

            def transpose_rows(i, k, r):
                pe.wait_ge(rows_in[k], 16 * (r + 1))
                if not (isinstance(i, int) and i == 0):
                    pe.wait_ge(sm["xTc_ok"], i)
                T.transpose(ps[:, 0, 0:P], rows[:, k, 0:D], ident[:, :]).then_inc(sm["xT_ok"], 1)

            def up(i, k):
                pe.wait_ge(sm["xTc_ok"], i + 1)
                pe.wait_ge(sm["chosen_ok"], i + 1)
                if not (isinstance(i, int) and i < 2):
                    pe.wait_ge(sm["gelu_ok"], i - 1)
                for c in range(FC):
                    last = T.matmul(ps[:, 1 + k % 2, P * c:P * (c + 1)], chosen[:, k % GROUP, P * c:P * (c + 1)],
                                    xT[:, k % 2, :], start=True, stop=True)
                last.then_inc(sm["mm1_ok"], 1)

            def down(i, k, e):
                pe.wait_ge(sm["gelu_ok"], i + 1)
                if not (isinstance(i, int) and i < 2):
                    pe.wait_ge(sm["yb_ok"], i - 1)
                for c in range(FC):
                    last = T.matmul(ps[:, 4 + k % 2, 0:D], hidT[:, k % 2, P * c:P * (c + 1)],
                                    w2_sb[:, bass.ds(e * (FC * D) + c * D, D)],
                                    start=(c == 0), stop=(c == FC - 1))
                last.then_inc(sm["mm2_ok"], 1)

            def steps(r, last):
                for k in range(NT - STEP * r if last else STEP):
                    i = STEP * r + k
                    e = expert_of(i)
                    if not (last and i + 2 >= NT):
                        transpose_rows(i + 2, (k + 2) % STEP, r + (k + 2) // STEP)
                    if not (last and i + 1 >= NT):
                        up(i + 1, (k + 1) % STEP)
                    down(i, k, e)

            transpose_rows(0, 0, 0)
            transpose_rows(1, 1, 0)
            up(0, 0)
            steps(0, False)
            with pe.Fori(1, PASSES - 1) as r:
                steps(r, False)
            steps(PASSES - 1, True)


_INS = ["z", "ln_w", "ln_b", "w_qk", "w_v", "b_qk", "b_v", "w_proj", "b_proj", "gate_w", "gate_b",
        "w1", "b1t", "w2", "b2"]


def kernel(**inputs):
    import numpy as np
    import concourse.bacc as bacc
    from concourse.bass_utils import run_bass_kernel_spmd

    def given(name):
        return np.asarray(inputs[name])

    z = given("L0_attn_z")
    w_qkv, b_qkv = given("L0_attn_W_qkv"), given("L0_attn_b_qkv")
    by_channel = np.arange(D).reshape(NG, GRP, DH).transpose(0, 2, 1).ravel()
    qk = np.concatenate([by_channel, D + by_channel])
    arrays = {
        "z": z.reshape(B * S, D), "ln_w": given("L0_attn_ln_w"), "ln_b": given("L0_attn_ln_b"),
        "w_qk": w_qkv[:, qk], "w_v": w_qkv[:, 2 * D:], "b_qk": b_qkv[qk], "b_v": b_qkv[2 * D:],
        "w_proj": given("L0_attn_W_proj"), "b_proj": given("L0_attn_b_proj"),
        "gate_w": given("L0_ffn_gate_w"), "gate_b": given("L0_ffn_gate_b"),
        "w1": given("L0_ffn_w1"), "b1t": given("L0_ffn_b1").reshape(E, FC, P).transpose(2, 0, 1),
        "w2": given("L0_ffn_w2"), "b2": given("L0_ffn_b2"),
    }
    arrays = {n: np.ascontiguousarray(arrays[n]) for n in _INS}
    nc = bacc.Bacc("TRN2", target_bir_lowering=False, num_devices=1)
    args = [nc.dram_tensor(n, arrays[n].shape, mybir.dt.from_np(arrays[n].dtype), kind="ExternalInput").ap()
            for n in _INS]
    out = nc.dram_tensor("out", (B * S, D), F32, kind="ExternalOutput").ap()
    build(nc, *args, out)
    r = run_bass_kernel_spmd(nc, [arrays], core_ids=[0])
    return r.results[0]["out"].reshape(B, S, D)
```
